# Optimizing a Trainium2 kernel written in Bass

```python
import numpy as np
import jax
import jax.numpy as jnp

def _softmax(x, axis=-1):
    return jax.nn.softmax(x, axis=axis)

def _gelu(x):
    return jax.nn.gelu(x, approximate=True)

def _silu(x):
    return jax.nn.silu(x)

def _sigmoid(x):
    return jax.nn.sigmoid(x)

def _layernorm(x, axis=-1, eps=1e-05):
    m = jnp.mean(x, axis=axis, keepdims=True)
    v = jnp.var(x, axis=axis, keepdims=True)
    return (x - m) / jnp.sqrt(v + eps)

def _scatter_add(tgt, idx, src, axis=0):
    return tgt.at[idx].add(src)

def _segment_sum(src, seg, n):
    return jax.ops.segment_sum(src, seg, n)
kernel_name = 'mk_decoder_postln_d2_seqx_r8_9d69ae'

def setup_inputs(seed: int=0):
    np.random.seed(seed)
    _w = jnp.asarray

    def _rec_inputs():
        import jax
        import jax.numpy as jnp
        _rk = jax.random.key(seed)
        x = 7.22e-05 + 1 * jax.random.normal(jax.random.fold_in(_rk, 1), (8, 256, 128), jnp.float32)
        _lenS = 256 - jax.random.randint(jax.random.fold_in(_rk, 7), (8,), 0, max(1, 256 // 4) + 1, jnp.int32)
        _lenS2 = 1601 - jax.random.randint(jax.random.fold_in(_rk, 8), (8,), 0, max(1, 1601 // 4) + 1, jnp.int32)
        _ctx_768P = jax.random.normal(jax.random.fold_in(_rk, 11), (8, 16, 96), jnp.float32)
        _ctx_768c = jax.random.dirichlet(jax.random.fold_in(_rk, 511), 0.3 * jnp.ones((16,), jnp.float32), (8, 1601))
        _ctx_768t = jnp.einsum('bsk,bkd->bsd', _ctx_768c, _ctx_768P)
        _ctx_768t = _ctx_768t * jax.lax.rsqrt(jnp.mean(jnp.square(_ctx_768t)) + 1e-12) * 0.953939
        ctx_768 = -0.000191848 + 0.999787 * (_ctx_768t + 0.3 * jax.random.normal(jax.random.fold_in(_rk, 611), (8, 1601, 96), jnp.float32))
        _validS = jnp.arange(256)[None, :] < _lenS[:, None]
        _validS2 = jnp.arange(1601)[None, :] < _lenS2[:, None]
        _causal = jnp.tril(jnp.ones((256, 256), dtype=bool))
        mask_BxS2_bk0 = jnp.logical_not(jnp.broadcast_to(_validS2[:, :], (8, 1601)))
        return (x, ctx_768, mask_BxS2_bk0)
    x, ctx_768, mask_BxS2_bk0 = _rec_inputs()

    def _L0_attn_setup():
        import jax, jax.numpy as jnp
        import numpy as np
        N_HEADS = 16
        ROPE_BASE = 10000.0

        def _rotate_every_two(x):
            x_even = x[..., ::2]
            x_odd = x[..., 1::2]
            return jnp.stack((-x_odd, x_even), axis=-1).reshape(x.shape)

        def _rope_cos_sin(seq_len, head_dim):
            inv_freq = 1.0 / ROPE_BASE ** (jnp.arange(0, head_dim, 2, dtype=jnp.float32) / head_dim)
            pos = jnp.arange(seq_len, dtype=jnp.float32)
            freqs = pos[:, None] * inv_freq[None, :]
            emb = jnp.repeat(freqs, 2, axis=-1)
            return (jnp.cos(emb)[None, None], jnp.sin(emb)[None, None])
        key = jax.random.key(seed)
        ks = jax.random.split(key, 5)
        B, S, D = (2, 256, 128)
        std = 0.02
        return {'x': jax.random.normal(ks[0], (B, S, D), dtype=jnp.float32), 'Wq': jax.random.normal(ks[1], (D, D), dtype=jnp.float32) * std, 'Wk': jax.random.normal(ks[2], (D, D), dtype=jnp.float32) * std, 'Wv': jax.random.normal(ks[3], (D, D), dtype=jnp.float32) * std, 'Wo': jax.random.normal(ks[4], (D, D), dtype=jnp.float32) * std}
    _L0_attn_all = _L0_attn_setup()
    _L0_attn_in = {k: v for k, v in _L0_attn_all.items() if k in ('Wq', 'Wk', 'Wv', 'Wo')}
    del _L0_attn_all

    def _L0_xattn_setup():
        import jax, jax.numpy as jnp
        import numpy as np
        B, LQ, LK = (4, 256, 256)
        D1, D2, H = (128, 96, 128)
        key = jax.random.key(seed)
        ks = jax.random.split(key, 9)
        s1, s2, sh = (1.0 / np.sqrt(D1), 1.0 / np.sqrt(D2), 1.0 / np.sqrt(H))
        return {'query': jax.random.normal(ks[0], (B, LQ, D1), jnp.float32), 'key': jax.random.normal(ks[1], (B, LK, D2), jnp.float32), 'value': jax.random.normal(ks[2], (B, LK, D2), jnp.float32), 'Wq': jax.random.normal(ks[3], (D1, H), jnp.float32) * s1, 'bq': jax.random.normal(ks[4], (H,), jnp.float32) * s1, 'Wk': jax.random.normal(ks[5], (D2, H), jnp.float32) * s2, 'bk': jax.random.normal(ks[6], (H,), jnp.float32) * s2, 'Wv': jax.random.normal(ks[7], (D2, H), jnp.float32) * s2, 'bv': jax.random.normal(ks[8], (H,), jnp.float32) * s2}
    _L0_xattn_all = _L0_xattn_setup()
    _L0_xattn_in = {k: v for k, v in _L0_xattn_all.items() if k in ('Wq', 'bq', 'Wk', 'bk', 'Wv', 'bv')}
    del _L0_xattn_all

    def _L0_ffn_setup():
        import jax, jax.numpy as jnp
        import numpy as np
        E = 32
        H = 128
        I = 64
        G = 8
        TKG = 4
        TOPK = 8
        NSH = 2
        SCALE = 2.5
        key = jax.random.key(seed)
        ks = jax.random.split(key, 10)
        s = 0.02
        return {'hidden_states': jax.random.normal(ks[0], (2, 128, H), jnp.float32), 'gate_w': jax.random.normal(ks[1], (E, H), jnp.float32) * s, 'gate_bias': jax.random.normal(ks[2], (E,), jnp.float32) * s, 'w_gate': jax.random.normal(ks[3], (E, I, H), jnp.float32) * s, 'w_up': jax.random.normal(ks[4], (E, I, H), jnp.float32) * s, 'w_down': jax.random.normal(ks[5], (E, H, I), jnp.float32) * s, 'sh_gate': jax.random.normal(ks[6], (I * NSH, H), jnp.float32) * s, 'sh_up': jax.random.normal(ks[7], (I * NSH, H), jnp.float32) * s, 'sh_down': jax.random.normal(ks[8], (H, I * NSH), jnp.float32) * s}
    _L0_ffn_all = _L0_ffn_setup()
    _L0_ffn_in = {k: v for k, v in _L0_ffn_all.items() if k in ('gate_w', 'gate_bias', 'w_gate', 'w_up', 'w_down', 'sh_gate', 'sh_up', 'sh_down')}
    del _L0_ffn_all

    def _L1_attn_setup():
        import jax, jax.numpy as jnp
        import numpy as np
        EMBED_DIM = 128
        NUM_HEADS = 16
        HEAD_DIM = EMBED_DIM // NUM_HEADS
        SEQ_LEN = 128
        BATCH = 4
        MAX_REL_POS = 2

        def _rel_index(length_q, length_k):
            q = jnp.arange(length_q)[:, None]
            k = jnp.arange(length_k)[None, :]
            return jnp.clip(k - q, -MAX_REL_POS, MAX_REL_POS) + MAX_REL_POS
        key = jax.random.key(seed)
        ks = jax.random.split(key, 12)
        s = 1.0 / np.sqrt(EMBED_DIM)
        x = jax.random.normal(ks[0], (BATCH, SEQ_LEN, EMBED_DIM), dtype=jnp.float32)
        W_q = jax.random.normal(ks[1], (EMBED_DIM, EMBED_DIM), dtype=jnp.float32) * s
        b_q = jnp.zeros((EMBED_DIM,), dtype=jnp.float32)
        W_k = jax.random.normal(ks[2], (EMBED_DIM, EMBED_DIM), dtype=jnp.float32) * s
        b_k = jnp.zeros((EMBED_DIM,), dtype=jnp.float32)
        W_v = jax.random.normal(ks[3], (EMBED_DIM, EMBED_DIM), dtype=jnp.float32) * s
        b_v = jnp.zeros((EMBED_DIM,), dtype=jnp.float32)
        W_o = jax.random.normal(ks[4], (EMBED_DIM, EMBED_DIM), dtype=jnp.float32) * s
        b_o = jnp.zeros((EMBED_DIM,), dtype=jnp.float32)
        lim = float(np.sqrt(6.0 / (2 * MAX_REL_POS + 1 + HEAD_DIM)))
        rel_k_table = jax.random.uniform(ks[5], (2 * MAX_REL_POS + 1, HEAD_DIM), jnp.float32, -lim, lim)
        rel_v_table = jax.random.uniform(ks[6], (2 * MAX_REL_POS + 1, HEAD_DIM), jnp.float32, -lim, lim)
        return {'x': x, 'W_q': W_q, 'b_q': b_q, 'W_k': W_k, 'b_k': b_k, 'W_v': W_v, 'b_v': b_v, 'W_o': W_o, 'b_o': b_o, 'rel_k_table': rel_k_table, 'rel_v_table': rel_v_table}
    _L1_attn_all = _L1_attn_setup()
    _L1_attn_in = {k: v for k, v in _L1_attn_all.items() if k in ('W_q', 'b_q', 'W_k', 'b_k', 'W_v', 'b_v', 'W_o', 'b_o', 'rel_k_table', 'rel_v_table')}
    del _L1_attn_all

    def _L1_xattn_setup():
        import jax, jax.numpy as jnp
        import numpy as np
        B, T_Q, T_C = (2, 256, 256)
        D_Q, D_C = (128, 96)
        H, DH = (12, 64)
        INNER = H * DH
        key = jax.random.key(seed)
        ks = jax.random.split(key, 12)

        def xavier(k, shape):
            fan_in, fan_out = (shape[1], shape[0])
            lim = float(np.sqrt(6.0 / (fan_in + fan_out)))
            return jax.random.uniform(k, shape, jnp.float32, -lim, lim)
        return {'query': jax.random.normal(ks[0], (B, T_Q, D_Q), jnp.float32), 'cross': jax.random.normal(ks[1], (B, T_C, D_C), jnp.float32), 'key_padding_mask': jax.random.randint(ks[2], (B, T_C), 0, 2).astype(bool), 'Wq': xavier(ks[3], (INNER, D_Q)), 'bq': jnp.zeros((INNER,), jnp.float32), 'Wk': xavier(ks[4], (INNER, D_C)), 'bk': jnp.zeros((INNER,), jnp.float32), 'Wv': xavier(ks[5], (INNER, D_C)), 'bv': jnp.zeros((INNER,), jnp.float32), 'Wo': xavier(ks[6], (D_Q, INNER)), 'bo': jnp.zeros((D_Q,), jnp.float32)}
    _L1_xattn_all = _L1_xattn_setup()
    _L1_xattn_in = {k: v for k, v in _L1_xattn_all.items() if k in ('Wq', 'bq', 'Wk', 'bk', 'Wv', 'bv', 'Wo', 'bo')}
    del _L1_xattn_all

    def _L1_ffn_setup():
        import jax, jax.numpy as jnp
        import numpy as np
        TOP_P = 0.3
        key = jax.random.key(seed)
        k1, k2, k3, k4 = jax.random.split(key, 4)
        B, S, D, H, E = (4, 512, 128, 128, 8)
        x = jax.random.normal(k1, (B, S, D), dtype=jnp.float32)
        gate_W = jax.random.normal(k2, (E, D), dtype=jnp.float32) / np.float32(np.sqrt(D))
        expert_W = jax.random.normal(k3, (E, H, D), dtype=jnp.float32) / np.float32(np.sqrt(D))
        out_W = jax.random.normal(k4, (D, H), dtype=jnp.float32) / np.float32(np.sqrt(H))
        return {'x': x, 'gate_W': gate_W, 'expert_W': expert_W, 'out_W': out_W}
    _L1_ffn_all = _L1_ffn_setup()
    _L1_ffn_in = {k: v for k, v in _L1_ffn_all.items() if k in ('gate_W', 'expert_W', 'out_W')}
    del _L1_ffn_all
    return {'x': x, 'ctx_768': ctx_768, 'mask_BxS2_bk0': mask_BxS2_bk0, 'L0_attn_Wq': _L0_attn_in['Wq'], 'L0_attn_Wk': _L0_attn_in['Wk'], 'L0_attn_Wv': _L0_attn_in['Wv'], 'L0_attn_Wo': _L0_attn_in['Wo'], 'L0_xattn_Wq': _L0_xattn_in['Wq'], 'L0_xattn_bq': _L0_xattn_in['bq'], 'L0_xattn_Wk': _L0_xattn_in['Wk'], 'L0_xattn_bk': _L0_xattn_in['bk'], 'L0_xattn_Wv': _L0_xattn_in['Wv'], 'L0_xattn_bv': _L0_xattn_in['bv'], 'L0_ffn_gate_w': _L0_ffn_in['gate_w'], 'L0_ffn_gate_bias': _L0_ffn_in['gate_bias'], 'L0_ffn_w_gate': _L0_ffn_in['w_gate'], 'L0_ffn_w_up': _L0_ffn_in['w_up'], 'L0_ffn_w_down': _L0_ffn_in['w_down'], 'L0_ffn_sh_gate': _L0_ffn_in['sh_gate'], 'L0_ffn_sh_up': _L0_ffn_in['sh_up'], 'L0_ffn_sh_down': _L0_ffn_in['sh_down'], 'L1_attn_W_q': _L1_attn_in['W_q'], 'L1_attn_b_q': _L1_attn_in['b_q'], 'L1_attn_W_k': _L1_attn_in['W_k'], 'L1_attn_b_k': _L1_attn_in['b_k'], 'L1_attn_W_v': _L1_attn_in['W_v'], 'L1_attn_b_v': _L1_attn_in['b_v'], 'L1_attn_W_o': _L1_attn_in['W_o'], 'L1_attn_b_o': _L1_attn_in['b_o'], 'L1_attn_rel_k_table': _L1_attn_in['rel_k_table'], 'L1_attn_rel_v_table': _L1_attn_in['rel_v_table'], 'L1_xattn_Wq': _L1_xattn_in['Wq'], 'L1_xattn_bq': _L1_xattn_in['bq'], 'L1_xattn_Wk': _L1_xattn_in['Wk'], 'L1_xattn_bk': _L1_xattn_in['bk'], 'L1_xattn_Wv': _L1_xattn_in['Wv'], 'L1_xattn_bv': _L1_xattn_in['bv'], 'L1_xattn_Wo': _L1_xattn_in['Wo'], 'L1_xattn_bo': _L1_xattn_in['bo'], 'L1_ffn_gate_W': _L1_ffn_in['gate_W'], 'L1_ffn_expert_W': _L1_ffn_in['expert_W'], 'L1_ffn_out_W': _L1_ffn_in['out_W']}

def reference(x, ctx_768, mask_BxS2_bk0, L0_attn_Wq, L0_attn_Wk, L0_attn_Wv, L0_attn_Wo, L0_xattn_Wq, L0_xattn_bq, L0_xattn_Wk, L0_xattn_bk, L0_xattn_Wv, L0_xattn_bv, L0_ffn_gate_w, L0_ffn_gate_bias, L0_ffn_w_gate, L0_ffn_w_up, L0_ffn_w_down, L0_ffn_sh_gate, L0_ffn_sh_up, L0_ffn_sh_down, L1_attn_W_q, L1_attn_b_q, L1_attn_W_k, L1_attn_b_k, L1_attn_W_v, L1_attn_b_v, L1_attn_W_o, L1_attn_b_o, L1_attn_rel_k_table, L1_attn_rel_v_table, L1_xattn_Wq, L1_xattn_bq, L1_xattn_Wk, L1_xattn_bk, L1_xattn_Wv, L1_xattn_bv, L1_xattn_Wo, L1_xattn_bo, L1_ffn_gate_W, L1_ffn_expert_W, L1_ffn_out_W):
    import jax
    import jax.numpy as jnp

    def _L0_attn_ref(x, Wq, Wk, Wv, Wo):
        import jax, jax.numpy as jnp
        import numpy as np
        N_HEADS = 16
        ROPE_BASE = 10000.0

        def _rotate_every_two(x):
            x_even = x[..., ::2]
            x_odd = x[..., 1::2]
            return jnp.stack((-x_odd, x_even), axis=-1).reshape(x.shape)

        def _rope_cos_sin(seq_len, head_dim):
            inv_freq = 1.0 / ROPE_BASE ** (jnp.arange(0, head_dim, 2, dtype=jnp.float32) / head_dim)
            pos = jnp.arange(seq_len, dtype=jnp.float32)
            freqs = pos[:, None] * inv_freq[None, :]
            emb = jnp.repeat(freqs, 2, axis=-1)
            return (jnp.cos(emb)[None, None], jnp.sin(emb)[None, None])
        B, S, D = x.shape
        H = N_HEADS
        hd = D // H
        scale = hd ** (-0.5)

        def shape_heads(t):
            return t.reshape(B, S, H, hd).transpose(0, 2, 1, 3)
        q = shape_heads(x @ Wq.T)
        k = shape_heads(x @ Wk.T)
        v = shape_heads(x @ Wv.T)
        cos, sin = _rope_cos_sin(S, hd)
        q = q * cos + _rotate_every_two(q) * sin
        k = k * cos + _rotate_every_two(k) * sin
        scores = jnp.einsum('bhqd,bhkd->bhqk', q, k) * scale
        qpos = jnp.arange(S)[:, None]
        kpos = jnp.arange(S)[None, :]
        mask = jnp.where(kpos > qpos, jnp.float32(-jnp.inf), jnp.float32(0.0))
        scores = scores + mask[None, None]
        attn = jax.nn.softmax(scores.astype(jnp.float32), axis=-1).astype(q.dtype)
        out = jnp.einsum('bhqk,bhkd->bhqd', attn, v)
        out = out.transpose(0, 2, 1, 3).reshape(B, S, D)
        return out @ Wo.T

    def _L0_xattn_ref(query, key, value, Wq, bq, Wk, bk, Wv, bv):
        import jax, jax.numpy as jnp
        import numpy as np
        B, LQ, LK = (4, 256, 256)
        D1, D2, H = (128, 96, 128)
        q = jnp.einsum('bqd,dh->bqh', query, Wq) + bq
        k = jnp.einsum('bkd,dh->bkh', key, Wk) + bk
        v = jnp.einsum('bkd,dh->bkh', value, Wv) + bv
        scores = jnp.einsum('bqh,bkh->bqk', q, k)
        weights = jax.nn.softmax(scores, axis=-1)
        return jnp.einsum('bqk,bkh->bqh', weights, v)

    def _L0_ffn_ref(hidden_states, gate_w, gate_bias, w_gate, w_up, w_down, sh_gate, sh_up, sh_down):
        import jax, jax.numpy as jnp
        import numpy as np
        E = 32
        H = 128
        I = 64
        G = 8
        TKG = 4
        TOPK = 8
        NSH = 2
        SCALE = 2.5
        B, S, Hd = hidden_states.shape
        h = hidden_states.reshape(-1, Hd)
        logits = h.astype(jnp.float32) @ gate_w.T
        scores = jax.nn.sigmoid(logits)
        sc = scores + gate_bias
        grp = sc.reshape(-1, G, E // G)
        group_scores = jax.lax.top_k(grp, 2)[0].sum(-1)
        gidx = jax.lax.top_k(group_scores, TKG)[1]
        gmask = jnp.sum(jax.nn.one_hot(gidx, G, dtype=sc.dtype), axis=1)
        smask = jnp.repeat(gmask, E // G, axis=1)
        masked = jnp.where(smask > 0, sc, jnp.zeros_like(sc))
        tki = jax.lax.top_k(masked, TOPK)[1]
        tkw = jnp.take_along_axis(scores, tki, axis=1)
        tkw = tkw / (tkw.sum(-1, keepdims=True) + 1e-20)
        tkw = tkw * SCALE
        combine = (jax.nn.one_hot(tki, E, dtype=tkw.dtype) * tkw[..., None]).sum(1)
        g = jax.nn.silu(jnp.einsum('th,eih->tei', h, w_gate))
        u = jnp.einsum('th,eih->tei', h, w_up)
        routed = jnp.einsum('tei,ehi->th', g * u * combine[:, :, None], w_down)
        sg = jax.nn.silu(h @ sh_gate.T)
        shared = sg * (h @ sh_up.T) @ sh_down.T
        return (routed + shared).reshape(B, S, Hd)

    def _L1_attn_ref(x, W_q, b_q, W_k, b_k, W_v, b_v, W_o, b_o, rel_k_table, rel_v_table):
        import jax, jax.numpy as jnp
        import numpy as np
        EMBED_DIM = 128
        NUM_HEADS = 16
        HEAD_DIM = EMBED_DIM // NUM_HEADS
        SEQ_LEN = 128
        BATCH = 4
        MAX_REL_POS = 2

        def _rel_index(length_q, length_k):
            q = jnp.arange(length_q)[:, None]
            k = jnp.arange(length_k)[None, :]
            return jnp.clip(k - q, -MAX_REL_POS, MAX_REL_POS) + MAX_REL_POS
        B, S, E = x.shape
        H, D = (NUM_HEADS, HEAD_DIM)
        scale = jnp.sqrt(jnp.asarray(D, x.dtype))
        Q = x @ W_q + b_q
        K = x @ W_k + b_k
        V = x @ W_v + b_v
        Qh = Q.reshape(B, S, H, D).transpose(0, 2, 1, 3)
        Kh = K.reshape(B, S, H, D).transpose(0, 2, 1, 3)
        Vh = V.reshape(B, S, H, D).transpose(0, 2, 1, 3)
        scores = jnp.einsum('bhqd,bhkd->bhqk', Qh, Kh)
        idx = _rel_index(S, S)
        rel_k = rel_k_table[idx]
        scores = (scores + jnp.einsum('bhqd,qkd->bhqk', Qh, rel_k)) / scale
        causal = jnp.tril(jnp.ones((S, S), dtype=bool))
        scores = jnp.where(causal[None, None], scores, jnp.asarray(-1000000000.0, scores.dtype))
        attn = jax.nn.softmax(scores, axis=-1)
        out = jnp.einsum('bhqk,bhkd->bhqd', attn, Vh)
        rel_v = rel_v_table[idx]
        out = out + jnp.einsum('bhqk,qkd->bhqd', attn, rel_v)
        out = out.transpose(0, 2, 1, 3).reshape(B, S, E)
        return out @ W_o + b_o

    def _L1_xattn_ref(query, cross, key_padding_mask, Wq, bq, Wk, bk, Wv, bv, Wo, bo):
        import jax, jax.numpy as jnp
        import numpy as np
        B, T_Q, T_C = (2, 256, 256)
        D_Q, D_C = (128, 96)
        H, DH = (12, 64)
        INNER = H * DH
        b, tq, _ = query.shape
        tc = cross.shape[1]
        q = (query @ Wq.T + bq).reshape(b, tq, H, DH)
        k = (cross @ Wk.T + bk).reshape(b, tc, H, DH)
        v = (cross @ Wv.T + bv).reshape(b, tc, H, DH)
        scores = jnp.einsum('bqhd,bkhd->bhqk', q, k) / jnp.sqrt(jnp.float32(DH))
        scores = jnp.where(key_padding_mask[:, None, None, :], -jnp.inf, scores)
        attn = jax.nn.softmax(scores, axis=-1)
        out = jnp.einsum('bhqk,bkhd->bqhd', attn, v).reshape(b, tq, INNER)
        return out @ Wo.T + bo

    def _L1_ffn_ref(x, gate_W, expert_W, out_W):
        import jax, jax.numpy as jnp
        import numpy as np
        TOP_P = 0.3
        B, S, D = x.shape
        E = gate_W.shape[0]
        N = B * S
        p = jax.nn.softmax(jnp.einsum('bsd,ed->bse', x, gate_W), axis=-1).reshape(N, E)
        tpi = (p > TOP_P).astype(jnp.int32)
        cnt = jnp.sum(tpi[:, :, None] == jnp.arange(E)[None, None, :], axis=1)
        scale = cnt.astype(x.dtype) * p
        x2 = x.reshape(N, D)
        h = jnp.einsum('nd,ehd->neh', x2, expert_W)
        final = jnp.einsum('neh,ne->nh', h, scale)
        out = jnp.einsum('nh,dh->nd', final, out_W).reshape(B, S, D)
        return out
    x = _layernorm(x + _L0_attn_ref(x, L0_attn_Wq, L0_attn_Wk, L0_attn_Wv, L0_attn_Wo), axis=-1)
    x = _layernorm(x + _L0_xattn_ref(x, ctx_768, ctx_768, L0_xattn_Wq, L0_xattn_bq, L0_xattn_Wk, L0_xattn_bk, L0_xattn_Wv, L0_xattn_bv), axis=-1)
    x = _layernorm(x + _L0_ffn_ref(x, L0_ffn_gate_w, L0_ffn_gate_bias, L0_ffn_w_gate, L0_ffn_w_up, L0_ffn_w_down, L0_ffn_sh_gate, L0_ffn_sh_up, L0_ffn_sh_down), axis=-1)
    x = _layernorm(x + _L1_attn_ref(x, L1_attn_W_q, L1_attn_b_q, L1_attn_W_k, L1_attn_b_k, L1_attn_W_v, L1_attn_b_v, L1_attn_W_o, L1_attn_b_o, L1_attn_rel_k_table, L1_attn_rel_v_table), axis=-1)
    x = _layernorm(x + _L1_xattn_ref(x, ctx_768, mask_BxS2_bk0, L1_xattn_Wq, L1_xattn_bq, L1_xattn_Wk, L1_xattn_bk, L1_xattn_Wv, L1_xattn_bv, L1_xattn_Wo, L1_xattn_bo), axis=-1)
    x = _layernorm(x + _L1_ffn_ref(x, L1_ffn_gate_W, L1_ffn_expert_W, L1_ffn_out_W), axis=-1)
    return x

_drawn_inputs = setup_inputs


def setup_inputs(seed=0):
    import zlib

    import numpy as np

    out = dict(_drawn_inputs(seed))
    spreads = {'L1_attn_b_q': (0.0, 0.283),
     'L1_attn_b_k': (0.0, 2.0),
     'L1_attn_b_v': (0.0, 0.1),
     'L1_attn_b_o': (0.0, 0.1),
     'L1_xattn_bq': (0.0, 0.778),
     'L1_xattn_bk': (0.0, 2.0),
     'L1_xattn_bv': (0.0, 0.1),
     'L1_xattn_bo': (0.0, 0.1)}
    factors = {'L0_attn_Wq': 8.0,
     'L0_attn_Wk': 8.0,
     'L0_xattn_bk': 64.0,
     'L0_ffn_gate_w': 7.922,
     'L0_ffn_gate_bias': 8.0,
     'L0_ffn_w_gate': 8.0,
     'L0_ffn_w_up': 8.0,
     'L0_ffn_w_down': 8.0,
     'L0_ffn_sh_gate': 4.868,
     'L0_ffn_sh_up': 6.256,
     'L0_ffn_sh_down': 6.107}
    for name, (base, spread) in spreads.items():
        noise = np.random.default_rng([zlib.crc32(name.encode()), seed]).standard_normal(out[name].shape)
        drawn = base * np.exp(spread * noise) if base else spread * noise
        out[name] = jnp.asarray(drawn.astype(out[name].dtype))
    for name, factor in factors.items():
        out[name] = (out[name] * factor).astype(out[name].dtype)
    return out
```

```python
from contextlib import ExitStack

import concourse.bass as bass
from concourse import mybir

F32 = mybir.dt.float32
F16 = mybir.dt.float16
BF16 = mybir.dt.bfloat16
I32 = mybir.dt.int32
U8 = mybir.dt.uint8
ALU = mybir.AluOpType
ACT = mybir.ActivationFunctionType
AX = mybir.AxisListType

P = 128
NB, SEQ, D = 8, 256, 128
QT = SEQ // P
CTX, DC = 1601, 96
NK = (CTX + P - 1) // P
LASTK = CTX - (NK - 1) * P
NH, HD = 16, 8
HALF = NH // 2
XH, XD = 12, 64
KE = DC + 3
SHIFT = DC
NE, EI = 32, 64
EC = NE * EI // P
NG = 8
E2 = 8
EPS = 1e-5
BIG = 60000.0
CHUNKS = [(0, 401), (401, 400), (801, 400), (1201, 400)]
QUADS = [(0, 4), (4, 4), (8, 4), (12, 1)]


class Count:

    def __init__(self, sem, per):
        self.sem, self.per = sem, per

    def at(self, b, n):
        assert 1 <= n <= self.per, (n, self.per)
        return b * self.per + n


def decoder_kernel(nc, d, out, stages=6, batches=NB, dve_steps=1):
    ctx = ExitStack()
    with ctx:
        def sb(name, shape, dt=F32):
            return ctx.enter_context(nc.sbuf_tensor(name, shape, dt))

        def count(name, per):
            return Count(ctx.enter_context(nc.semaphore(name)), per)

        loads = []

        p0 = sb("p0", [P, NH, SEQ])
        p1 = sb("p1", [P, NH, P])
        qtmp = sb("qtmp", [P, 4, 2 * SEQ])
        xp = sb("xp", [P, 2, 4 * SEQ])

        vm = sb("vm", [P, (QT * NH + 1) * P])
        setup = vm[:, 0:XH * (D + KE + DC + 1)].rearrange("p (h n) -> p h n", h=XH)

        def const(name, home=None, at=0):
            src = d[name]
            if home is None:
                t = sb("c_" + name, list(src.shape))[:]
            elif home is setup:
                t = setup[0:src.shape[0], :, at:at + src.shape[2]]
            else:
                flat = home[0:src.shape[0]].rearrange("p a n -> p (a n)")
                t = flat[:, at:at + src.shape[1] * src.shape[2]].rearrange("p (a n) -> p a n", n=src.shape[2])
            loads.append((t, src))
            return t

        ident = const("ident")
        rope = const("rope")
        tri = const("tri")
        hmask = const("hmask")
        onehot = const("onehot", p0, NH * P)
        corner = const("corner")
        before = const("before")
        sel3 = const("sel3", p0)
        first = const("first")
        xcol = const("xcol")
        w0qk = const("w0qk")
        w0v = const("w0v")
        w0o = const("w0o")
        w1qk = const("w1qk")
        w1bqk = const("w1bqk")
        w1tok = const("w1tok")
        b1tok = const("b1tok")
        r1k = const("r1k")
        r1v = const("r1v")
        w1o = const("w1o")
        b1o = const("b1o")
        x0wq = const("x0wq")
        x0wk = const("x0wk")
        x0b = const("x0b")
        x0v = const("x0v")
        x1wq = const("x1wq", p1)
        x1wk = const("x1wk", qtmp)
        x1wv = const("x1wv", xp)
        x1wo = const("x1wo", setup, 0)
        x1b = const("x1b")
        x1bo = const("x1bo")
        gw = const("gw")
        gb = const("gb")
        wg = const("wg")
        wu = const("wu")
        wd = const("wd")
        f_gate = const("f_gate")
        f_we = const("f_we")
        f_wo = const("f_wo")
        NLOAD = len(loads)

        ident16 = sb("ident16", [P, P], F16)
        identb = sb("identb", [P, P], BF16)
        trib = sb("trib", [P, 4, P], BF16)
        onehotb = sb("onehotb", [NH, NH, P], BF16)
        cornerb = sb("cornerb", [1, 2 * P + 1], BF16)
        sel3b = sb("sel3b", [96, EC, P], BF16)
        k1b = sb("k1b", [P, 2])
        bias0 = sb("bias0", [P, 3, D])
        bias1 = sb("bias1", [P, 2, D])
        vfar = sb("vfar", [P, D])
        xk_e = setup[0:XD, :, D:D + KE]
        x0k_e = sb("x0k_e", [P, KE])
        x1v_e = setup[0:XD, :, D + KE:]
        a_mat = sb("a_mat", [P, 1 + XH, KE])
        a_c = sb("a_c", [KE, 1 + XH])
        g_mat = sb("g_mat", [DC + 1, 1 + XH, D + 1])
        f_m = sb("f_m", [P, 2 * D])

        xs = sb("xs", [P, QT, D])
        xt = sb("xt", [P, 1 + SEQ])
        res = sb("res", [P, QT, D])
        st6 = sb("st6", [P, QT, 6])
        mv = sb("mv", [P, QT, 2])
        nr = sb("nr", [P, 4, QT])
        nri = sb("nri", [P, QT], I32)
        carrier = sb("carrier", [P, 1])

        qk = sb("qk", [P, 4, SEQ])
        qk_h = sb("qk_h", [P, 4, SEQ], F16)
        q_l = sb("q_l", [P, 2, SEQ], F16)
        qm_h = sb("qm_h", [P, NH, SEQ], F16)
        qm_l = sb("qm_l", [P, NH, SEQ], F16)
        smax = sb("smax", [P, QT, NH])
        nmb = sb("nmb", [P, QT, NH], BF16)
        nmt = sb("nmt", [NH, SEQ], BF16)
        rden = sb("rden", [P, SEQ])
        ot = sb("ot", [P, SEQ])
        tok = sb("tok", [P, QT, 3, D])
        tok1 = sb("tok1", [P, QT, 2, D])
        near = sb("near", [P, QT, 2, NH])
        prod = sb("prod", [P, QT, 2, D])
        esum = sb("esum", [P, QT, NH])
        wnear = sb("wnear", [P, QT, 2, 2, HALF * HD])

        ct32 = sb("ct32", [P, CTX])
        c_h = sb("c_h", [KE, CTX], F16)
        c_l = sb("c_l", [DC, CTX], F16)
        mrow_u8 = sb("mrow_u8", [P, CTX], U8)
        c_tok = sb("c_tok", [P, NK, DC + 1])
        xq_h = qm_h[0:KE, 0:XH, :]
        xq_l = qm_l[0:KE, 0:XH, :]
        xmax = sb("xmax", [P, QT, 4])
        xneg = sb("xneg", [P, QT], F16)
        xo = sb("xo", [DC + 1, SEQ])
        xr = sb("xr", [P, QT])

        sg = sb("sg", [P, QT, NE])
        sc = sb("sc", [P, QT, NE])
        g2 = sb("g2", [P, 2, QT * NG, 2])
        g1 = sb("g1", [P, 6, QT, NG])
        gr = sb("gr", [P, 3, QT, NG, NG])
        msk = sb("msk", [P, QT, NE])
        rep = sb("rep", [P, QT, NE])
        v8 = sb("v8", [P, QT, 8])
        comb = sb("comb", [P, QT, NE])
        wsum = sb("wsum", [P, QT])
        combt = sb("combt", [NE, SEQ])
        combm = sb("combm", [NE, SEQ], BF16)
        comb3 = sb("comb3", [96, SEQ], BF16)
        tnh = sb("tnh", [P, 2, SEQ])
        h1 = sb("h1", [P, 2, SEQ])
        h2 = sb("h2", [P, 2, SEQ])
        yt = sb("yt", [P, SEQ])
        fp = sb("fp", [P, QT, E2])
        fq = sb("fq", [P, QT, E2])
        fs = sb("fs", [P, 4, QT])

        ps = ctx.enter_context(nc.psum_tensor("ps", [P, 8, 512], F32))

        def bank(i, rows=P, c0=0, n=512):
            return ps[0:rows, i, c0:c0 + n]

        def tiles(ap, n=P):
            return ap.rearrange("p (t n) -> p t n", n=n)

        def value_slots(t, f, off):
            at = (t * NH + f * HALF) * P + off
            return vm[:, at:at + HALF * (P + HD)].rearrange("p (h c) -> p h c", c=P + HD)[:, :, 0:HD]

        def value_of(t, h):
            at = (t * NH + h) * P
            return vm[:, at:at + P]

        loaded = ctx.enter_context(nc.semaphore("loaded"))
        made = ctx.enter_context(nc.semaphore("made"))
        folded = ctx.enter_context(nc.semaphore("folded"))
        unfolded = ctx.enter_context(nc.semaphore("unfolded"))
        dve_self = ctx.enter_context(nc.semaphore("dve_self"))
        x_in = count("x_in", 16)
        ct_in = count("ct_in", 48)
        x_out = count("x_out", 16)
        xt_ready = count("xt_ready", 6)
        xs_ready = count("xs_ready", 6)
        tr_ready = count("tr_ready", 6)
        dstep = count("dve_step", dve_steps)
        def both(name, per):
            return count(name, 2 * per)
        sa_proj = both("sa_proj", 4)
        sa_tok = both("sa_tok", 2)
        sa_qk = both("sa_qk", 4)
        sa_hi = both("sa_hi", 1)
        sa_ks = both("sa_ks", 1)
        sa_qm = both("sa_qm", 2)
        sa_v = both("sa_v", 1)
        sa_x = both("sa_x", 12)
        sa_xd = both("sa_xd", 12)
        sa_nm = both("sa_nm", 1)
        sa_nt = both("sa_nt", 1)
        sa_ntc = both("sa_ntc", 1)
        sa_s = both("sa_s", 6)
        sa_e = both("sa_e", 6)
        sa_u = both("sa_u", 1)
        sa_ot = both("sa_ot", 1)
        sa_y = both("sa_y", 1)
        sa_ne = count("sa_ne", 1)
        sa_nx = count("sa_nx", 1)
        sa_w = count("sa_w", 1)
        U = 1 + XH
        c_hi = count("c_hi", 1)
        c_ext = count("c_ext", 1)
        c_lo = count("c_lo", 1)
        xa_q = count("xa_q", U)
        xa_qh = count("xa_qh", U)
        xa_ql = count("xa_ql", U)
        xa_x = count("xa_x", 8 * U)
        xa_xd = count("xa_xd", 8 * U)
        xa_nm = count("xa_nm", U)
        xa_mr = count("xa_mr", U)
        xa_mc = count("xa_mc", U)
        xa_s = count("xa_s", 4 * U)
        xa_e = count("xa_e", 4 * U)
        xa_pv = count("xa_pv", 4 * U)
        xa_o = count("xa_o", U)
        xa_f = count("xa_f", U)
        xa_a = count("xa_a", U)
        me_l = count("me_l", 1)
        me_t = count("me_t", 1)
        me_c = count("me_c", 1)
        me_ct = count("me_ct", 1)
        me_c3 = count("me_c3", 1)
        me_gu = count("me_gu", EC + 1)
        me_tn = count("me_tn", EC + 1)
        me_cb = count("me_cb", EC)
        me_h = count("me_h", EC + 1)
        me_d = count("me_d", 1)
        me_yt = count("me_yt", 1)
        me_y = count("me_y", 1)
        ff_l = count("ff_l", 1)
        ff_d = count("ff_d", 1)
        ff_e = count("ff_e", 1)
        ff_h = count("ff_h", 1)

        SETUP = 8
        SA_SCALE = HD ** -0.5
        block = ctx.enter_context(nc.Block())

        @block.sync
        def _(sp):
            for t, src in loads:
                sp.dma_start(t[:], src).then_inc(loaded, 16)
            sp.sem_inc(x_out.sem, 16)
            with sp.Fori(0, batches) as b:
                sp.wait_ge(x_out.sem, b * 16 + 16)
                sp.dma_start(xs[:], d["x"][bass.ds(b, 1)].rearrange("a (t p) n -> p (a t) n", p=P)).then_inc(x_in.sem, 16)
                sp.dma_start(ct32[0:DC, :], d["ctxT"][bass.ds(b, 1)].rearrange("a c k -> (a c) k")).then_inc(ct_in.sem, 16)
                sp.dma_start(mrow_u8[DC + 2:DC + 3, :], d["mask"][bass.ds(b, 1), :]).then_inc(ct_in.sem, 16)
                sp.dma_start(c_tok[:, 0:NK - 1, 0:DC],
                             d["ctx"][bass.ds(b, 1), 0:(NK - 1) * P, :].rearrange("a (t p) c -> p (a t) c", p=P)).then_inc(ct_in.sem, 16)
                sp.dma_start(c_tok[0:LASTK, NK - 1, 0:DC],
                             d["ctx"][bass.ds(b, 1), (NK - 1) * P:CTX, :].rearrange("a k c -> (a k) c")).then_inc(ct_in.sem, 16)
                sp.wait_ge(xs_ready.sem, b * stages + stages)
                sp.dma_start(out[bass.ds(b, 1)].rearrange("a (t p) n -> p (a t) n", p=P), xs[:]).then_inc(x_out.sem, 16)
            sp.wait_ge(x_out.sem, batches * 16 + 16)
        ct_in.per = 64
        xs_ready.per = xt_ready.per = tr_ready.per = stages
        STG = stages

        @block.tensor
        def _(pe):
            mm = nc.tensor.matmul
            pe.wait_ge(loaded, 16 * NLOAD)
            pe.wait_ge(made, SETUP)
            for h in range(1 + XH):
                wq, wk = (x0wq[:, :], x0k_e[:, :]) if h == 0 else (x1wq[:, h - 1, :], xk_e[:, h - 1, :])
                bq = x0b[:, 0:1] if h == 0 else x1b[:, 0, h - 1:h]
                if h >= 2:
                    pe.wait_ge(unfolded, 2 * (h - 1))
                mm(bank(h % 2, P, 0, KE), wq, wk, start=True, stop=True)
                mm(bank(h % 2, KE, 256, 1), wk, bq, start=False, stop=True, skip_group_check=True).then_inc(folded, 1)
            for h in range(XH):
                if h >= 2:
                    pe.wait_ge(unfolded, 2 * (1 + XH) + h - 1)
                mm(bank(2 + h % 2, DC + 1, 0, D), x1v_e[:, h, :], x1wo[:, h, :], start=True, stop=True).then_inc(folded, 1)
            for e in range(2):
                mm(bank(4 + e, P, 0, D), f_we[:, e, :], f_wo[:, :], start=True, stop=True).then_inc(folded, 1)
            pe.wait_ge(unfolded, 2 * (1 + XH) + XH + 3)

            def transposes(b, n):
                if n == 0:
                    pe.wait_ge(x_in.sem, x_in.at(b, 16))
                else:
                    pe.wait_ge(xs_ready.sem, xs_ready.at(b, n))
                for t in range(QT):
                    m = nc.tensor.transpose(bank(1, P, t * P, P), xs[:, t, :], ident[:])
                m.then_inc(tr_ready.sem, 1)

            def self_attention(b, i):
                w = w0qk if i == 0 else w1qk
                pe.wait_ge(xt_ready.sem, xt_ready.at(b, 1 + 3 * i))
                x = xt[:, 1:1 + SEQ]
                for j in range(4):
                    if i == 0:
                        mm(bank(j, P, 0, SEQ), w[:, 2 * j, :], x, start=True, stop=True)
                        m = mm(bank(j, P, SEQ, SEQ), w[:, 2 * j + 1, :], x, start=False, stop=True, skip_group_check=True)
                    else:
                        m = mm(bank(j, P, 0, SEQ), w[:, j, :], x, start=True, stop=True)
                    m.then_inc(sa_proj.sem, 1)
                for t in range(QT):
                    if i == 0:
                        m = mm(bank(6, P, t * P, P), xt[:, 1 + t * P:1 + (t + 1) * P], w0v[:], start=(t == 0), stop=True, skip_group_check=True)
                    else:
                        mm(bank(4 + 2 * t, P, 0, 3 * D), xt[:, 1 + t * P:1 + (t + 1) * P], w1tok[:], start=True, stop=True)
                        m = mm(bank(5 + 2 * t, P, 0, 2 * D), xt[:, t * P:(t + 1) * P], w1tok[:, D:], start=True, stop=True)
                    m.then_inc(sa_tok.sem, 1)
                pe.wait_ge(sa_ks.sem, sa_ks.at(b, i + 1))
                pe.wait_ge(sa_qm.sem, sa_qm.at(b, 2 * i + 1))
                g = 0
                trq = trib[:, 2 * i + 1, :]
                for t in range(QT):
                    n = (t + 1) * P
                    per = 512 // n
                    for h0 in range(0, NH, per):
                        if g >= 4:
                            pe.wait_ge(sa_xd.sem, sa_xd.at(b, 12 * i + g - 3))
                        o = ps[:, g % 4, :].rearrange("p (h n) -> p h n", n=n)
                        for k in range(per):
                            mm(o[:, k, t * P:n], identb[:], trq, start=(k == 0), stop=False, skip_group_check=True)
                            if i == 1 and t == 1:
                                mm(o[:, k, P - 1:P], cornerb[0:1, P:2 * P], cornerb[0:1, 2 * P:], start=False, stop=False, skip_group_check=True)
                        for k in range(per):
                            h = h0 + k
                            m = mm(o[:, k, :], qm_h[:, h, t * P:(t + 1) * P], qk_h[:, 2 + h // HALF, 0:n],
                                   start=False, stop=True, skip_group_check=True)
                        m.then_inc(sa_x.sem, 1)
                        g += 1
                pe.wait_ge(sa_nm.sem, sa_nm.at(b, i + 1))
                psb = ps[0:NH, 7, :].bitcast(BF16)
                for t in range(QT):
                    m = nc.tensor.transpose(psb[:, t * P:(t + 1) * P], nmb[:, t, :], identb[:])
                m.then_inc(sa_nt.sem, 1)
                pe.wait_ge(sa_ntc.sem, sa_ntc.at(b, i + 1))
                pe.wait_ge(sa_qm.sem, sa_qm.at(b, 2 * i + 2))
                trk = trib[:, 2 * i, :]

                def scores(g):
                    if g >= 3:
                        pe.wait_ge(sa_e.sem, sa_e.at(b, 6 * i + g - 2))
                    kt, heads = (0, range(4 * g, 4 * g + 4)) if g < 4 else (1, range(8 * (g - 4), 8 * (g - 4) + 8))
                    n = SEQ if kt == 0 else P
                    per = 512 // n
                    for j in range(2):
                        bk = 2 * (g % 3) + j
                        o = ps[:, bk, :].rearrange("p (h n) -> p h n", n=n)
                        hs = heads[j * per:(j + 1) * per]
                        for k, h in enumerate(hs):
                            keys = qk_h[:, 2 + h // HALF, kt * P:(kt + 1) * P]
                            mm(o[:, k, :], keys, qm_h[:, h, SEQ - n:], start=(k == 0), stop=False, skip_group_check=True)
                            if i == 1 and kt == 0:
                                mm(o[:, k, P:P + 1], cornerb[0:1, 0:P], cornerb[0:1, 2 * P:], start=False, stop=False, skip_group_check=True)
                            mm(o[:, k, 0:P], identb[:], trk, start=False, stop=False, skip_group_check=True)
                            mm(o[:, k, :], onehotb[:, h, :], nmt[:, SEQ - n:], start=False, stop=False, skip_group_check=True)
                            m = mm(o[:, k, :], keys, qm_l[:, h, SEQ - n:], start=False, stop=True, skip_group_check=True)
                    m.then_inc(sa_s.sem, 1)

                def values(g):
                    pe.wait_ge(sa_e.sem, sa_e.at(b, 6 * i + g + 1))
                    kt, heads = (0, range(4 * g, 4 * g + 4)) if g < 4 else (1, range(8 * (g - 4), 8 * (g - 4) + 8))
                    for h in heads:
                        o = ps[:, 6 + h // HALF, 0:SEQ]
                        if kt == 0:
                            mm(o, value_of(0, h), p0[:, h, :], start=(h % HALF == 0), stop=(h % HALF == HALF - 1), skip_group_check=True)
                        else:
                            m = mm(o[:, P:], value_of(1, h), p1[:, h, :], start=False, stop=(h % HALF == HALF - 1), skip_group_check=True)
                    if g == 5:
                        if i == 1:
                            pe.wait_ge(sa_w.sem, sa_w.at(b, 1))
                            for f in range(2):
                                for t in range(QT):
                                    m = mm(ps[:, 6 + f, t * P:(t + 1) * P], wnear[:, t, f, :, :].rearrange("p a n -> p (a n)"),
                                           ident[:], start=False, stop=True, skip_group_check=True)
                        m.then_inc(sa_u.sem, 1)

                pe.wait_ge(sa_v.sem, sa_v.at(b, i + 1))
                scores(0)
                for g in range(1, 6):
                    scores(g)
                    values(g - 1)
                values(5)
                pe.wait_ge(sa_ot.sem, sa_ot.at(b, i + 1))
                for t in range(QT):
                    m = mm(bank(0, P, t * P, P), ot[:, t * P:(t + 1) * P], w0o[:] if i == 0 else w1o[:],
                           start=(t == 0), stop=True, skip_group_check=True)
                m.then_inc(sa_y.sem, 1)

            def cross_attention(b, i):
                n_heads, u0 = (1, 0) if i == 0 else (XH, 1)
                pe.wait_ge(xt_ready.sem, xt_ready.at(b, 2 + 3 * i))
                x = xt[:, 1:1 + SEQ]
                for h in range(n_heads):
                    u = u0 + h
                    if h >= 2:
                        pe.wait_ge(xa_ql.sem, xa_ql.at(b, u - 1))
                    mm(bank(6 + h % 2, KE, 0, SEQ), a_mat[:, u, :], x, start=True, stop=True).then_inc(xa_q.sem, 1)
                if i == 0:
                    pe.wait_ge(c_ext.sem, c_ext.at(b, 1))
                    pe.wait_ge(c_hi.sem, c_hi.at(b, 1))
                items = [0]
                done = []

                def ring():
                    n = items[0]
                    items[0] += 1
                    if n >= 2:
                        c, v = done[n - 2]
                        pe.wait_ge(c.sem, c.at(b, v))
                    return n % 2

                def max_pass(h, q):
                    u, t, (k0, n) = u0 + h, q // 4, CHUNKS[q % 4]
                    if q == 0:
                        pe.wait_ge(xa_qh.sem, xa_qh.at(b, u + 1))
                    r = ring()
                    mm(bank(r, P, 0, n), xq_h[:, h, t * P:(t + 1) * P], c_h[:, k0:k0 + n], start=True, stop=True).then_inc(xa_x.sem, 1)
                    done.append((xa_xd, 8 * u + q + 1))

                def max_row(h):
                    u = u0 + h
                    pe.wait_ge(xa_nm.sem, xa_nm.at(b, u + 1))
                    r = ring()
                    for t in range(QT):
                        m = mm(bank(r, 1, t * P, P), xneg[:, t:t + 1], ident16[:], start=(t == 0), stop=True, skip_group_check=True)
                    m.then_inc(xa_mr.sem, 1)
                    done.append((xa_mc, u + 1))

                def scores(h, q):
                    u = u0 + h
                    n = 4 * u + q
                    if q == 0:
                        pe.wait_ge(xa_mc.sem, xa_mc.at(b, u + 1))
                        pe.wait_ge(xa_ql.sem, xa_ql.at(b, u + 1))
                    if h > 0 or q >= 2:
                        pe.wait_ge(xa_e.sem, xa_e.at(b, n - 1))
                    for j in range(QUADS[q][1]):
                        kt = QUADS[q][0] + j
                        m_ = P if kt < NK - 1 else LASTK
                        o = ps[0:m_, 2 + 2 * (q % 2) + j // 2, (j % 2) * SEQ:(j % 2 + 1) * SEQ]
                        ks = slice(kt * P, kt * P + m_)
                        mm(o, c_h[:, ks], xq_h[:, h, :], start=(j % 2 == 0), stop=False, skip_group_check=True)
                        mm(o, c_h[:, ks], xq_l[:, h, :], start=False, stop=False, skip_group_check=True)
                        m = mm(o, c_l[:, ks], xq_h[0:DC, h, :], start=False, stop=True, skip_group_check=True)
                    m.then_inc(xa_s.sem, 1)

                def values(h, q):
                    u = u0 + h
                    pe.wait_ge(xa_e.sem, xa_e.at(b, 4 * u + q + 1))
                    if q == 0 and h > 0:
                        pe.wait_ge(xa_o.sem, xa_o.at(b, u))
                    for j in range(QUADS[q][1]):
                        kt = QUADS[q][0] + j
                        k_ = P if kt < NK - 1 else LASTK
                        m = mm(bank(6, DC + 1, 0, SEQ), c_tok[0:k_, kt, :], xp[0:k_, q % 2, j * SEQ:(j + 1) * SEQ],
                               start=(kt == 0), stop=(kt == NK - 1), skip_group_check=True)
                    m.then_inc(xa_pv.sem, 1)

                def output(h):
                    u = u0 + h
                    pe.wait_ge(xa_o.sem, xa_o.at(b, u + 1))
                    if h > 0:
                        pe.wait_ge(xa_a.sem, xa_a.at(b, u))
                    for t in range(QT):
                        m = mm(ps[:, 7, t * 256:t * 256 + D + 1], xo[:, t * P:(t + 1) * P], g_mat[:, u, :],
                               start=(t == 0), stop=True, skip_group_check=True)
                    m.then_inc(xa_f.sem, 1)

                for q in range(8):
                    max_pass(0, q)
                max_row(0)
                if i == 0:
                    pe.wait_ge(c_lo.sem, c_lo.at(b, 1))
                    pe.wait_ge(ct_in.sem, ct_in.at(b, 64))
                for h in range(n_heads):
                    more = h + 1 < n_heads
                    scores(h, 0)
                    if h > 0:
                        values(h - 1, 2)
                    if more:
                        max_pass(h + 1, 0)
                        max_pass(h + 1, 1)
                    scores(h, 1)
                    if h > 0:
                        values(h - 1, 3)
                    if more:
                        max_pass(h + 1, 2)
                        max_pass(h + 1, 3)
                    if h == 0:
                        pe.wait_ge(xa_ql.sem, xa_ql.at(b, u0 + n_heads))
                    values(h, 0)
                    if more:
                        max_pass(h + 1, 4)
                        max_pass(h + 1, 5)
                    scores(h, 2)
                    if h > 0:
                        output(h - 1)
                    if more:
                        max_pass(h + 1, 6)
                        max_pass(h + 1, 7)
                    values(h, 1)
                    scores(h, 3)
                    if more:
                        max_row(h + 1)
                values(n_heads - 1, 2)
                values(n_heads - 1, 3)
                output(n_heads - 1)

            def experts(b):
                pe.wait_ge(xt_ready.sem, xt_ready.at(b, 3))
                x = xt[:, 1:1 + SEQ]
                for t in range(QT):
                    m = mm(bank(7, P, t * NE, NE), xt[:, 1 + t * P:1 + (t + 1) * P], gw[:], start=(t == 0), stop=True, skip_group_check=True)
                m.then_inc(me_l.sem, 1)

                def up(c):
                    if c >= 2:
                        pe.wait_ge(me_h.sem, me_h.at(b, c - 1))
                    mm(bank(2 + c % 2, P, 0, SEQ), wg[:, c, :], x, start=True, stop=True)
                    mm(bank(2 + c % 2, P, SEQ, SEQ), wu[:, c, :], x, start=False, stop=True, skip_group_check=True).then_inc(me_gu.sem, 1)

                def weights(c):
                    if c == 1:
                        pass
                    if c >= 3:
                        pe.wait_ge(me_h.sem, me_h.at(b, c - 1))
                    mm(bank(4 + c % 2, P, 0, SEQ), sel3b[:, c - 1, :], comb3[:], start=True, stop=True).then_inc(me_cb.sem, 1)

                def down(c):
                    pe.wait_ge(me_h.sem, me_h.at(b, c + 1))
                    m = mm(bank(6, P, 0, SEQ), wd[:, c, :], h2[:, c % 2, :], start=(c == 0), stop=(c == EC), skip_group_check=True)
                    if c == EC:
                        m.then_inc(me_d.sem, 1)

                up(0)
                up(1)
                pe.wait_ge(me_c.sem, me_c.at(b, 1))
                for t in range(QT):
                    m = nc.tensor.transpose(bank(7, NE, t * P, P), comb[:, t, :], ident[:])
                m.then_inc(me_ct.sem, 1)
                pe.wait_ge(me_c3.sem, me_c3.at(b, 1))
                for c in range(1, EC + 1):
                    weights(c)
                    down(c - 1)
                    if c + 1 <= EC:
                        up(c + 1)
                down(EC)
                pe.wait_ge(me_yt.sem, me_yt.at(b, 1))
                for t in range(QT):
                    m = nc.tensor.transpose(bank(0, P, t * P, P), yt[:, t * P:(t + 1) * P], ident[:])
                m.then_inc(me_y.sem, 1)

            def last_ffn(b):
                pe.wait_ge(xt_ready.sem, xt_ready.at(b, 6))
                for t in range(QT):
                    xx = xt[:, 1 + t * P:1 + (t + 1) * P]
                    mm(bank(2, P, t * E2, E2), xx, f_gate[:], start=(t == 0), stop=True, skip_group_check=True)
                    m = mm(bank(3, P, t * 2 * D, 2 * D), xx, f_m[:], start=(t == 0), stop=True, skip_group_check=True)
                m.then_inc(ff_l.sem, 1)

            with pe.Fori(0, batches) as b:
                transposes(b, 0)
                self_attention(b, 0)
                if stages > 1:
                    transposes(b, 1)
                    cross_attention(b, 0)
                if stages > 2:
                    transposes(b, 2)
                    experts(b)
                if stages > 3:
                    transposes(b, 3)
                    self_attention(b, 1)
                if stages > 4:
                    transposes(b, 4)
                    cross_attention(b, 1)
                if stages > 5:
                    transposes(b, 5)
                    last_ffn(b)


        @block.scalar
        def _(act):
            fn = nc.scalar.activation

            def stream(b, n):
                act.wait_ge(tr_ready.sem, tr_ready.at(b, n + 1))
                nc.scalar.copy(xt[:, 1:1 + SEQ], bank(1, P, 0, SEQ)).then_inc(xt_ready.sem, 1)

            def self_attention(b, i):
                if i == 1:
                    for j in range(4):
                        act.wait_ge(sa_proj.sem, sa_proj.at(b, 4 + j + 1))
                        bias = w1bqk[:, j:j + 1] if j < 2 else k1b[:, j - 2:j - 1]
                        fn(qk[:, j, :], bank(j, P, 0, SEQ), ACT.Identity, bias=bias).then_inc(sa_qk.sem, 1)
                act.wait_ge(sa_qk.sem, sa_qk.at(b, 4 * i + 4))
                nc.scalar.copy(qk_h[:], qk[:]).then_inc(sa_hi.sem, 1)
                if i == 0:
                    act.wait_ge(sa_tok.sem, sa_tok.at(b, 2))
                    for t in range(QT):
                        for f in range(2):
                            m = nc.scalar.copy(value_slots(t, f, 0), bank(6, P, t * P + f * HALF * HD, HALF * HD).rearrange("p (h c) -> p h c", c=HD))
                    m.then_inc(sa_v.sem, 1)
                act.wait_ge(sa_nt.sem, sa_nt.at(b, i + 1))
                nc.scalar.copy(nmt[:], ps[0:NH, 7, :].bitcast(BF16)[:, 0:SEQ]).then_inc(sa_ntc.sem, 1)
                if i == 1:
                    act.wait_ge(sa_ne.sem, sa_ne.at(b, 1))
                    fn(near[:], near[:], ACT.Exp, scale=SA_SCALE).then_inc(sa_nx.sem, 1)
                for g in range(6):
                    act.wait_ge(sa_s.sem, sa_s.at(b, 6 * i + g + 1))
                    src = ps[:, 2 * (g % 3):2 * (g % 3) + 2, :].rearrange("p a n -> p (a n)")
                    dst = p0[:, 4 * g:4 * g + 4, :] if g < 4 else p1[:, 8 * (g - 4):8 * (g - 4) + 8, :]
                    fn(dst.rearrange("p h n -> p (h n)"), src, ACT.Exp, scale=SA_SCALE).then_inc(sa_e.sem, 1)

            def cross_attention(b, i):
                n_heads, u0 = (1, 0) if i == 0 else (XH, 1)
                scale = 1.0 if i == 0 else XD ** -0.5
                for h in range(n_heads):
                    u = u0 + h
                    act.wait_ge(xa_q.sem, xa_q.at(b, u + 1))
                    fn(xq_h[:, h, :], bank(6 + h % 2, KE, 0, SEQ), ACT.Identity, bias=a_c[:, u:u + 1]).then_inc(xa_qh.sem, 1)

                def row(h):
                    act.wait_ge(xa_mr.sem, xa_mr.at(b, u0 + h + 1))
                    nc.scalar.copy(xq_h[SHIFT:SHIFT + 1, h, :], bank((9 * h + 8) % 2, 1, 0, SEQ)).then_inc(xa_mc.sem, 1)

                def exps(h, q):
                    n = 4 * (u0 + h) + q
                    act.wait_ge(xa_s.sem, xa_s.at(b, n + 1))
                    if h > 0 or q >= 2:
                        act.wait_ge(xa_pv.sem, xa_pv.at(b, n - 1))
                    k_, w = (P, 4 * SEQ) if q < 3 else (LASTK, SEQ)
                    s0 = 2 + 2 * (q % 2)
                    fn(xp[0:k_, q % 2, 0:w], ps[0:k_, s0:s0 + 2, :].rearrange("p a n -> p (a n)")[:, 0:w], ACT.Exp, scale=scale).then_inc(xa_e.sem, 1)

                def sums(h):
                    u = u0 + h
                    act.wait_ge(xa_pv.sem, xa_pv.at(b, 4 * u + 4))
                    if h > 0:
                        act.wait_ge(xa_f.sem, xa_f.at(b, u))
                    nc.scalar.copy(xo[:], bank(6, DC + 1, 0, SEQ)).then_inc(xa_o.sem, 1)

                row(0)
                for h in range(n_heads):
                    exps(h, 0)
                    exps(h, 1)
                    if h > 0:
                        sums(h - 1)
                    exps(h, 2)
                    exps(h, 3)
                    if h + 1 < n_heads:
                        row(h + 1)
                sums(n_heads - 1)

            def experts(b):
                act.wait_ge(me_l.sem, me_l.at(b, 1))
                fn(sg[:].rearrange("p t n -> p (t n)"), bank(7, P, 0, QT * NE), ACT.Tanh, scale=0.5).then_inc(me_t.sem, 1)
                for c in range(EC + 1):
                    act.wait_ge(me_gu.sem, me_gu.at(b, c + 1))
                    if c >= 2:
                        act.wait_ge(me_h.sem, me_h.at(b, c - 1))
                    fn(tnh[:, c % 2, :], bank(2 + c % 2, P, 0, SEQ), ACT.Tanh, scale=0.5).then_inc(me_tn.sem, 1)
                act.wait_ge(me_d.sem, me_d.at(b, 1))
                nc.scalar.copy(yt[:], bank(6, P, 0, SEQ)).then_inc(me_yt.sem, 1)

            with act.Fori(0, batches) as b:
                stream(b, 0)
                act.wait_ge(ct_in.sem, ct_in.at(b, 64))
                nc.scalar.copy(c_h[0:DC, :], ct32[0:DC, :]).then_inc(c_hi.sem, 1)
                self_attention(b, 0)
                if stages > 1:
                    stream(b, 1)
                    cross_attention(b, 0)
                if stages > 2:
                    stream(b, 2)
                    experts(b)
                if stages > 3:
                    stream(b, 3)
                    self_attention(b, 1)
                if stages > 4:
                    stream(b, 4)
                    cross_attention(b, 1)
                if stages > 5:
                    stream(b, 5)
                    act.wait_ge(ff_d.sem, ff_d.at(b, 1))
                    fn(fp[:], fp[:], ACT.Exp).then_inc(ff_e.sem, 1)

        @block.gpsimd
        def _(pool):
            with pool.Fori(0, batches) as b:
                pool.wait_ge(ct_in.sem, ct_in.at(b, 64))
                pool.wait_ge(made, SETUP)
                pool.wait_ge(c_hi.sem, c_hi.at(b, 1))
                nc.gpsimd.tensor_tensor(c_l[:], ct32[0:DC, :], c_h[0:DC, :], ALU.subtract).then_inc(c_lo.sem, 1)
                nc.gpsimd.tensor_scalar(c_h[DC:KE, :], mrow_u8[DC:KE, :], xcol[DC:KE, 0:1], xcol[DC:KE, 1:2],
                                        ALU.mult, ALU.add).then_inc(c_ext.sem, 1)

        @block.vector
        def _(dve):
            v = nc.vector
            tt, ts, stt, red = v.tensor_tensor, v.tensor_scalar, v.scalar_tensor_tensor, v.tensor_reduce
            v.memset(xk_e, 0.0).then_inc(dve_self, 1)
            v.memset(x0k_e[:], 0.0).then_inc(dve_self, 1)
            v.memset(g_mat[:, :, D:D + 1], 0.0).then_inc(dve_self, 1)
            v.memset(mrow_u8[DC:DC + 2, :], 0.0).then_inc(dve_self, 1)
            v.memset(xt[:, 0:1], 0.0)
            v.memset(c_tok[:, :, DC:DC + 1], 1.0)
            dve.wait_ge(dve_self, 4)
            v.memset(g_mat[DC:DC + 1, :, D:D + 1], 1.0)
            dve.wait_ge(loaded, 16 * NLOAD)
            for dst, src in ((ident16, ident), (identb, ident), (trib, tri), (onehotb, onehot), (cornerb, corner), (sel3b, sel3)):
                v.tensor_copy(dst[:], src[:])
            ts(k1b[:], w1bqk[:, 2:4], w1bqk[:, 4:5], None, ALU.add)
            v.tensor_copy(bias0[:, 0, :], b1tok[:, 0, :])
            tt(bias0[:, 1, :], b1tok[:, 1, :], r1k[:, 2, :], ALU.add)
            tt(bias0[:, 2, :], b1tok[:, 2, :], r1v[:, 2, :], ALU.add)
            tt(bias1[:, 0, :], b1tok[:, 1, :], r1k[:, 1, :], ALU.add)
            tt(bias1[:, 1, :], b1tok[:, 2, :], r1v[:, 1, :], ALU.add)
            tt(vfar[:], b1tok[:, 2, :], r1v[:, 0, :], ALU.add).then_inc(made, 1)
            v.tensor_copy(xk_e[:, :, 0:DC], x1wk[:]).then_inc(made, 1)
            v.tensor_copy(xk_e[:, :, DC + 1], x1b[:, 1, :]).then_inc(made, 1)
            v.tensor_copy(x0k_e[:, 0:DC], x0wk[:]).then_inc(made, 1)
            v.tensor_copy(x0k_e[:, DC + 1:DC + 2], x0b[:, 1:2]).then_inc(made, 1)
            v.tensor_copy(x1v_e[:, :, 0:DC], x1wv[:]).then_inc(made, 1)
            v.tensor_copy(x1v_e[:, :, DC], x1b[:, 2, :]).then_inc(made, 1)
            v.tensor_copy(g_mat[:, 0, 0:D], x0v[:]).then_inc(made, 1)
            for h in range(1 + XH):
                dve.wait_ge(folded, h + 1)
                v.tensor_copy(a_mat[:, h, :], bank(h % 2, P, 0, KE)).then_inc(unfolded, 1)
                xc = xcol[0:KE, 2:3] if h == 0 else xcol[0:KE, 3:4]
                tt(a_c[:, h:h + 1], bank(h % 2, KE, 256, 1), xc, ALU.add).then_inc(unfolded, 1)
            for h in range(XH):
                dve.wait_ge(folded, 1 + XH + h + 1)
                v.tensor_copy(g_mat[:, 1 + h, 0:D], bank(2 + h % 2, DC + 1, 0, D)).then_inc(unfolded, 1)
            for e in range(2):
                dve.wait_ge(folded, 1 + 2 * XH + e + 1)
                v.tensor_copy(f_m[:, e * D:(e + 1) * D], bank(4 + e, P, 0, D)).then_inc(unfolded, 1)
            v.memset(vm[:], 0.0).then_inc(dve_self, 1)
            dve.wait_ge(dve_self, 5)
            for t in range(QT):
                for f in range(2):
                    m = v.memset(value_slots(t, f, HALF * HD), 1.0)
            m.then_inc(unfolded, 1)

            taken = [0]

            def step(ins):
                ins.then_inc(dstep.sem, 1)
                taken[0] += 1

            def settle(b):
                dve.wait_ge(dstep.sem, dstep.at(b, taken[0]))

            def pace():
                v.memset(carrier[:], 0.0)

            def over(ap, n):
                return ap.unsqueeze(ap.ndim).to_broadcast(list(ap.shape) + [n])

            def normalise(b):
                for t in range(QT):
                    m = v.bn_stats(st6[:, t, :], res[:, t, :])
                step(m)
                settle(b)
                pace()
                for t in range(QT):
                    m = v.bn_aggr(mv[:, t, :], st6[:, t, :])
                step(m)
                settle(b)
                var, y, q = nr[:, 0, :], nri[:].bitcast(F32), nr[:, 1, :]
                step(ts(var, mv[:, :, 1], EPS, None, ALU.add))
                settle(b)
                step(ts(nri[:], nr[:, 0, :].bitcast(I32), 1, None, ALU.logical_shift_right))
                settle(b)
                step(ts(nri[:], nri[:], -1.0, float(0x5F3759DF), ALU.mult, ALU.add))
                settle(b)
                for _ in range(3):
                    step(tt(q, y, y, ALU.mult))
                    settle(b)
                    step(tt(q, q, var, ALU.mult))
                    settle(b)
                    step(ts(q, q, -0.5, 1.5, ALU.mult, ALU.add))
                    settle(b)
                    step(tt(y, y, q, ALU.mult))
                    settle(b)
                for t in range(QT):
                    m = ts(xs[:, t, :], res[:, t, :], mv[:, t, 0:1], y[:, t:t + 1], ALU.subtract, ALU.mult)
                m.then_inc(xs_ready.sem, 1)

            def self_attention(b, i):
                if i == 0:
                    dve.wait_ge(x_in.sem, x_in.at(b, 16))
                    for j in range(4):
                        dve.wait_ge(sa_proj.sem, sa_proj.at(b, j + 1))
                        m = tt(qtmp[:, j, :], bank(j), rope[:].rearrange("p a n -> p (a n)"), ALU.mult)
                        step(m)
                    for j in range(4):
                        if j == 0:
                            settle(b)
                        tt(qk[:, j, :], qtmp[:, j, 0:SEQ], qtmp[:, j, SEQ:], ALU.add).then_inc(sa_qk.sem, 1)
                else:
                    for t in range(QT):
                        dve.wait_ge(sa_tok.sem, sa_tok.at(b, 3 + t))
                        kv = bank(4 + 2 * t, P, 0, 3 * D)
                        tt(tok[:, t, :, :].rearrange("p a n -> p (a n)"), kv, bias0[:].rearrange("p a n -> p (a n)"), ALU.add)
                        m = tt(tok1[:, t, :, :].rearrange("p a n -> p (a n)"), bank(5 + 2 * t, P, 0, 2 * D), bias1[:].rearrange("p a n -> p (a n)"), ALU.add)
                        step(m)
                        for f in range(2):
                            fs_ = slice(f * HALF * HD, (f + 1) * HALF * HD)
                            m = tt(value_slots(t, f, 0), bank(4 + 2 * t, P, 2 * D + f * HALF * HD, HALF * HD).rearrange("p (h c) -> p h c", c=HD),
                                   vfar[:, fs_].rearrange("p (h c) -> p h c", c=HD), ALU.add)
                    m.then_inc(sa_v.sem, 1)
                dve.wait_ge(sa_hi.sem, sa_hi.at(b, i + 1))
                dve.wait_ge(sa_qk.sem, sa_qk.at(b, 4 * i + 4))
                h2_ = slice(P // 2, P)
                tt(qk_h[h2_, 2:4, :], qk[h2_, 2:4, :], qk_h[h2_, 2:4, :], ALU.subtract).then_inc(sa_ks.sem, 1)
                step(tt(q_l[:], qk[:, 0:2, :], qk_h[:, 0:2, :], ALU.subtract))
                for h in range(NH):
                    m = ts(qm_h[:, h, :], qk_h[:, h // HALF, :], hmask[:, h % HALF:h % HALF + 1], None, ALU.mult)
                m.then_inc(sa_qm.sem, 1)
                g = 0
                for t in range(QT):
                    n = (t + 1) * P
                    per = 512 // n
                    for h0 in range(0, NH, per):
                        dve.wait_ge(sa_x.sem, sa_x.at(b, 12 * i + g + 1))
                        red(smax[:, t, h0:h0 + per], ps[:, g % 4, :].rearrange("p (h n) -> p h n", n=n), AX.X, ALU.max).then_inc(sa_xd.sem, 1)
                        g += 1
                        if g == 4:
                            settle(b)
                            for h in range(NH):
                                m = ts(qm_l[:, h, :], q_l[:, h // HALF, :], hmask[:, h % HALF:h % HALF + 1], None, ALU.mult)
                            m.then_inc(sa_qm.sem, 1)
                if i == 0:
                    dve.wait_ge(sa_xd.sem, sa_xd.at(b, 12))
                    ts(nmb[:], smax[:], -1.0, None, ALU.mult).then_inc(sa_nm.sem, 1)
                else:
                    tt(prod[:, :, 0, :], tok[:, :, 0, :], tok[:, :, 1, :], ALU.mult)
                    step(tt(prod[:, :, 1, :], tok[:, :, 0, :], tok1[:, :, 0, :], ALU.mult))
                    settle(b)
                    step(red(near[:], prod[:].rearrange("p t a (h c) -> p (t a h) c", c=HD), AX.X, ALU.add))
                    settle(b)
                    step(tt(near[:, :, 1, :], near[:, :, 1, :], first[:], ALU.add))
                    dve.wait_ge(sa_xd.sem, sa_xd.at(b, 24))
                    step(tt(smax[:], smax[:], near[:, :, 0, :], ALU.max))
                    settle(b)
                    step(tt(smax[:], smax[:], near[:, :, 1, :], ALU.max))
                    settle(b)
                    ts(nmb[:], smax[:], -1.0, None, ALU.mult).then_inc(sa_nm.sem, 1)
                    dve.wait_ge(sa_nm.sem, sa_nm.at(b, 2))
                    for j in range(2):
                        m = tt(near[:, :, j, :], near[:, :, j, :], nmb[:], ALU.add)
                    m.then_inc(sa_ne.sem, 1)
                    dve.wait_ge(sa_nx.sem, sa_nx.at(b, 1))
                    for t in range(QT):
                        tt(prod[:, t, 0, :].rearrange("p (h c) -> p h c", c=HD), tok[:, t, 2, :].rearrange("p (h c) -> p h c", c=HD), over(near[:, t, 0, :], HD), ALU.mult)
                        m = tt(prod[:, t, 1, :].rearrange("p (h c) -> p h c", c=HD), tok1[:, t, 1, :].rearrange("p (h c) -> p h c", c=HD), over(near[:, t, 1, :], HD), ALU.mult)
                    step(m)
                    step(tt(esum[:], near[:, :, 0, :], near[:, :, 1, :], ALU.add))
                    settle(b)
                    for t in range(QT):
                        tt(wnear[:, t, :, 0, :], prod[:, t, 0, :].rearrange("p (f n) -> p f n", f=2), prod[:, t, 1, :].rearrange("p (f n) -> p f n", f=2), ALU.add)
                        for f in range(2):
                            m = v.tensor_copy(wnear[:, t, f, 1, :].rearrange("p (h c) -> p h c", c=HD), over(esum[:, t, f * HALF:(f + 1) * HALF], HD))
                    m.then_inc(sa_w.sem, 1)
                    step(tt(res[:], xs[:], b1o[:].unsqueeze(1).to_broadcast([P, QT, D]), ALU.add))
                dve.wait_ge(sa_u.sem, sa_u.at(b, i + 1))
                for f in range(2):
                    m = v.reciprocal(rden[64 * f:64 * f + 64, :], ps[64:128, 6 + f, 0:SEQ])
                step(m)
                settle(b)
                for f in range(2):
                    m = tt(ot[64 * f:64 * f + 64, :], ps[0:64, 6 + f, 0:SEQ], rden[64 * f:64 * f + 64, :], ALU.mult)
                m.then_inc(sa_ot.sem, 1)
                dve.wait_ge(sa_y.sem, sa_y.at(b, i + 1))
                step(tt(res[:], tiles(bank(0, P, 0, SEQ)), xs[:] if i == 0 else res[:], ALU.add))
                settle(b)
                normalise(b)

            def cross_attention(b, i):
                n_heads, u0 = (1, 0) if i == 0 else (XH, 1)
                if i == 1:
                    dve.wait_ge(xs_ready.sem, xs_ready.at(b, 4))
                    step(tt(res[:], xs[:], x1bo[:].unsqueeze(1).to_broadcast([P, QT, D]), ALU.add))
                for h in range(n_heads):
                    u = u0 + h
                    dve.wait_ge(xa_qh.sem, xa_qh.at(b, u + 1))
                    stt(xq_l[:, h, :], bank(6 + h % 2, KE, 0, SEQ), a_c[:, u:u + 1], xq_h[:, h, :], ALU.add, ALU.subtract).then_inc(xa_ql.sem, 1)

                def chunk(h, q):
                    t, c = q // 4, q % 4
                    dve.wait_ge(xa_x.sem, xa_x.at(b, 8 * (u0 + h) + q + 1))
                    red(xmax[:, t, c:c + 1], bank((9 * h + q) % 2, P, 0, CHUNKS[c][1]), AX.X, ALU.max).then_inc(xa_xd.sem, 1)

                def highest(h):
                    dve.wait_ge(xa_xd.sem, xa_xd.at(b, 8 * (u0 + h) + 8))
                    if h > 0:
                        dve.wait_ge(xa_mr.sem, xa_mr.at(b, u0 + h))
                    red(xneg[:], xmax[:], AX.X, ALU.max, negate=True).then_inc(xa_nm.sem, 1)

                def add(h):
                    u = u0 + h
                    dve.wait_ge(xa_f.sem, xa_f.at(b, u + 1))
                    step(v.reciprocal(xr[:], ps[:, 7, :].rearrange("p (t n) -> p t n", n=256)[:, :, D]))
                    settle(b)
                    for t in range(QT):
                        m = stt(res[:, t, :], ps[:, 7, t * 256:t * 256 + D], xr[:, t:t + 1],
                                xs[:, t, :] if i == 0 else res[:, t, :], ALU.mult, ALU.add)
                    m.then_inc(xa_a.sem, 1)

                for q in range(8):
                    chunk(0, q)
                highest(0)
                for h in range(n_heads):
                    more = h + 1 < n_heads
                    if more:
                        for q in range(6):
                            chunk(h + 1, q)
                    if h > 0:
                        add(h - 1)
                    if more:
                        chunk(h + 1, 6)
                        chunk(h + 1, 7)
                        highest(h + 1)
                add(n_heads - 1)
                dve.wait_ge(xa_a.sem, xa_a.at(b, u0 + n_heads))
                normalise(b)

            def experts(b):
                dve.wait_ge(me_t.sem, me_t.at(b, 1))
                step(ts(sg[:], sg[:], 0.5, 0.5, ALU.mult, ALU.add))
                settle(b)
                step(tt(sc[:], sg[:], gb[:].unsqueeze(1).to_broadcast([P, QT, NE]), ALU.add))
                settle(b)
                pair = sc[:].rearrange("p t (g a c) -> p (t g) a c", a=2, c=2)
                tt(g2[:, 0, :, :], pair[:, :, :, 0], pair[:, :, :, 1], ALU.max)
                step(tt(g2[:, 1, :, :], pair[:, :, :, 0], pair[:, :, :, 1], ALU.min))
                settle(b)
                gg = g1[:].rearrange("p a t g -> p a (t g)")
                tt(gg[:, 0, :], g2[:, 0, :, 0], g2[:, 0, :, 1], ALU.max)
                tt(gg[:, 1, :], g2[:, 0, :, 0], g2[:, 0, :, 1], ALU.min)
                step(tt(gg[:, 2, :], g2[:, 1, :, 0], g2[:, 1, :, 1], ALU.max))
                settle(b)
                step(tt(gg[:, 1, :], gg[:, 1, :], gg[:, 2, :], ALU.max))
                settle(b)
                step(tt(gg[:, 3, :], gg[:, 0, :], gg[:, 1, :], ALU.add))
                settle(b)
                for t in range(QT):
                    gj = g1[:, 3, t, :].unsqueeze(1).to_broadcast([P, NG, NG])
                    gi = over(g1[:, 3, t, :], NG)
                    tt(gr[:, 0, t, :, :], gj, gi, ALU.is_gt)
                    m = tt(gr[:, 1, t, :, :], gj, gi, ALU.is_equal)
                step(m)
                settle(b)
                for t in range(QT):
                    m = tt(gr[:, 1, t, :, :], gr[:, 1, t, :, :], before[:], ALU.mult)
                step(m)
                settle(b)
                step(tt(gr[:, 2, :, :, :], gr[:, 0, :, :, :], gr[:, 1, :, :, :], ALU.add))
                settle(b)
                step(red(g1[:, 4, :, :], gr[:, 2, :, :, :], AX.X, ALU.add))
                settle(b)
                step(ts(g1[:, 5, :, :], g1[:, 4, :, :], 4.0, None, ALU.is_lt))
                settle(b)
                step(tt(msk[:].rearrange("p t (g c) -> p (t g) c", c=NE // NG), sc[:].rearrange("p t (g c) -> p (t g) c", c=NE // NG),
                        over(gg[:, 5, :], NE // NG), ALU.mult))
                settle(b)
                step(ts(msk[:], msk[:], 0.0, None, ALU.add))
                settle(b)
                pace()
                for t in range(QT):
                    m = v.max(v8[:, t, :], msk[:, t, :])
                step(m)
                settle(b)
                pace()
                for t in range(QT):
                    m = v.match_replace(rep[:, t, :], v8[:, t, :], msk[:, t, :], -1e30)
                step(m)
                settle(b)
                step(tt(rep[:], rep[:], msk[:], ALU.not_equal))
                settle(b)
                step(tt(comb[:], rep[:], sg[:], ALU.mult))
                settle(b)
                step(red(wsum[:], comb[:], AX.X, ALU.add))
                settle(b)
                step(ts(wsum[:], wsum[:], 1e-20, None, ALU.add))
                settle(b)
                step(v.reciprocal(wsum[:], wsum[:]))
                settle(b)
                for t in range(QT):
                    m = ts(comb[:, t, :], comb[:, t, :], wsum[:, t:t + 1], 1.25, ALU.mult, ALU.mult)
                m.then_inc(me_c.sem, 1)
                dve.wait_ge(me_ct.sem, me_ct.at(b, 1))
                step(v.tensor_copy(combt[:], bank(7, NE, 0, SEQ)))
                settle(b)
                step(v.tensor_copy(comb3[0:NE, :], combt[:]))
                settle(b)
                step(tt(combt[:], combt[:], comb3[0:NE, :], ALU.subtract))
                settle(b)
                step(v.tensor_copy(combm[:], combt[:]))
                settle(b)
                v.tensor_copy(comb3[NE:2 * NE, :], combm[:])
                step(tt(combt[:], combt[:], combm[:], ALU.subtract))
                settle(b)
                v.tensor_copy(comb3[2 * NE:, :], combt[:]).then_inc(me_c3.sem, 1)
                for c in range(EC + 1):
                    s = c % 2
                    dve.wait_ge(me_tn.sem, me_tn.at(b, c + 1))
                    step(stt(h1[:, s, :], tnh[:, s, :], 1.0, bank(2 + s, P, 0, SEQ), ALU.add, ALU.mult))
                    settle(b)
                    if c == 0:
                        stt(h2[:, s, :], h1[:, s, :], 0.5, bank(2 + s, P, SEQ, SEQ), ALU.mult, ALU.mult).then_inc(me_h.sem, 1)
                    else:
                        step(tt(h1[:, s, :], h1[:, s, :], bank(2 + s, P, SEQ, SEQ), ALU.mult))
                        settle(b)
                        dve.wait_ge(me_cb.sem, me_cb.at(b, c))
                        tt(h2[:, s, :], h1[:, s, :], bank(4 + s, P, 0, SEQ), ALU.mult).then_inc(me_h.sem, 1)
                dve.wait_ge(me_y.sem, me_y.at(b, 1))
                step(tt(res[:], tiles(bank(0, P, 0, SEQ)), xs[:], ALU.add))
                settle(b)
                normalise(b)

            def last_ffn(b):
                lg = bank(2, P, 0, QT * E2).rearrange("p (t n) -> p t n", n=E2)
                dve.wait_ge(ff_l.sem, ff_l.at(b, 1))
                step(red(fs[:, 0, :], lg, AX.X, ALU.max))
                settle(b)
                tt(fp[:], lg, over(fs[:, 0, :], E2), ALU.subtract).then_inc(ff_d.sem, 1)
                dve.wait_ge(ff_e.sem, ff_e.at(b, 1))
                step(red(fs[:, 1, :], fp[:], AX.X, ALU.add))
                settle(b)
                step(v.reciprocal(fs[:, 1, :], fs[:, 1, :]))
                settle(b)
                step(tt(fp[:], fp[:], over(fs[:, 1, :], E2), ALU.mult))
                settle(b)
                step(ts(fq[:], fp[:], 0.3, None, ALU.is_gt))
                settle(b)
                step(red(fs[:, 2, :], fq[:], AX.X, ALU.add))
                settle(b)
                step(ts(fs[:, 3, :], fs[:, 2, :], -1.0, float(E2), ALU.mult, ALU.add))
                settle(b)
                tt(fs[:, 3, :], fs[:, 3, :], fp[:, :, 0], ALU.mult)
                step(tt(fs[:, 2, :], fs[:, 2, :], fp[:, :, 1], ALU.mult))
                settle(b)
                for t in range(QT):
                    m = stt(res[:, t, :], bank(3, P, t * 2 * D, D), fs[:, 3, t:t + 1], xs[:, t, :], ALU.mult, ALU.add)
                step(m)
                settle(b)
                for t in range(QT):
                    m = stt(res[:, t, :], bank(3, P, t * 2 * D + D, D), fs[:, 2, t:t + 1], res[:, t, :], ALU.mult, ALU.add)
                step(m)
                settle(b)
                normalise(b)

            with dve.Fori(0, batches) as b:
                self_attention(b, 0)
                if stages > 1:
                    cross_attention(b, 0)
                if stages > 2:
                    experts(b)
                if stages > 3:
                    self_attention(b, 1)
                if stages > 4:
                    cross_attention(b, 1)
                if stages > 5:
                    last_ffn(b)
            assert taken[0] == dve_steps, taken[0]


def shape_constants():
    import numpy as np
    f = np.float32
    c = {"ident": np.eye(P, dtype=f)}
    inv = (1.0 / f(10000.0) ** (np.arange(0, HD, 2, dtype=f) / f(HD))).astype(f)
    fr = (np.arange(SEQ, dtype=f)[:, None] * inv[None, :]).astype(f)
    emb = np.repeat(fr, 2, axis=-1)
    cos, sin = np.cos(emb).astype(f).T, np.sin(emb).astype(f).T
    sign = np.where(np.arange(HD) % 2 == 0, -1.0, 1.0).astype(f)[:, None]
    c["rope"] = np.stack([np.tile(cos, (P // HD, 1)), np.tile(sin * sign, (P // HD, 1))], 1).astype(f)
    k, q = np.arange(P)[:, None], np.arange(P)[None, :]
    no = f(-1e30)
    c["tri"] = np.stack([np.where(k > q, no, 0), np.where(q > k, no, 0),
                         np.where(k > q - 2, no, 0), np.where(q > k - 2, no, 0)], 1).astype(f)
    c["hmask"] = ((np.arange(P) % 64 // HD)[:, None] == np.arange(HALF)[None, :]).astype(f)
    c["onehot"] = np.repeat(np.eye(NH, dtype=f)[:, :, None], P, 2)
    corner = np.zeros((1, 2 * P + 1), f)
    corner[0, P - 1], corner[0, P], corner[0, 2 * P] = 1, 1, no
    c["corner"] = corner
    j, g = np.arange(NG)[None, :], np.arange(NG)[:, None]
    c["before"] = np.broadcast_to((j < g).astype(f), (P, NG, NG)).copy()
    e, cc, m = np.arange(96) % NE, np.arange(EC), np.arange(P)
    c["sel3"] = (e[:, None, None] == 2 * cc[None, :, None] + m[None, None, :] // EI).astype(f)
    first = np.zeros((P, QT, NH), f)
    first[0, 0] = no
    c["first"] = first
    xcol = np.zeros((P, 4), f)
    xcol[DC:DC + 2, 1] = 1
    xcol[DC + 2, 0] = -BIG
    xcol[DC + 2, 3] = BIG
    c["xcol"] = xcol
    return c


def layouts(a):
    import numpy as np
    f = np.float32
    c = {}

    def halves(w):
        return np.stack([np.concatenate([w[:, 64 * k:64 * k + 64]] * 2, 1) for k in range(2)], 1)

    def rows(r):
        return np.ascontiguousarray(np.broadcast_to(r, (P,) + r.shape))

    swap = np.arange(D) ^ 1
    wq, wk = a["L0_attn_Wq"].T, a["L0_attn_Wk"].T
    c["w0qk"] = np.stack([x for w in (wq, wk) for k in range(2) for x in (halves(w)[:, k], halves(w[:, swap])[:, k])], 1)
    c["w0v"], c["w0o"] = a["L0_attn_Wv"].T, a["L0_attn_Wo"].T
    c["w1qk"] = np.concatenate([halves(a["L1_attn_W_q"]), halves(a["L1_attn_W_k"])], 1)
    bq, bk = a["L1_attn_b_q"], a["L1_attn_b_k"]
    rk, rv = a["L1_attn_rel_k_table"], a["L1_attn_rel_v_table"]
    twice = lambda x: [np.tile(x[:64], 2), np.tile(x[64:], 2)]
    c["w1bqk"] = np.stack(twice(bq) + twice(bk) + [np.tile(rk[0], P // HD)], 1)
    c["w1tok"] = np.concatenate([a["L1_attn_W_q"], a["L1_attn_W_k"], a["L1_attn_W_v"]], 1)
    c["b1tok"] = rows(np.stack([bq, bk, a["L1_attn_b_v"]]))
    c["r1k"] = rows(np.stack([np.tile(rk[n], NH) for n in range(3)]))
    c["r1v"] = rows(np.stack([np.tile(rv[n], NH) for n in range(3)]))
    c["w1o"], c["b1o"] = a["L1_attn_W_o"], rows(a["L1_attn_b_o"])
    c["x0wq"], c["x0wk"] = a["L0_xattn_Wq"].T, a["L0_xattn_Wk"].T
    c["x0b"] = np.stack([a["L0_xattn_bq"], a["L0_xattn_bk"]], 1)
    c["x0v"] = np.concatenate([a["L0_xattn_Wv"], a["L0_xattn_bv"][None]], 0)
    heads = lambda w: w.reshape(XH, XD, -1).transpose(1, 0, 2)
    c["x1wq"], c["x1wk"], c["x1wv"] = heads(a["L1_xattn_Wq"]), heads(a["L1_xattn_Wk"]), heads(a["L1_xattn_Wv"])
    c["x1wo"] = heads(a["L1_xattn_Wo"].T)
    c["x1b"] = np.stack([a[n].reshape(XH, XD).T for n in ("L1_xattn_bq", "L1_xattn_bk", "L1_xattn_bv")], 1)
    c["x1bo"] = rows(a["L1_xattn_bo"])
    c["gw"], c["gb"] = a["L0_ffn_gate_w"].T, rows(a["L0_ffn_gate_bias"])
    up = lambda w, s: np.concatenate([s.T[:, None, :], w.reshape(EC, P, D).transpose(2, 0, 1)], 1)
    c["wg"], c["wu"] = up(a["L0_ffn_w_gate"], a["L0_ffn_sh_gate"]), up(a["L0_ffn_w_up"], a["L0_ffn_sh_up"])
    wd = a["L0_ffn_w_down"].transpose(0, 2, 1).reshape(EC, P, D).transpose(1, 0, 2)
    c["wd"] = np.concatenate([a["L0_ffn_sh_down"].T[:, None, :], wd], 1)
    c["f_gate"] = a["L1_ffn_gate_W"].T
    c["f_we"] = a["L1_ffn_expert_W"][0:2].transpose(1, 0, 2)
    c["f_wo"] = a["L1_ffn_out_W"].T
    c["x"], c["ctx"] = a["x"], a["ctx_768"]
    c["ctxT"] = a["ctx_768"].transpose(0, 2, 1)
    c["mask"] = a["mask_BxS2_bk0"]
    return c


def kernel(**inputs):
    import numpy as np
    import concourse.bacc as bacc
    from concourse.bass_utils import run_bass_kernel_spmd

    tables = dict(shape_constants())
    tables.update(layouts({k: np.asarray(v) for k, v in inputs.items()}))
    nc = bacc.Bacc("TRN2", target_bir_lowering=False, num_devices=1)
    arrays, d = {}, {}
    for name, t in tables.items():
        t = np.ascontiguousarray(t)
        arrays["in_" + name] = t
        d[name] = nc.dram_tensor("in_" + name, t.shape, mybir.dt.from_np(t.dtype), kind="ExternalInput").ap()
    out = nc.dram_tensor("out_0", (NB, SEQ, D), F32, kind="ExternalOutput").ap()
    decoder_kernel(nc, d, out, dve_steps=DVE_STEPS)
    r = run_bass_kernel_spmd(nc, [arrays], core_ids=[0])
    return r.results[0]["out_0"]


DVE_STEPS = 205
```

```python
from contextlib import ExitStack

import concourse.bass as bass
from concourse import mybir

F32 = mybir.dt.float32
F16 = mybir.dt.float16
BF16 = mybir.dt.bfloat16
I32 = mybir.dt.int32
U8 = mybir.dt.uint8
ALU = mybir.AluOpType
ACT = mybir.ActivationFunctionType
AX = mybir.AxisListType

P = 128
NB, SEQ, D = 8, 256, 128
QT = SEQ // P
CTX, DC = 1601, 96
NK = (CTX + P - 1) // P
LASTK = CTX - (NK - 1) * P
NH, HD = 16, 8
HALF = NH // 2
XH, XD = 12, 64
KE = DC + 3
SHIFT = DC
NE, EI = 32, 64
EC = NE * EI // P
NG = 8
E2 = 8
EPS = 1e-5
BIG = 60000.0
CHUNKS = [(0, 401), (401, 400), (801, 400), (1201, 400)]
NPAIR = (NK + 1) // 2


class Count:

    def __init__(self, sem, per):
        self.sem, self.per = sem, per

    def at(self, b, n):
        assert 1 <= n <= self.per, (n, self.per)
        return b * self.per + n


def weave(front, cross, weights, n_cross):
    total, done, b = sum(weights), 0, 0
    for w in weights:
        while (2 * b + 1) * total <= (2 * done + w) * n_cross and b < n_cross:
            next(cross)
            b += 1
        next(front)
        done += w
    while b < n_cross:
        next(cross)
        b += 1


def chain(*parts):
    for p in parts:
        yield from p


def counted(pieces, n):
    taken = 0
    for p in pieces:
        taken += 1
        yield
    assert taken == n, (taken, n)


def pair_tiles(p):
    return [(kt, P if kt < NK - 1 else LASTK) for kt in (2 * p, 2 * p + 1) if kt < NK]


def next_chunks(h, p):
    if p >= 4:
        return [(h + 2, p - 4)] if h + 2 < XH else []
    return [(h + 1, q) for q in ((3,), (4,), (5, 6), (7,))[p]] if h + 1 < XH else []


CHUNK_BANK = [4, 0, 4, 0, 4, 0, 4, 4]
AHEAD = 3


def decoder_kernel(nc, d, out, dve_steps):
    ctx = ExitStack()
    with ctx:
        def sb(name, shape, dt=F32):
            return ctx.enter_context(nc.sbuf_tensor(name, shape, dt))

        def count(name, per=1):
            return Count(ctx.enter_context(nc.semaphore(name)), per)

        loads = []

        qk = sb("qk", [P, 4, SEQ])
        qtmp = sb("qtmp", [P, 4, 2 * SEQ])
        pr = sb("pr", [P, 4, 2 * SEQ])
        xp = sb("xp", [P, 3, 2 * SEQ])
        qm_h = sb("qm_h", [P, NH, SEQ], F16)
        qm_l = sb("qm_l", [P, NH, SEQ], F16)
        vm = sb("vm", [P, (QT * NH + 1) * P])
        setup = vm[:, 0:XH * (D + KE + DC + 1)].rearrange("p (h n) -> p h n", h=XH)

        def flat(t):
            return t.rearrange("p a n -> p (a n)")

        def const(name, home=None, at=0):
            src = d[name]
            if home is None:
                t = sb("c_" + name, list(src.shape))[:]
            elif home is setup:
                t = setup[0:src.shape[0], :, at:at + src.shape[2]]
            else:
                t = home[0:src.shape[0], at:at + src.shape[1] * src.shape[2]].rearrange("p (a n) -> p a n", n=src.shape[2])
            loads.append((t, src))
            return t

        ident = const("ident")
        rope = const("rope")
        tri = const("tri", flat(qk[:]))
        hmask = const("hmask")
        onehot = const("onehot", flat(qm_h[:]).bitcast(F32))
        corner = const("corner")
        before = const("before")
        sel3 = const("sel3", flat(pr[:]))
        first = const("first")
        xcol = const("xcol")
        w0qk = const("w0qk")
        w0v = const("w0v")
        w0o = const("w0o")
        w1qk = const("w1qk")
        w1bqk = const("w1bqk")
        w1tok = const("w1tok")
        b1tok = const("b1tok", flat(qtmp[:]), 1152)
        r1k = const("r1k", flat(qtmp[:]), 1536)
        r1v = const("r1v", flat(qm_l[:]).bitcast(F32), 1536)
        w1o = const("w1o")
        b1o = const("b1o")
        x0wq = const("x0wq")
        x0wk = const("x0wk")
        x0b = const("x0b")
        x0v = const("x0v")
        x1wq = const("x1wq", flat(qm_l[:]).bitcast(F32))
        x1wk = const("x1wk", flat(qtmp[:]))
        x1wv = const("x1wv", flat(xp[:]))
        x1wo = const("x1wo", setup, 0)
        x1b = const("x1b")
        x1bo = const("x1bo")
        gw = const("gw")
        gb = const("gb")
        wg = const("wg")
        wu = const("wu")
        wd = const("wd")
        f_gate = const("f_gate")
        f_we = const("f_we")
        f_wo = const("f_wo")
        NLOAD = len(loads)

        ident16 = sb("ident16", [P, P], F16)
        identb = sb("identb", [P, P], BF16)
        trib = sb("trib", [P, 4, P], BF16)
        onehotb = sb("onehotb", [NH, NH, P], BF16)
        cornerb = sb("cornerb", [1, 2 * P + 1], BF16)
        sel3b = sb("sel3b", [96, EC, P], BF16)
        k1b = sb("k1b", [P, 2])
        bias0 = sb("bias0", [P, 3, D])
        bias1 = sb("bias1", [P, 2, D])
        vfar = sb("vfar", [P, D])
        xk_e = setup[0:XD, :, D:D + KE]
        x0k_e = sb("x0k_e", [P, KE])
        x1v_e = setup[0:XD, :, D + KE:]
        a_mat = sb("a_mat", [P, 1 + XH, KE])
        a_c = sb("a_c", [KE, 1 + XH])
        g_mat = sb("g_mat", [DC + 1, 1 + XH, D + 1])
        f_m = sb("f_m", [P, 2 * D])

        xin = sb("xin", [P, QT, D])
        xsf = sb("xsf", [P, QT, D])
        xsx = sb("xsx", [P, QT, D])
        xst = sb("xst", [P, QT, D])
        ys = sb("ys", [P, QT, D])
        source = [xin, xsf, xsf, xsf, xsx, xst, ys]

        class Side:

            def __init__(self, c):
                self.xt = sb("xt" + c, [P, 1 + SEQ])
                self.res = sb("res" + c, [P, QT, D])
                self.st6 = sb("st6" + c, [P, QT, 6])
                self.mv = sb("mv" + c, [P, QT, 2])
                self.nr = sb("nr" + c, [P, 2, QT])
                self.nri = sb("nri" + c, [P, QT], I32)
                self.xmax = sb("xmax" + c, [P, QT, 4])
                self.xneg = sb("xneg" + c, [P, QT], F16)
                self.xo = sb("xo" + c, [DC + 1, SEQ])
                self.xr = sb("xr" + c, [P, QT])

        front, cross = Side("_f"), Side("_x")
        carrier = sb("carrier", [P, 1])
        pool_carrier = sb("pool_carrier", [P // 4, 1])

        qk_h = sb("qk_h", [P, 4, SEQ], F16)
        q_l = sb("q_l", [P, 2, SEQ], F16)
        smax = sb("smax", [P, QT, NH])
        nmb = sb("nmb", [P, QT, NH], BF16)
        nmt = sb("nmt", [NH, SEQ], BF16)
        rden = sb("rden", [P, SEQ])
        ot = sb("ot", [P, SEQ])
        tok = sb("tok", [P, QT, 3, D])
        tok1 = sb("tok1", [P, QT, 2, D])
        near = sb("near", [P, QT, 2, NH])
        prod = sb("prod", [P, QT, 2, D])
        esum = sb("esum", [P, QT, NH])
        wnear = sb("wnear", [P, QT, 2, 2, HALF * HD])

        ct32 = sb("ct32", [P, CTX])
        mrow_u8 = sb("mrow_u8", [P, CTX], U8)

        class Context:
            def __init__(self, c):
                self.h = sb("c_h" + c, [KE, CTX], F16)
                self.l = sb("c_l" + c, [DC, CTX], F16)
                self.tok = sb("c_tok" + c, [P, NK, DC + 1])

        cf, cx = Context("_f"), Context("_x")
        xq_h = sb("xq_h", [KE, XH, SEQ], F16)
        xq_l = sb("xq_l", [KE, XH, SEQ], F16)
        x0q_h = sb("x0q_h", [KE, 1, SEQ], F16)
        x0q_l = sb("x0q_l", [KE, 1, SEQ], F16)

        sg = sb("sg", [P, QT, NE])
        sc = sb("sc", [P, QT, NE])
        g2 = sb("g2", [P, 2, QT * NG, 2])
        g1 = sb("g1", [P, 6, QT, NG])
        gr = sb("gr", [P, 3, QT, NG, NG])
        msk = sb("msk", [P, QT, NE])
        rep = sb("rep", [P, QT, NE])
        v8 = sb("v8", [P, QT, 8])
        comb = sb("comb", [P, QT, NE])
        wsum = sb("wsum", [P, QT])
        combt = sb("combt", [NE, SEQ])
        combm = sb("combm", [NE, SEQ], BF16)
        comb3 = sb("comb3", [96, SEQ], BF16)
        tnh = sb("tnh", [P, SEQ])
        h1 = sb("h1", [P, SEQ])
        h2 = sb("h2", [P, 2, SEQ])
        yt = tnh
        fp = sb("fp", [P, QT, E2])
        fq = sb("fq", [P, QT, E2])
        fs = sb("fs", [P, 4, QT])

        ps = ctx.enter_context(nc.psum_tensor("ps", [P, 8, 512], F32))

        def bank(i, rows=P, c0=0, n=512):
            return ps[0:rows, i, c0:c0 + n]

        def tiles(ap, n=P):
            return ap.rearrange("p (t n) -> p t n", n=n)

        def value_slots(t, f, off):
            at = (t * NH + f * HALF) * P + off
            return vm[:, at:at + HALF * (P + HD)].rearrange("p (h c) -> p h c", c=P + HD)[:, :, 0:HD]

        def value_of(t, h):
            at = (t * NH + h) * P
            return vm[:, at:at + P]

        def xp_slot(i, n):
            return xp[:, n % 3, :] if i == 1 else pr[:, n % 4, :]

        loaded = ctx.enter_context(nc.semaphore("loaded"))
        made = ctx.enter_context(nc.semaphore("made"))
        folded = ctx.enter_context(nc.semaphore("folded"))
        unfolded = ctx.enter_context(nc.semaphore("unfolded"))
        dve_self = ctx.enter_context(nc.semaphore("dve_self"))
        dve_step = ctx.enter_context(nc.semaphore("dve_step"))
        x_in = count("x_in", 16)
        ct_in = count("ct_in", 64)
        ct_copied = count("ct_copied", 64)
        x_out = count("x_out", 16)
        tr_ready = [count(f"tr_ready{n}") for n in range(6)]
        xt_ready = [count(f"xt_ready{n}") for n in range(6)]
        xs_ready = [count(f"xs_ready{n}") for n in range(7)]

        def both(name, per):
            return [count(f"{name}{i}", per) for i in range(2)]

        sa_proj = both("sa_proj", 4)
        sa_tok = [count("sa_tok0"), count("sa_tok1", 4)]
        sa_qk = both("sa_qk", 4)
        sa_hi = both("sa_hi", 1)
        sa_ks = both("sa_ks", 1)
        sa_qm = both("sa_qm", 2)
        sa_v = [count("sa_v0"), count("sa_v1", 4)]
        sa_x = both("sa_x", 12)
        sa_xd = both("sa_xd", 12)
        sa_nm = both("sa_nm", 1)
        sa_nt = both("sa_nt", 1)
        sa_ntc = both("sa_ntc", 1)
        sa_s = both("sa_s", 12)
        sa_e = both("sa_e", 12)
        sa_u = both("sa_u", 1)
        sa_ot = both("sa_ot", 1)
        sa_y = both("sa_y", 1)
        sa_r = both("sa_r", 1)
        sa_ne = count("sa_ne")
        sa_nx = count("sa_nx")
        sa_w = count("sa_w")
        c_hi = count("c_hi")
        c_ext = count("c_ext")
        c_lo = count("c_lo")

        def heads_(name, per):
            return [count(f"{name}0", per), count(f"{name}1", per * XH)]

        xa_q = heads_("xa_q", 1)
        xa_qh = heads_("xa_qh", 1)
        xa_ql = heads_("xa_ql", 1)
        xa_x = heads_("xa_x", 8)
        xa_xd = heads_("xa_xd", 8)
        xa_nm = heads_("xa_nm", 1)
        xa_mr = heads_("xa_mr", 1)
        xa_mc = heads_("xa_mc", 1)
        xa_s = heads_("xa_s", NPAIR)
        xa_e = heads_("xa_e", NPAIR)
        xa_pv = heads_("xa_pv", 1)
        xa_o = heads_("xa_o", 1)
        xa_f = heads_("xa_f", 1)
        xa_a = heads_("xa_a", 1)
        me_l = count("me_l")
        me_t = count("me_t")
        me_c = count("me_c")
        me_ct = count("me_ct")
        me_c3 = count("me_c3")
        me_gu = count("me_gu", EC + 1)
        me_tn = count("me_tn", EC + 1)
        me_cb = count("me_cb", EC)
        me_h = count("me_h", EC + 1)
        me_d = count("me_d")
        me_yt = count("me_yt")
        me_y = count("me_y")
        qdone = [count("qdone", 4), sa_qk[1]]
        ff_l = count("ff_l")
        ff_d = count("ff_d")
        ff_e = count("ff_e")
        ff_r = count("ff_r")

        SETUP = 8
        SA_SCALE = HD ** -0.5
        block = ctx.enter_context(nc.Block())

        def run(eng, sublayer, begin=lambda part, i=None: None):
            def part(n, b):
                return counted(sublayer(n, b), PIECES[n])

            def front_chain(b, last):
                if b is None:
                    return part(5, last)
                return chain(part(0, b), part(1, b), *([part(5, last)] if last is not None else []), part(2, b), part(3, b))

            def rest(b):
                return chain(part(7, b), part(6, b))

            def weights(*parts):
                return [WEIGHT[n] for n in parts for _ in range(PIECES[n])]

            begin(0)
            weave(front_chain(0, None), iter(()), weights(0, 1, 2, 3), 0)
            begin(1)
            weave(front_chain(1, None), part(4, 0), weights(0, 1, 2, 3), PIECES[4])
            with eng.Fori(2, NB) as i:
                begin(2, i)
                weave(front_chain(i, i - 2), chain(rest(i - 2), part(4, i - 1)), weights(0, 1, 5, 2, 3),
                      PIECES[7] + PIECES[6] + PIECES[4])
            begin(3)
            weave(rest(NB - 2), iter(()), weights(7, 6), 0)
            weave(front_chain(None, NB - 2), part(4, NB - 1), weights(5), PIECES[4])
            begin(4)
            weave(chain(rest(NB - 1), part(5, NB - 1)), iter(()), weights(7, 6, 5), 0)

        NORM = 6
        WEIGHT = [4, 3, 5, 4, 0, 3, 3, 1]
        CUT = 11
        QUOTIENTS = 2
        ROUTING = 5
        PIECES = [19 + QUOTIENTS + NORM, 17 + NORM, EC + 4 + ROUTING + NORM, 20 + QUOTIENTS + NORM, 1 + XH // 2 + 4 + 2 + CUT * NPAIR, 2 + NORM, NORM,
                  (XH - CUT) * NPAIR + 2]

        @block.sync
        def _(sp):
            for t, src in loads:
                sp.dma_start(t, src).then_inc(loaded, 16)
            sp.sem_inc(x_out.sem, 16)

            def at_(b):
                return bass.ds(b, 1)

            def load_x(b):
                sp.dma_start(xin[:], d["x"][at_(b)].rearrange("a (t p) n -> p (a t) n", p=P)).then_inc(x_in.sem, 16)

            def load_context(b):
                sp.dma_start(ct32[0:DC, :], d["ctxT"][at_(b)].rearrange("a c k -> (a c) k")).then_inc(ct_in.sem, 16)
                sp.dma_start(mrow_u8[DC + 2:DC + 3, :], d["mask"][at_(b), :]).then_inc(ct_in.sem, 16)
                sp.dma_start(cf.tok[:, 0:NK - 1, 0:DC],
                             d["ctx"][at_(b), 0:(NK - 1) * P, :].rearrange("a (t p) c -> p (a t) c", p=P)).then_inc(ct_in.sem, 16)
                sp.dma_start(cf.tok[0:LASTK, NK - 1, 0:DC],
                             d["ctx"][at_(b), (NK - 1) * P:CTX, :].rearrange("a k c -> (a k) c")).then_inc(ct_in.sem, 16)

            def hand_over(b):
                sp.wait_ge(c_lo.sem, c_lo.at(b, 1))
                sp.wait_ge(c_ext.sem, c_ext.at(b, 1))
                sp.wait_ge(xs_ready[2].sem, xs_ready[2].at(b, 1))
                sp.dma_start(cx.h[:], cf.h[:]).then_inc(ct_copied.sem, 16)
                sp.dma_start(cx.l[:], cf.l[:]).then_inc(ct_copied.sem, 16)
                sp.dma_start(cx.tok[:, 0:NK - 1, :], cf.tok[:, 0:NK - 1, :]).then_inc(ct_copied.sem, 16)
                sp.dma_start(cx.tok[0:LASTK, NK - 1, :], cf.tok[0:LASTK, NK - 1, :]).then_inc(ct_copied.sem, 16)
                sp.wait_ge(ct_copied.sem, ct_copied.at(b, 64))

            def store(b):
                sp.wait_ge(xs_ready[6].sem, xs_ready[6].at(b, 1))
                sp.dma_start(out[at_(b)].rearrange("a (t p) n -> p (a t) n", p=P), ys[:]).then_inc(x_out.sem, 16)

            def next_x(b):
                sp.wait_ge(xs_ready[1].sem, xs_ready[1].at(b, 1))
                load_x(b + 1)

            load_x(0)
            load_context(0)
            next_x(0)
            hand_over(0)
            load_context(1)
            next_x(1)
            with sp.Fori(2, NB - 1) as i:
                sp.wait_ge(xa_a[1].sem, xa_a[1].at(i - 2, XH))
                hand_over(i - 1)
                load_context(i)
                next_x(i)
                store(i - 2)
            sp.wait_ge(xa_a[1].sem, xa_a[1].at(NB - 3, XH))
            hand_over(NB - 2)
            load_context(NB - 1)
            store(NB - 3)
            sp.wait_ge(xa_a[1].sem, xa_a[1].at(NB - 2, XH))
            hand_over(NB - 1)
            store(NB - 2)
            store(NB - 1)
            sp.wait_ge(x_out.sem, 16 * NB + 16)

        @block.tensor
        def _(pe):
            mm = nc.tensor.matmul
            pe.wait_ge(loaded, 16 * NLOAD)
            pe.wait_ge(made, SETUP)
            for h in range(1 + XH):
                wq, wk = (x0wq[:, :], x0k_e[:, :]) if h == 0 else (x1wq[:, h - 1, :], xk_e[:, h - 1, :])
                bq = x0b[:, 0:1] if h == 0 else x1b[:, 0, h - 1:h]
                if h >= 2:
                    pe.wait_ge(unfolded, 2 * (h - 1))
                mm(bank(h % 2, P, 0, KE), wq, wk, start=True, stop=True)
                mm(bank(h % 2, KE, 256, 1), wk, bq, start=False, stop=True, skip_group_check=True).then_inc(folded, 1)
            for h in range(XH):
                if h >= 2:
                    pe.wait_ge(unfolded, 2 * (1 + XH) + h - 1)
                mm(bank(2 + h % 2, DC + 1, 0, D), x1v_e[:, h, :], x1wo[:, h, :], start=True, stop=True).then_inc(folded, 1)
            for e in range(2):
                mm(bank(4 + e, P, 0, D), f_we[:, e, :], f_wo[:, :], start=True, stop=True).then_inc(folded, 1)
            pe.wait_ge(unfolded, 2 * (1 + XH) + XH + 3)

            def transposes(b, n):
                if n == 0:
                    pe.wait_ge(x_in.sem, x_in.at(b, 16))
                else:
                    pe.wait_ge(xs_ready[n].sem, xs_ready[n].at(b, 1))
                for t in range(QT):
                    m = nc.tensor.transpose(bank(4 if n == 4 else 5, P, t * P, P), source[n][:, t, :], ident)
                m.then_inc(tr_ready[n].sem, 1)

            def self_attention(b, i):
                w = w0qk if i == 0 else w1qk
                xt = front.xt
                x = xt[:, 1:1 + SEQ]
                transposes(b, 3 * i)
                yield
                if i == 0 and not (isinstance(b, int) and b == 0):
                    pe.wait_ge(sa_r[1].sem, sa_r[1].at(b - 1, 1))
                pe.wait_ge(xt_ready[3 * i].sem, xt_ready[3 * i].at(b, 1))
                for j in range(4):
                    if j >= 2:
                        pe.wait_ge(qdone[i].sem, qdone[i].at(b, j - 1))
                    if i == 0:
                        mm(bank(6 + j % 2, P, 0, SEQ), w[:, 2 * j, :], x, start=True, stop=True)
                        m = mm(bank(6 + j % 2, P, SEQ, SEQ), w[:, 2 * j + 1, :], x, start=False, stop=True, skip_group_check=True)
                    else:
                        m = mm(bank(6 + j % 2, P, 0, SEQ), w[:, j, :], x, start=True, stop=True)
                    m.then_inc(sa_proj[i].sem, 1)
                    if j == 1:
                        if i == 0:
                            for t in range(QT):
                                m = mm(bank(5, P, t * P, P), xt[:, 1 + t * P:1 + (t + 1) * P], w0v, start=(t == 0), stop=True, skip_group_check=True)
                            m.then_inc(sa_tok[i].sem, 1)
                        else:
                            mm(bank(5, P, 0, 3 * D), xt[:, 1:1 + P], w1tok, start=True, stop=True).then_inc(sa_tok[i].sem, 1)
                        yield
                if i == 1:
                    pe.wait_ge(sa_v[i].sem, sa_v[i].at(b, 1))
                    mm(bank(5, P, 0, 2 * D), xt[:, 0:P], w1tok[:, D:], start=True, stop=True).then_inc(sa_tok[i].sem, 1)
                    yield
                    pe.wait_ge(qdone[i].sem, qdone[i].at(b, 4))
                    mm(bank(6, P, 0, 3 * D), xt[:, 1 + P:1 + 2 * P], w1tok, start=True, stop=True).then_inc(sa_tok[i].sem, 1)
                    mm(bank(7, P, 0, 2 * D), xt[:, P:2 * P], w1tok[:, D:], start=True, stop=True).then_inc(sa_tok[i].sem, 1)
                yield
                for _ in range(3):
                    yield
                pe.wait_ge(sa_ks[i].sem, sa_ks[i].at(b, 1))
                pe.wait_ge(sa_qm[i].sem, sa_qm[i].at(b, 1))
                pe.wait_ge(sa_v[i].sem, sa_v[i].at(b, 1 if i == 0 else 4))
                g = 0
                trq = trib[:, 2 * i + 1, :]
                for t in range(QT):
                    n = (t + 1) * P
                    per = 512 // n
                    for h0 in range(0, NH, per):
                        if g >= 3:
                            pe.wait_ge(sa_xd[i].sem, sa_xd[i].at(b, g - 2))
                        o = ps[:, 5 + g % 3, :].rearrange("p (h n) -> p h n", n=n)
                        for k in range(per):
                            mm(o[:, k, t * P:n], identb[:], trq, start=(k == 0), stop=False, skip_group_check=True)
                            if i == 1 and t == 1:
                                mm(o[:, k, P - 1:P], cornerb[0:1, P:2 * P], cornerb[0:1, 2 * P:], start=False, stop=False, skip_group_check=True)
                        for k in range(per):
                            h = h0 + k
                            m = mm(o[:, k, :], qm_h[:, h, t * P:(t + 1) * P], qk_h[:, 2 + h // HALF, 0:n],
                                   start=False, stop=True, skip_group_check=True)
                        m.then_inc(sa_x[i].sem, 1)
                        g += 1
                        if g % 3 == 0:
                            yield
                yield
                pe.wait_ge(sa_nm[i].sem, sa_nm[i].at(b, 1))
                psb = ps[0:NH, 5, :].bitcast(BF16)
                for t in range(QT):
                    m = nc.tensor.transpose(psb[:, t * P:(t + 1) * P], nmb[:, t, :], identb[:])
                m.then_inc(sa_nt[i].sem, 1)
                yield
                pe.wait_ge(sa_ntc[i].sem, sa_ntc[i].at(b, 1))
                pe.wait_ge(sa_qm[i].sem, sa_qm[i].at(b, 2))
                trk = trib[:, 2 * i, :]

                def scores(g):
                    if g >= 2:
                        pe.wait_ge(sa_e[i].sem, sa_e[i].at(b, g - 1))
                    kt, per, h0 = (0, 2, 2 * g) if g < 8 else (1, 4, 4 * (g - 8))
                    n = SEQ if kt == 0 else P
                    o = ps[:, 6 + g % 2, :].rearrange("p (h n) -> p h n", n=n)
                    for k in range(per):
                        h = h0 + k
                        keys = qk_h[:, 2 + h // HALF, kt * P:(kt + 1) * P]
                        mm(o[:, k, :], keys, qm_h[:, h, SEQ - n:], start=(k == 0), stop=False, skip_group_check=True)
                        if i == 1 and kt == 0:
                            mm(o[:, k, P:P + 1], cornerb[0:1, 0:P], cornerb[0:1, 2 * P:], start=False, stop=False, skip_group_check=True)
                        mm(o[:, k, 0:P], identb[:], trk, start=False, stop=False, skip_group_check=True)
                        mm(o[:, k, :], onehotb[:, h, :], nmt[:, SEQ - n:], start=False, stop=False, skip_group_check=True)
                        m = mm(o[:, k, :], keys, qm_l[:, h, SEQ - n:], start=False, stop=True, skip_group_check=True)
                    m.then_inc(sa_s[i].sem, 1)

                def values(g):
                    pe.wait_ge(sa_e[i].sem, sa_e[i].at(b, g + 1))
                    kt, per, h0 = (0, 2, 2 * g) if g < 8 else (1, 4, 4 * (g - 8))
                    n = SEQ if kt == 0 else P
                    for k in range(per):
                        h = h0 + k
                        o = bank(5, P, (h // HALF) * SEQ + SEQ - n, n)
                        m = mm(o, value_of(kt, h), pr[:, g % 4, k * n:(k + 1) * n], start=(g == 0 and k == 0),
                               stop=(kt == 1 or h % HALF == HALF - 1), skip_group_check=True)
                    return m

                for g in range(0, 12, 2):
                    scores(g)
                    scores(g + 1)
                    if g:
                        values(g - 2)
                        values(g - 1)
                    yield
                values(10)
                m = values(11)
                if i == 1:
                    pe.wait_ge(sa_w.sem, sa_w.at(b, 1))
                    for f in range(2):
                        for t in range(QT):
                            m = mm(bank(5, P, f * SEQ + t * P, P), wnear[:, t, f, :, :].rearrange("p a n -> p (a n)"),
                                   ident, start=False, stop=True, skip_group_check=True)
                m.then_inc(sa_u[i].sem, 1)
                for _ in range(1 + QUOTIENTS):
                    yield
                pe.wait_ge(sa_ot[i].sem, sa_ot[i].at(b, 1))
                for t in range(QT):
                    m = mm(bank(6, P, t * P, P), ot[:, t * P:(t + 1) * P], w0o if i == 0 else w1o,
                           start=(t == 0), stop=True, skip_group_check=True)
                m.then_inc(sa_y[i].sem, 1)
                for _ in range(NORM):
                    yield

            def cross_attention(b, i, h_from, h_to):
                n_heads, side, c, qh, ql = (1, front, cf, x0q_h, x0q_l) if i == 0 else (XH, cross, cx, xq_h, xq_l)
                b_row, b_s, b_o, b_y = (5, 6, 5, 6) if i == 0 else (0, 1, 3, 0)
                u_a = 0 if i == 0 else 1
                def max_pass(h, q, bk):
                    t, (k0, n) = q // 4, CHUNKS[q % 4]
                    mm(bank(bk, P, 0, n), qh[:, h, t * P:(t + 1) * P], c.h[:, k0:k0 + n], start=True, stop=True).then_inc(xa_x[i].sem, 1)

                def next_chunk(h, q):
                    if q == 1:
                        if h > 0:
                            pe.wait_ge(xa_mc[i].sem, xa_mc[i].at(b, h))
                    elif h > 0 or q > 0:
                        pe.wait_ge(xa_xd[i].sem, xa_xd[i].at(b, 8 * h + (q - 1 if 1 < q < 7 else q)))
                    max_pass(h, q, CHUNK_BANK[q])

                def max_row(h):
                    pe.wait_ge(xa_nm[i].sem, xa_nm[i].at(b, h + 1))
                    if h > 1:
                        pe.wait_ge(xa_a[i].sem, xa_a[i].at(b, h - 1))
                    for t in range(QT):
                        m = mm(bank(b_row, 1, t * P, P), side.xneg[:, t:t + 1], ident16[:], start=(t == 0), stop=True, skip_group_check=True)
                    m.then_inc(xa_mr[i].sem, 1)

                def scores(h, p):
                    n = NPAIR * h + p
                    if n >= 2:
                        pe.wait_ge(xa_e[i].sem, xa_e[i].at(b, n - 1))
                    for j, (kt, k_) in enumerate(pair_tiles(p)):
                        o = bank(b_s + n % 2, k_, j * SEQ, SEQ)
                        ks = slice(kt * P, kt * P + k_)
                        mm(o, c.h[:, ks], qh[:, h, :], start=(j == 0), stop=False, skip_group_check=True)
                        mm(o, c.h[:, ks], ql[:, h, :], start=False, stop=False, skip_group_check=True)
                        m = mm(o, c.l[:, ks], qh[0:DC, h, :], start=False, stop=True, skip_group_check=True)
                    m.then_inc(xa_s[i].sem, 1)

                def values(h, p):
                    n = NPAIR * h + p
                    pe.wait_ge(xa_e[i].sem, xa_e[i].at(b, n + 1))
                    if p == 0 and h > 0:
                        pe.wait_ge(xa_o[i].sem, xa_o[i].at(b, h))
                    for j, (kt, k_) in enumerate(pair_tiles(p)):
                        m = mm(bank(b_o, DC + 1, 0, SEQ), c.tok[0:k_, kt, :], xp_slot(i, n)[0:k_, j * SEQ:(j + 1) * SEQ],
                               start=(kt == 0), stop=(kt == NK - 1), skip_group_check=True)
                    if p == NPAIR - 1:
                        m.then_inc(xa_pv[i].sem, 1)

                def output(h):
                    pe.wait_ge(xa_o[i].sem, xa_o[i].at(b, h + 1))
                    if h == n_heads - 1 and h > 0:
                        pe.wait_ge(xa_a[i].sem, xa_a[i].at(b, h))
                    elif i == 1 and h + 2 < n_heads:
                        pe.wait_ge(xa_xd[i].sem, xa_xd[i].at(b, 8 * (h + 2) + 6))
                    for t in range(QT):
                        m = mm(ps[:, b_y, t * 256:t * 256 + D + 1], side.xo[:, t * P:(t + 1) * P], g_mat[:, u_a + h, :],
                               start=(t == 0), stop=True, skip_group_check=True)
                    m.then_inc(xa_f[i].sem, 1)

                def start():
                    transposes(b, 1 + 3 * i)
                    yield
                    x = side.xt[:, 1:1 + SEQ]
                    pe.wait_ge(xt_ready[1 + 3 * i].sem, xt_ready[1 + 3 * i].at(b, 1))
                    if i == 1 and not (isinstance(b, int) and b == 0):
                        pe.wait_ge(xa_a[1].sem, xa_a[1].at(b - 1, XH))
                    for h in range(n_heads):
                        if h >= 5:
                            pe.wait_ge(xa_ql[i].sem, xa_ql[i].at(b, h - 4))
                        mm(bank(6 if i == 0 else h % 5, KE, 0, SEQ), a_mat[:, u_a + h, :], x, start=True, stop=True).then_inc(xa_q[i].sem, 1)
                        if h % 2 == 1 or n_heads == 1:
                            yield

                    if i == 0:
                        pe.wait_ge(c_ext.sem, c_ext.at(b, 1))
                        pe.wait_ge(c_hi.sem, c_hi.at(b, 1))
                    else:
                        pe.wait_ge(ct_copied.sem, ct_copied.at(b, 64))
                    pe.wait_ge(xa_ql[i].sem, xa_ql[i].at(b, n_heads))
                    for q in range(8):
                        if i == 1:
                            next_chunk(0, q)
                        else:
                            if q >= 3:
                                pe.wait_ge(xa_xd[0].sem, xa_xd[0].at(b, q - 2))
                            max_pass(0, q, 5 + q % 3)
                        if q % 2:
                            yield
                    yield
                    max_row(0)
                    if i == 1:
                        for q in range(AHEAD):
                            next_chunk(1, q)
                    yield
                    if i == 0:
                        pe.wait_ge(c_lo.sem, c_lo.at(b, 1))
                        pe.wait_ge(ct_in.sem, ct_in.at(b, 64))

                if h_from == 0:
                    yield from start()
                for h in range(h_from, h_to):
                    for p in range(NPAIR):
                        n = NPAIR * h + p
                        chunks = next_chunks(h, p) if i == 1 else []
                        if i == 1 and p == 5 and h + 1 < n_heads:
                            max_row(h + 1)
                        elif chunks:
                            next_chunk(*chunks.pop(0))
                        if p == 0:
                            pe.wait_ge(xa_mc[i].sem, xa_mc[i].at(b, h + 1))
                        scores(h, p)
                        for hc, q in chunks:
                            next_chunk(hc, q)
                        if n:
                            values(*divmod(n - 1, NPAIR))
                        if p == 2 and h > 0:
                            output(h - 1)
                        yield
                if h_to == n_heads:
                    values(n_heads - 1, NPAIR - 1)
                    yield
                    output(n_heads - 1)
                    yield
                    if i == 0:
                        for _ in range(NORM):
                            yield

            def experts(b):
                if not (isinstance(b, int) and b < 2):
                    pe.wait_ge(ff_r.sem, ff_r.at(b - 2, 1))
                transposes(b, 2)
                yield
                pe.wait_ge(xt_ready[2].sem, xt_ready[2].at(b, 1))
                x = front.xt[:, 1:1 + SEQ]
                for t in range(QT):
                    m = mm(bank(7, P, t * NE, NE), front.xt[:, 1 + t * P:1 + (t + 1) * P], gw, start=(t == 0), stop=True, skip_group_check=True)
                m.then_inc(me_l.sem, 1)

                def up(c):
                    if c >= 1:
                        pe.wait_ge(me_h.sem, me_h.at(b, c))
                    mm(bank(6, P, 0, SEQ), wg[:, c, :], x, start=True, stop=True)
                    mm(bank(6, P, SEQ, SEQ), wu[:, c, :], x, start=False, stop=True, skip_group_check=True).then_inc(me_gu.sem, 1)

                def weights(c):
                    mm(bank(7, P, 0, SEQ), sel3b[:, c - 1, :], comb3[:], start=True, stop=True).then_inc(me_cb.sem, 1)

                def down(c):
                    pe.wait_ge(me_h.sem, me_h.at(b, c + 1))
                    m = mm(bank(5, P, 0, SEQ), wd[:, c, :], h2[:, c % 2, :], start=(c == 0), stop=(c == EC), skip_group_check=True)
                    if c == EC:
                        m.then_inc(me_d.sem, 1)

                yield
                up(0)
                for _ in range(ROUTING):
                    yield
                pe.wait_ge(me_c.sem, me_c.at(b, 1))
                for t in range(QT):
                    m = nc.tensor.transpose(bank(7, NE, t * P, P), comb[:, t, :], ident)
                m.then_inc(me_ct.sem, 1)
                yield
                pe.wait_ge(me_c3.sem, me_c3.at(b, 1))
                for c in range(1, EC + 1):
                    up(c)
                    weights(c)
                    down(c - 1)
                    yield
                down(EC)
                yield
                pe.wait_ge(me_yt.sem, me_yt.at(b, 1))
                for t in range(QT):
                    m = nc.tensor.transpose(bank(6, P, t * P, P), yt[:, t * P:(t + 1) * P], ident)
                m.then_inc(me_y.sem, 1)
                for _ in range(NORM):
                    yield

            def last_ffn(b):
                transposes(b, 5)
                yield
                if not isinstance(b, int):
                    pe.wait_ge(xa_a[0].sem, xa_a[0].at(b + 2, 1))
                elif b == NB - 2:
                    pe.wait_ge(sa_r[1].sem, sa_r[1].at(NB - 1, 1))
                else:
                    pe.wait_ge(ff_r.sem, ff_r.at(NB - 2, 1))
                pe.wait_ge(xt_ready[5].sem, xt_ready[5].at(b, 1))
                for t in range(QT):
                    xx = front.xt[:, 1 + t * P:1 + (t + 1) * P]
                    mm(bank(6, P, t * E2, E2), xx, f_gate, start=(t == 0), stop=True, skip_group_check=True)
                    m = mm(bank(7, P, t * 2 * D, 2 * D), xx, f_m[:], start=(t == 0), stop=True, skip_group_check=True)
                m.then_inc(ff_l.sem, 1)
                yield
                for _ in range(NORM):
                    yield

            def left_over(b):
                for _ in range(NORM):
                    yield

            run(pe, lambda n, b: [lambda: self_attention(b, 0), lambda: cross_attention(b, 0, 0, 1), lambda: experts(b),
                                  lambda: self_attention(b, 1), lambda: cross_attention(b, 1, 0, CUT), lambda: last_ffn(b),
                                  lambda: left_over(b), lambda: cross_attention(b, 1, CUT, XH)][n]())

        @block.scalar
        def _(act):
            fn = nc.scalar.activation

            def stream(b, n):
                act.wait_ge(tr_ready[n].sem, tr_ready[n].at(b, 1))
                side, bk = (cross, 4) if n == 4 else (front, 5)
                nc.scalar.copy(side.xt[:, 1:1 + SEQ], bank(bk, P, 0, SEQ)).then_inc(xt_ready[n].sem, 1)

            def self_attention(b, i):
                stream(b, 3 * i)
                yield
                for j in range(4):
                    if i == 1:
                        act.wait_ge(sa_proj[1].sem, sa_proj[1].at(b, j + 1))
                        bias = w1bqk[:, j:j + 1] if j < 2 else k1b[:, j - 2:j - 1]
                        fn(qk[:, j, :], bank(6 + j % 2, P, 0, SEQ), ACT.Identity, bias=bias).then_inc(sa_qk[1].sem, 1)
                    elif j == 1:
                        act.wait_ge(sa_tok[0].sem, sa_tok[0].at(b, 1))
                        for t in range(QT):
                            for f in range(2):
                                m = nc.scalar.copy(value_slots(t, f, 0), bank(5, P, t * P + f * HALF * HD, HALF * HD).rearrange("p (h c) -> p h c", c=HD))
                        m.then_inc(sa_v[0].sem, 1)
                    if j == 1:
                        yield
                if i == 1:
                    yield
                yield
                act.wait_ge(sa_qk[i].sem, sa_qk[i].at(b, 4))
                nc.scalar.copy(qk_h[:], qk[:]).then_inc(sa_hi[i].sem, 1)
                for _ in range(3):
                    yield
                for _ in range(5):
                    yield
                act.wait_ge(sa_nt[i].sem, sa_nt[i].at(b, 1))
                nc.scalar.copy(nmt[:], ps[0:NH, 5, :].bitcast(BF16)[:, 0:SEQ]).then_inc(sa_ntc[i].sem, 1)
                if i == 1:
                    act.wait_ge(sa_ne.sem, sa_ne.at(b, 1))
                    fn(near[:], near[:], ACT.Exp, scale=SA_SCALE).then_inc(sa_nx.sem, 1)
                yield
                for g in range(12):
                    act.wait_ge(sa_s[i].sem, sa_s[i].at(b, g + 1))
                    fn(pr[:, g % 4, :], bank(6 + g % 2), ACT.Exp, scale=SA_SCALE).then_inc(sa_e[i].sem, 1)
                    if g % 2:
                        yield
                for _ in range(1 + QUOTIENTS + NORM):
                    yield

            def cross_attention(b, i, h_from, h_to):
                n_heads, side, qh = (1, front, x0q_h) if i == 0 else (XH, cross, xq_h)
                b_row, b_s, b_o = (5, 6, 5) if i == 0 else (0, 1, 3)
                u_a = 0 if i == 0 else 1
                scale = 1.0 if i == 0 else XD ** -0.5
                def row(h):
                    act.wait_ge(xa_mr[i].sem, xa_mr[i].at(b, h + 1))
                    nc.scalar.copy(qh[SHIFT:SHIFT + 1, h, :], bank(b_row, 1, 0, SEQ)).then_inc(xa_mc[i].sem, 1)

                def exps(h, p):
                    n = NPAIR * h + p
                    act.wait_ge(xa_s[i].sem, xa_s[i].at(b, n + 1))
                    w, k_ = (2 * SEQ, P) if p < NPAIR - 1 else (SEQ, LASTK)
                    fn(xp_slot(i, n)[0:k_, 0:w], bank(b_s + n % 2, k_, 0, w), ACT.Exp, scale=scale).then_inc(xa_e[i].sem, 1)

                def sums(h):
                    act.wait_ge(xa_pv[i].sem, xa_pv[i].at(b, h + 1))
                    if h > 0:
                        act.wait_ge(xa_f[i].sem, xa_f[i].at(b, h))
                    nc.scalar.copy(side.xo[:], bank(b_o, DC + 1, 0, SEQ)).then_inc(xa_o[i].sem, 1)

                if h_from == 0:
                    stream(b, 1 + 3 * i)
                    yield
                    for h in range(n_heads):
                        act.wait_ge(xa_q[i].sem, xa_q[i].at(b, h + 1))
                        fn(qh[:, h, :], bank(6 if i == 0 else h % 5, KE, 0, SEQ), ACT.Identity, bias=a_c[:, u_a + h:u_a + h + 1]).then_inc(xa_qh[i].sem, 1)
                        if h % 2 == 1 or n_heads == 1:
                            yield

                    if i == 0:
                        act.wait_ge(ct_in.sem, ct_in.at(b, 64))
                        nc.scalar.copy(cf.h[0:DC, :], ct32[0:DC, :]).then_inc(c_hi.sem, 1)
                    for _ in range(4):
                        yield
                    yield
                    row(0)
                    yield
                for h in range(h_from, h_to):
                    for p in range(NPAIR):
                        if i == 1 and p == 5 and h + 1 < n_heads:
                            row(h + 1)
                        exps(h, p)
                        if p == 0 and h > 0:
                            sums(h - 1)
                        yield
                if h_to == n_heads:
                    sums(n_heads - 1)
                    yield
                    yield
                    if i == 0:
                        for _ in range(NORM):
                            yield

            def experts(b):
                stream(b, 2)
                yield
                act.wait_ge(me_l.sem, me_l.at(b, 1))
                fn(sg[:].rearrange("p t n -> p (t n)"), bank(7, P, 0, QT * NE), ACT.Tanh, scale=0.5).then_inc(me_t.sem, 1)
                for _ in range(1 + ROUTING):
                    yield
                for c in range(EC + 1):
                    act.wait_ge(me_gu.sem, me_gu.at(b, c + 1))
                    fn(tnh[:], bank(6, P, 0, SEQ), ACT.Tanh, scale=0.5).then_inc(me_tn.sem, 1)
                    yield
                act.wait_ge(me_d.sem, me_d.at(b, 1))
                nc.scalar.copy(yt[:], bank(5, P, 0, SEQ)).then_inc(me_yt.sem, 1)
                yield
                for _ in range(NORM):
                    yield

            def last_ffn(b):
                stream(b, 5)
                yield
                act.wait_ge(ff_d.sem, ff_d.at(b, 1))
                fn(fp[:], fp[:], ACT.Exp).then_inc(ff_e.sem, 1)
                yield
                for _ in range(NORM):
                    yield

            def left_over(b):
                for _ in range(NORM):
                    yield

            run(act, lambda n, b: [lambda: self_attention(b, 0), lambda: cross_attention(b, 0, 0, 1), lambda: experts(b),
                                   lambda: self_attention(b, 1), lambda: cross_attention(b, 1, 0, CUT), lambda: last_ffn(b),
                                  lambda: left_over(b), lambda: cross_attention(b, 1, CUT, XH)][n]())

        @block.gpsimd
        def _(pool):
            with pool.Fori(0, NB) as b:
                pool.wait_ge(made, SETUP)
                pool.wait_ge(ct_in.sem, ct_in.at(b, 64))
                nc.gpsimd.tensor_tensor(pool_carrier[:], xcol[0:P // 4, 0:1], xcol[0:P // 4, 1:2], ALU.add)
                nc.gpsimd.tensor_scalar(cf.h[DC:KE, :], mrow_u8[DC:KE, :], xcol[DC:KE, 0:1], xcol[DC:KE, 1:2],
                                        ALU.mult, ALU.add).then_inc(c_ext.sem, 1)
                pool.wait_ge(c_hi.sem, c_hi.at(b, 1))
                nc.gpsimd.tensor_tensor(cf.l[:], ct32[0:DC, :], cf.h[0:DC, :], ALU.subtract).then_inc(c_lo.sem, 1)

        @block.vector
        def _(dve):
            v = nc.vector
            tt, ts, stt, red = v.tensor_tensor, v.tensor_scalar, v.scalar_tensor_tensor, v.tensor_reduce
            v.memset(xk_e, 0.0).then_inc(dve_self, 1)
            v.memset(x0k_e[:], 0.0).then_inc(dve_self, 1)
            v.memset(g_mat[:, :, D:D + 1], 0.0).then_inc(dve_self, 1)
            v.memset(mrow_u8[DC:DC + 2, :], 0.0).then_inc(dve_self, 1)
            v.memset(front.xt[:, 0:1], 0.0)
            v.memset(cf.tok[:, :, DC:DC + 1], 1.0)
            dve.wait_ge(dve_self, 4)
            v.memset(g_mat[DC:DC + 1, :, D:D + 1], 1.0)
            dve.wait_ge(loaded, 16 * NLOAD)
            for dst, src in ((ident16, ident), (identb, ident), (trib, tri), (onehotb, onehot), (cornerb, corner), (sel3b, sel3)):
                v.tensor_copy(dst[:], src)
            ts(k1b[:], w1bqk[:, 2:4], w1bqk[:, 4:5], None, ALU.add)
            v.tensor_copy(bias0[:, 0, :], b1tok[:, 0, :])
            tt(bias0[:, 1, :], b1tok[:, 1, :], r1k[:, 2, :], ALU.add)
            tt(bias0[:, 2, :], b1tok[:, 2, :], r1v[:, 2, :], ALU.add)
            tt(bias1[:, 0, :], b1tok[:, 1, :], r1k[:, 1, :], ALU.add)
            tt(bias1[:, 1, :], b1tok[:, 2, :], r1v[:, 1, :], ALU.add)
            tt(vfar[:], b1tok[:, 2, :], r1v[:, 0, :], ALU.add).then_inc(made, 1)
            v.tensor_copy(xk_e[:, :, 0:DC], x1wk[:]).then_inc(made, 1)
            v.tensor_copy(xk_e[:, :, DC + 1], x1b[:, 1, :]).then_inc(made, 1)
            v.tensor_copy(x0k_e[:, 0:DC], x0wk[:]).then_inc(made, 1)
            v.tensor_copy(x0k_e[:, DC + 1:DC + 2], x0b[:, 1:2]).then_inc(made, 1)
            v.tensor_copy(x1v_e[:, :, 0:DC], x1wv[:]).then_inc(made, 1)
            v.tensor_copy(x1v_e[:, :, DC], x1b[:, 2, :]).then_inc(made, 1)
            v.tensor_copy(g_mat[:, 0, 0:D], x0v[:]).then_inc(made, 1)
            for h in range(1 + XH):
                dve.wait_ge(folded, h + 1)
                v.tensor_copy(a_mat[:, h, :], bank(h % 2, P, 0, KE)).then_inc(unfolded, 1)
                xc = xcol[0:KE, 2:3] if h == 0 else xcol[0:KE, 3:4]
                tt(a_c[:, h:h + 1], bank(h % 2, KE, 256, 1), xc, ALU.add).then_inc(unfolded, 1)
            for h in range(XH):
                dve.wait_ge(folded, 1 + XH + h + 1)
                v.tensor_copy(g_mat[:, 1 + h, 0:D], bank(2 + h % 2, DC + 1, 0, D)).then_inc(unfolded, 1)
            for e in range(2):
                dve.wait_ge(folded, 1 + 2 * XH + e + 1)
                v.tensor_copy(f_m[:, e * D:(e + 1) * D], bank(4 + e, P, 0, D)).then_inc(unfolded, 1)
            v.memset(vm[:], 0.0).then_inc(dve_self, 1)
            dve.wait_ge(dve_self, 5)
            for t in range(QT):
                for f in range(2):
                    m = v.memset(value_slots(t, f, HALF * HD), 1.0)
            m.then_inc(unfolded, 1)

            base, taken, counts = [0], [0], []

            def begin(part, i=None):
                if part > 0:
                    counts.append(taken[0])
                taken[0] = 0
                if part < 3:
                    base[0] = sum(dve_steps[0:part]) + (0 if i is None else (i - 2) * dve_steps[2])
                else:
                    base[0] = sum(dve_steps[0:part]) + (NB - 3) * dve_steps[2]

            def step(ins):
                ins.then_inc(dve_step, 1)
                taken[0] += 1

            def settle():
                dve.wait_ge(dve_step, base[0] + taken[0])

            def pace():
                v.memset(carrier[:], 0.0)

            def over(ap, n):
                return ap.unsqueeze(ap.ndim).to_broadcast(list(ap.shape) + [n])

            def normalise(b, n, side):
                res, st6, mv, nr, nri, xs = side.res, side.st6, side.mv, side.nr, side.nri, source[n]
                for t in range(QT):
                    m = v.bn_stats(st6[:, t, :], res[:, t, :])
                step(m)
                settle()
                pace()
                for t in range(QT):
                    m = v.bn_aggr(mv[:, t, :], st6[:, t, :])
                step(m)
                settle()
                yield
                var, y, q = nr[:, 0, :], nri[:].bitcast(F32), nr[:, 1, :]
                step(ts(var, mv[:, :, 1], EPS, None, ALU.add))
                settle()
                step(ts(nri[:], nr[:, 0, :].bitcast(I32), 1, None, ALU.logical_shift_right))
                settle()
                step(ts(nri[:], nri[:], -1.0, float(0x5F3759DF), ALU.mult, ALU.add))
                settle()
                yield
                for _ in range(3):
                    step(tt(q, y, y, ALU.mult))
                    settle()
                    step(tt(q, q, var, ALU.mult))
                    settle()
                    step(ts(q, q, -0.5, 1.5, ALU.mult, ALU.add))
                    settle()
                    step(tt(y, y, q, ALU.mult))
                    settle()
                    yield
                if n == 6:
                    dve.wait_ge(x_out.sem, b * 16 + 16)
                for t in range(QT):
                    m = ts(xs[:, t, :], res[:, t, :], mv[:, t, 0:1], y[:, t:t + 1], ALU.subtract, ALU.mult)
                m.then_inc(xs_ready[n].sem, 1)
                yield

            def self_attention(b, i):
                res, xs = front.res, source[3 * i]
                yield
                if i == 0:
                    dve.wait_ge(x_in.sem, x_in.at(b, 16))
                    for j in range(4):
                        dve.wait_ge(sa_proj[0].sem, sa_proj[0].at(b, j + 1))
                        tt(qtmp[:, j, :], bank(6 + j % 2), rope.rearrange("p a n -> p (a n)"), ALU.mult).then_inc(qdone[0].sem, 1)
                        if j % 2:
                            dve.wait_ge(qdone[0].sem, qdone[0].at(b, j + 1))
                            for k in (j - 1, j):
                                tt(qk[:, k, :], qtmp[:, k, 0:SEQ], qtmp[:, k, SEQ:], ALU.add).then_inc(sa_qk[0].sem, 1)
                            yield
                else:
                    def token(t):
                        bk = 5 if t == 0 else 6
                        tt(tok[:, t, :, :].rearrange("p a n -> p (a n)"), bank(bk, P, 0, 3 * D), bias0[:].rearrange("p a n -> p (a n)"), ALU.add)
                        for f in range(2):
                            m = tt(value_slots(t, f, 0), bank(bk, P, 2 * D + f * HALF * HD, HALF * HD).rearrange("p (h c) -> p h c", c=HD),
                                   vfar[:, f * HALF * HD:(f + 1) * HALF * HD].rearrange("p (h c) -> p h c", c=HD), ALU.add)
                        m.then_inc(sa_v[1].sem, 1)

                    def shifted(t):
                        bk = 5 if t == 0 else 7
                        tt(tok1[:, t, :, :].rearrange("p a n -> p (a n)"), bank(bk, P, 0, 2 * D), bias1[:].rearrange("p a n -> p (a n)"), ALU.add).then_inc(sa_v[1].sem, 1)

                    dve.wait_ge(sa_tok[1].sem, sa_tok[1].at(b, 1))
                    token(0)
                    yield
                    dve.wait_ge(sa_tok[1].sem, sa_tok[1].at(b, 2))
                    shifted(0)
                    yield
                    dve.wait_ge(sa_tok[1].sem, sa_tok[1].at(b, 3))
                    token(1)
                    dve.wait_ge(sa_tok[1].sem, sa_tok[1].at(b, 4))
                    shifted(1)
                    yield
                yield
                dve.wait_ge(sa_hi[i].sem, sa_hi[i].at(b, 1))
                dve.wait_ge(sa_qk[i].sem, sa_qk[i].at(b, 4))
                hi = slice(P // 2, P)
                tt(qk_h[hi, 2:4, :], qk[hi, 2:4, :], qk_h[hi, 2:4, :], ALU.subtract).then_inc(sa_ks[i].sem, 1)
                step(tt(q_l[:], qk[:, 0:2, :], qk_h[:, 0:2, :], ALU.subtract))
                for h in range(NH):
                    if h == HALF:
                        yield
                    m = ts(qm_h[:, h, :], qk_h[:, h // HALF, :], hmask[:, h % HALF:h % HALF + 1], None, ALU.mult)
                m.then_inc(sa_qm[i].sem, 1)
                settle()
                yield
                g = 0
                for t in range(QT):
                    n = (t + 1) * P
                    per = 512 // n
                    for h0 in range(0, NH, per):
                        dve.wait_ge(sa_x[i].sem, sa_x[i].at(b, g + 1))
                        red(smax[:, t, h0:h0 + per], ps[:, 5 + g % 3, :].rearrange("p (h n) -> p h n", n=n), AX.X, ALU.max).then_inc(sa_xd[i].sem, 1)
                        g += 1
                        if g % 3 == 0:
                            for h in range(4 * (g // 3 - 1), 4 * (g // 3)):
                                m = ts(qm_l[:, h, :], q_l[:, h // HALF, :], hmask[:, h % HALF:h % HALF + 1], None, ALU.mult)
                            if g == 12:
                                m.then_inc(sa_qm[i].sem, 1)
                            yield
                dve.wait_ge(sa_xd[i].sem, sa_xd[i].at(b, 12))
                if i == 0:
                    ts(nmb[:], smax[:], -1.0, None, ALU.mult).then_inc(sa_nm[0].sem, 1)
                    yield
                    yield
                else:
                    dve.wait_ge(sa_v[1].sem, sa_v[1].at(b, 4))
                    tt(prod[:, :, 0, :], tok[:, :, 0, :], tok[:, :, 1, :], ALU.mult)
                    step(tt(prod[:, :, 1, :], tok[:, :, 0, :], tok1[:, :, 0, :], ALU.mult))
                    settle()
                    step(red(near[:], prod[:].rearrange("p t a (h c) -> p (t a h) c", c=HD), AX.X, ALU.add))
                    settle()
                    step(tt(near[:, :, 1, :], near[:, :, 1, :], first, ALU.add))
                    step(tt(smax[:], smax[:], near[:, :, 0, :], ALU.max))
                    settle()
                    step(tt(smax[:], smax[:], near[:, :, 1, :], ALU.max))
                    settle()
                    ts(nmb[:], smax[:], -1.0, None, ALU.mult).then_inc(sa_nm[1].sem, 1)
                    dve.wait_ge(sa_nm[1].sem, sa_nm[1].at(b, 1))
                    for j in range(2):
                        m = tt(near[:, :, j, :], near[:, :, j, :], nmb[:], ALU.add)
                    m.then_inc(sa_ne.sem, 1)
                    step(tt(res[:], xs[:], b1o.unsqueeze(1).to_broadcast([P, QT, D]), ALU.add))
                    yield
                    yield
                if i == 1:
                    dve.wait_ge(sa_nx.sem, sa_nx.at(b, 1))
                    for t in range(QT):
                        tt(prod[:, t, 0, :].rearrange("p (h c) -> p h c", c=HD), tok[:, t, 2, :].rearrange("p (h c) -> p h c", c=HD), over(near[:, t, 0, :], HD), ALU.mult)
                        m = tt(prod[:, t, 1, :].rearrange("p (h c) -> p h c", c=HD), tok1[:, t, 1, :].rearrange("p (h c) -> p h c", c=HD), over(near[:, t, 1, :], HD), ALU.mult)
                    step(m)
                    step(tt(esum[:], near[:, :, 0, :], near[:, :, 1, :], ALU.add))
                    settle()
                    for t in range(QT):
                        tt(wnear[:, t, :, 0, :], prod[:, t, 0, :].rearrange("p (f n) -> p f n", f=2), prod[:, t, 1, :].rearrange("p (f n) -> p f n", f=2), ALU.add)
                        for f in range(2):
                            m = v.tensor_copy(wnear[:, t, f, 1, :].rearrange("p (h c) -> p h c", c=HD), over(esum[:, t, f * HALF:(f + 1) * HALF], HD))
                    m.then_inc(sa_w.sem, 1)
                for _ in range(6):
                    yield
                dve.wait_ge(sa_u[i].sem, sa_u[i].at(b, 1))
                for f in range(2):
                    m = v.reciprocal(rden[64 * f:64 * f + 64, :], ps[64:128, 5, f * SEQ:(f + 1) * SEQ])
                    yield
                step(m)
                settle()
                for f in range(2):
                    m = tt(ot[64 * f:64 * f + 64, :], ps[0:64, 5, f * SEQ:(f + 1) * SEQ], rden[64 * f:64 * f + 64, :], ALU.mult)
                m.then_inc(sa_ot[i].sem, 1)
                yield
                dve.wait_ge(sa_y[i].sem, sa_y[i].at(b, 1))
                tt(res[:], tiles(bank(6, P, 0, SEQ)), xs[:] if i == 0 else res[:], ALU.add).then_inc(sa_r[i].sem, 1)
                dve.wait_ge(sa_r[i].sem, sa_r[i].at(b, 1))
                yield from normalise(b, 3 * i + 1, front)

            def cross_attention(b, i, h_from, h_to):
                n_heads, side, qh, ql = (1, front, x0q_h, x0q_l) if i == 0 else (XH, cross, xq_h, xq_l)
                b_row, b_s, b_o, b_y = (5, 6, 5, 6) if i == 0 else (0, 1, 3, 0)
                u_a = 0 if i == 0 else 1
                res, xs = side.res, source[1 + 3 * i]
                def chunk(h, q, bk):
                    t, c = q // 4, q % 4
                    dve.wait_ge(xa_x[i].sem, xa_x[i].at(b, 8 * h + q + 1))
                    red(side.xmax[:, t, c:c + 1], bank(bk, P, 0, CHUNKS[c][1]), AX.X, ALU.max).then_inc(xa_xd[i].sem, 1)

                def highest(h):
                    dve.wait_ge(xa_xd[i].sem, xa_xd[i].at(b, 8 * h + 8))
                    if h > 0:
                        dve.wait_ge(xa_mr[i].sem, xa_mr[i].at(b, h))
                    red(side.xneg[:], side.xmax[:], AX.X, ALU.max, negate=True).then_inc(xa_nm[i].sem, 1)

                def add(h):
                    dve.wait_ge(xa_f[i].sem, xa_f[i].at(b, h + 1))
                    step(v.reciprocal(side.xr[:], ps[:, b_y, :].rearrange("p (t n) -> p t n", n=256)[:, :, D]))
                    settle()
                    for t in range(QT):
                        m = stt(res[:, t, :], ps[:, b_y, t * 256:t * 256 + D], side.xr[:, t:t + 1],
                                xs[:, t, :] if i == 0 else res[:, t, :], ALU.mult, ALU.add)
                    m.then_inc(xa_a[i].sem, 1)

                if h_from == 0:
                    if i == 1:
                        dve.wait_ge(xs_ready[4].sem, xs_ready[4].at(b, 1))
                        if not (isinstance(b, int) and b == 0):
                            dve.wait_ge(xs_ready[5].sem, xs_ready[5].at(b - 1, 1))
                        step(tt(res[:], xs[:], x1bo.unsqueeze(1).to_broadcast([P, QT, D]), ALU.add))
                    yield
                    for h in range(n_heads):
                        dve.wait_ge(xa_qh[i].sem, xa_qh[i].at(b, h + 1))
                        stt(ql[:, h, :], bank(6 if i == 0 else h % 5, KE, 0, SEQ), a_c[:, u_a + h:u_a + h + 1], qh[:, h, :], ALU.add, ALU.subtract).then_inc(xa_ql[i].sem, 1)
                        if h % 2 == 1 or n_heads == 1:
                            yield

                    for q in range(8):
                        chunk(0, q, 5 + q % 3 if i == 0 else CHUNK_BANK[q])
                        if q % 2:
                            yield
                    highest(0)
                    yield
                    if i == 1:
                        dve.wait_ge(xa_nm[i].sem, xa_nm[i].at(b, 1))
                        for q in range(AHEAD):
                            chunk(1, q, CHUNK_BANK[q])
                    yield
                for h in range(h_from, h_to):
                    for p in range(NPAIR):
                        for hc, q in next_chunks(h, p) if i == 1 else ():
                            if q == 0:
                                dve.wait_ge(xa_nm[i].sem, xa_nm[i].at(b, hc))
                            chunk(hc, q, CHUNK_BANK[q])
                            if q == 7:
                                highest(hc)
                        if p == 2 and h > 0:
                            add(h - 1)
                        yield
                if h_to == n_heads:
                    yield
                    add(n_heads - 1)
                    yield
                    if i == 0:
                        dve.wait_ge(xa_a[0].sem, xa_a[0].at(b, 1))
                        yield from normalise(b, 2, side)

            def left_over(b):
                dve.wait_ge(xa_a[1].sem, xa_a[1].at(b, XH))
                yield from normalise(b, 5, cross)

            def experts(b):
                res, xs = front.res, source[2]
                yield
                dve.wait_ge(me_t.sem, me_t.at(b, 1))
                step(ts(sg[:], sg[:], 0.5, 0.5, ALU.mult, ALU.add))
                settle()
                step(tt(sc[:], sg[:], gb.unsqueeze(1).to_broadcast([P, QT, NE]), ALU.add))
                settle()
                pair = sc[:].rearrange("p t (g a c) -> p (t g) a c", a=2, c=2)
                tt(g2[:, 0, :, :], pair[:, :, :, 0], pair[:, :, :, 1], ALU.max)
                step(tt(g2[:, 1, :, :], pair[:, :, :, 0], pair[:, :, :, 1], ALU.min))
                settle()
                gg = g1[:].rearrange("p a t g -> p a (t g)")
                tt(gg[:, 0, :], g2[:, 0, :, 0], g2[:, 0, :, 1], ALU.max)
                tt(gg[:, 1, :], g2[:, 0, :, 0], g2[:, 0, :, 1], ALU.min)
                step(tt(gg[:, 2, :], g2[:, 1, :, 0], g2[:, 1, :, 1], ALU.max))
                settle()
                step(tt(gg[:, 1, :], gg[:, 1, :], gg[:, 2, :], ALU.max))
                settle()
                step(tt(gg[:, 3, :], gg[:, 0, :], gg[:, 1, :], ALU.add))
                settle()
                yield
                for t in range(QT):
                    gj = g1[:, 3, t, :].unsqueeze(1).to_broadcast([P, NG, NG])
                    gi = over(g1[:, 3, t, :], NG)
                    tt(gr[:, 0, t, :, :], gj, gi, ALU.is_gt)
                    m = tt(gr[:, 1, t, :, :], gj, gi, ALU.is_equal)
                step(m)
                settle()
                for t in range(QT):
                    m = tt(gr[:, 1, t, :, :], gr[:, 1, t, :, :], before, ALU.mult)
                step(m)
                settle()
                yield
                step(tt(gr[:, 2, :, :, :], gr[:, 0, :, :, :], gr[:, 1, :, :, :], ALU.add))
                settle()
                step(red(g1[:, 4, :, :], gr[:, 2, :, :, :], AX.X, ALU.add))
                settle()
                step(ts(g1[:, 5, :, :], g1[:, 4, :, :], 4.0, None, ALU.is_lt))
                settle()
                yield
                step(tt(msk[:].rearrange("p t (g c) -> p (t g) c", c=NE // NG), sc[:].rearrange("p t (g c) -> p (t g) c", c=NE // NG),
                        over(gg[:, 5, :], NE // NG), ALU.mult))
                settle()
                step(ts(msk[:], msk[:], 0.0, None, ALU.add))
                settle()
                pace()
                for t in range(QT):
                    m = v.max(v8[:, t, :], msk[:, t, :])
                step(m)
                settle()
                yield
                pace()
                for t in range(QT):
                    m = v.match_replace(rep[:, t, :], v8[:, t, :], msk[:, t, :], -1e30)
                step(m)
                settle()
                step(tt(rep[:], rep[:], msk[:], ALU.not_equal))
                settle()
                step(tt(comb[:], rep[:], sg[:], ALU.mult))
                settle()
                yield
                step(red(wsum[:], comb[:], AX.X, ALU.add))
                settle()
                step(ts(wsum[:], wsum[:], 1e-20, None, ALU.add))
                settle()
                step(v.reciprocal(wsum[:], wsum[:]))
                settle()
                for t in range(QT):
                    m = ts(comb[:, t, :], comb[:, t, :], wsum[:, t:t + 1], 1.25, ALU.mult, ALU.mult)
                m.then_inc(me_c.sem, 1)
                yield
                dve.wait_ge(me_ct.sem, me_ct.at(b, 1))
                step(v.tensor_copy(combt[:], bank(7, NE, 0, SEQ)))
                settle()
                step(v.tensor_copy(comb3[0:NE, :], combt[:]))
                settle()
                step(tt(combt[:], combt[:], comb3[0:NE, :], ALU.subtract))
                settle()
                step(v.tensor_copy(combm[:], combt[:]))
                settle()
                v.tensor_copy(comb3[NE:2 * NE, :], combm[:])
                step(tt(combt[:], combt[:], combm[:], ALU.subtract))
                settle()
                v.tensor_copy(comb3[2 * NE:, :], combt[:]).then_inc(me_c3.sem, 1)
                for c in range(EC + 1):
                    dve.wait_ge(me_tn.sem, me_tn.at(b, c + 1))
                    step(stt(h1[:], tnh[:], 1.0, bank(6, P, 0, SEQ), ALU.add, ALU.mult))
                    settle()
                    if c == 0:
                        stt(h2[:, 0, :], h1[:], 0.5, bank(6, P, SEQ, SEQ), ALU.mult, ALU.mult).then_inc(me_h.sem, 1)
                    else:
                        step(tt(h1[:], h1[:], bank(6, P, SEQ, SEQ), ALU.mult))
                        settle()
                        dve.wait_ge(me_cb.sem, me_cb.at(b, c))
                        tt(h2[:, c % 2, :], h1[:], bank(7, P, 0, SEQ), ALU.mult).then_inc(me_h.sem, 1)
                    yield
                yield
                dve.wait_ge(me_y.sem, me_y.at(b, 1))
                step(tt(res[:], tiles(bank(6, P, 0, SEQ)), xs[:], ALU.add))
                settle()
                yield from normalise(b, 3, front)

            def last_ffn(b):
                res, xs = front.res, xst
                yield
                lg = bank(6, P, 0, QT * E2).rearrange("p (t n) -> p t n", n=E2)
                dve.wait_ge(ff_l.sem, ff_l.at(b, 1))
                step(red(fs[:, 0, :], lg, AX.X, ALU.max))
                settle()
                tt(fp[:], lg, over(fs[:, 0, :], E2), ALU.subtract).then_inc(ff_d.sem, 1)
                dve.wait_ge(ff_e.sem, ff_e.at(b, 1))
                step(red(fs[:, 1, :], fp[:], AX.X, ALU.add))
                settle()
                step(v.reciprocal(fs[:, 1, :], fs[:, 1, :]))
                settle()
                step(tt(fp[:], fp[:], over(fs[:, 1, :], E2), ALU.mult))
                settle()
                step(ts(fq[:], fp[:], 0.3, None, ALU.is_gt))
                settle()
                step(red(fs[:, 2, :], fq[:], AX.X, ALU.add))
                settle()
                step(ts(fs[:, 3, :], fs[:, 2, :], -1.0, float(E2), ALU.mult, ALU.add))
                settle()
                tt(fs[:, 3, :], fs[:, 3, :], fp[:, :, 0], ALU.mult)
                step(tt(fs[:, 2, :], fs[:, 2, :], fp[:, :, 1], ALU.mult))
                settle()
                for t in range(QT):
                    m = stt(res[:, t, :], bank(7, P, t * 2 * D, D), fs[:, 3, t:t + 1], xs[:, t, :], ALU.mult, ALU.add)
                step(m)
                settle()
                for t in range(QT):
                    m = stt(res[:, t, :], bank(7, P, t * 2 * D + D, D), fs[:, 2, t:t + 1], res[:, t, :], ALU.mult, ALU.add)
                m.then_inc(ff_r.sem, 1)
                dve.wait_ge(ff_r.sem, ff_r.at(b, 1))
                yield
                yield from normalise(b, 6, front)

            run(dve, lambda n, b: [lambda: self_attention(b, 0), lambda: cross_attention(b, 0, 0, 1), lambda: experts(b),
                                   lambda: self_attention(b, 1), lambda: cross_attention(b, 1, 0, CUT), lambda: last_ffn(b),
                                  lambda: left_over(b), lambda: cross_attention(b, 1, CUT, XH)][n](), begin)
            counts.append(taken[0])
            assert counts == list(dve_steps), counts


def shape_constants():
    import numpy as np
    f = np.float32
    c = {"ident": np.eye(P, dtype=f)}
    inv = (1.0 / f(10000.0) ** (np.arange(0, HD, 2, dtype=f) / f(HD))).astype(f)
    fr = (np.arange(SEQ, dtype=f)[:, None] * inv[None, :]).astype(f)
    emb = np.repeat(fr, 2, axis=-1)
    cos, sin = np.cos(emb).astype(f).T, np.sin(emb).astype(f).T
    sign = np.where(np.arange(HD) % 2 == 0, -1.0, 1.0).astype(f)[:, None]
    c["rope"] = np.stack([np.tile(cos, (P // HD, 1)), np.tile(sin * sign, (P // HD, 1))], 1).astype(f)
    k, q = np.arange(P)[:, None], np.arange(P)[None, :]
    no = f(-1e30)
    c["tri"] = np.stack([np.where(k > q, no, 0), np.where(q > k, no, 0),
                         np.where(k > q - 2, no, 0), np.where(q > k - 2, no, 0)], 1).astype(f)
    c["hmask"] = ((np.arange(P) % 64 // HD)[:, None] == np.arange(HALF)[None, :]).astype(f)
    c["onehot"] = np.repeat(np.eye(NH, dtype=f)[:, :, None], P, 2)
    corner = np.zeros((1, 2 * P + 1), f)
    corner[0, P - 1], corner[0, P], corner[0, 2 * P] = 1, 1, no
    c["corner"] = corner
    j, g = np.arange(NG)[None, :], np.arange(NG)[:, None]
    c["before"] = np.broadcast_to((j < g).astype(f), (P, NG, NG)).copy()
    e, cc, m = np.arange(96) % NE, np.arange(EC), np.arange(P)
    c["sel3"] = (e[:, None, None] == 2 * cc[None, :, None] + m[None, None, :] // EI).astype(f)
    first = np.zeros((P, QT, NH), f)
    first[0, 0] = no
    c["first"] = first
    xcol = np.zeros((P, 4), f)
    xcol[DC:DC + 2, 1] = 1
    xcol[DC + 2, 0] = -BIG
    xcol[DC + 2, 3] = BIG
    c["xcol"] = xcol
    return c


def layouts(a):
    import numpy as np
    f = np.float32
    c = {}

    def halves(w):
        return np.stack([np.concatenate([w[:, 64 * k:64 * k + 64]] * 2, 1) for k in range(2)], 1)

    def rows(r):
        return np.ascontiguousarray(np.broadcast_to(r, (P,) + r.shape))

    swap = np.arange(D) ^ 1
    wq, wk = a["L0_attn_Wq"].T, a["L0_attn_Wk"].T
    c["w0qk"] = np.stack([x for w in (wq, wk) for k in range(2) for x in (halves(w)[:, k], halves(w[:, swap])[:, k])], 1)
    c["w0v"], c["w0o"] = a["L0_attn_Wv"].T, a["L0_attn_Wo"].T
    c["w1qk"] = np.concatenate([halves(a["L1_attn_W_q"]), halves(a["L1_attn_W_k"])], 1)
    bq, bk = a["L1_attn_b_q"], a["L1_attn_b_k"]
    rk, rv = a["L1_attn_rel_k_table"], a["L1_attn_rel_v_table"]
    twice = lambda x: [np.tile(x[:64], 2), np.tile(x[64:], 2)]
    c["w1bqk"] = np.stack(twice(bq) + twice(bk) + [np.tile(rk[0], P // HD)], 1)
    c["w1tok"] = np.concatenate([a["L1_attn_W_q"], a["L1_attn_W_k"], a["L1_attn_W_v"]], 1)
    c["b1tok"] = rows(np.stack([bq, bk, a["L1_attn_b_v"]]))
    c["r1k"] = rows(np.stack([np.tile(rk[n], NH) for n in range(3)]))
    c["r1v"] = rows(np.stack([np.tile(rv[n], NH) for n in range(3)]))
    c["w1o"], c["b1o"] = a["L1_attn_W_o"], rows(a["L1_attn_b_o"])
    c["x0wq"], c["x0wk"] = a["L0_xattn_Wq"].T, a["L0_xattn_Wk"].T
    c["x0b"] = np.stack([a["L0_xattn_bq"], a["L0_xattn_bk"]], 1)
    c["x0v"] = np.concatenate([a["L0_xattn_Wv"], a["L0_xattn_bv"][None]], 0)
    heads = lambda w: w.reshape(XH, XD, -1).transpose(1, 0, 2)
    c["x1wq"], c["x1wk"], c["x1wv"] = heads(a["L1_xattn_Wq"]), heads(a["L1_xattn_Wk"]), heads(a["L1_xattn_Wv"])
    c["x1wo"] = heads(a["L1_xattn_Wo"].T)
    c["x1b"] = np.stack([a[n].reshape(XH, XD).T for n in ("L1_xattn_bq", "L1_xattn_bk", "L1_xattn_bv")], 1)
    c["x1bo"] = rows(a["L1_xattn_bo"])
    c["gw"], c["gb"] = a["L0_ffn_gate_w"].T, rows(a["L0_ffn_gate_bias"])
    up = lambda w, s: np.concatenate([s.T[:, None, :], w.reshape(EC, P, D).transpose(2, 0, 1)], 1)
    c["wg"], c["wu"] = up(a["L0_ffn_w_gate"], a["L0_ffn_sh_gate"]), up(a["L0_ffn_w_up"], a["L0_ffn_sh_up"])
    wd = a["L0_ffn_w_down"].transpose(0, 2, 1).reshape(EC, P, D).transpose(1, 0, 2)
    c["wd"] = np.concatenate([a["L0_ffn_sh_down"].T[:, None, :], wd], 1)
    c["f_gate"] = a["L1_ffn_gate_W"].T
    c["f_we"] = a["L1_ffn_expert_W"][0:2].transpose(1, 0, 2)
    c["f_wo"] = a["L1_ffn_out_W"].T
    c["x"], c["ctx"] = a["x"], a["ctx_768"]
    c["ctxT"] = a["ctx_768"].transpose(0, 2, 1)
    c["mask"] = a["mask_BxS2_bk0"]
    return c


def kernel(**inputs):
    import numpy as np
    import concourse.bacc as bacc
    from concourse.bass_utils import run_bass_kernel_spmd

    tables = dict(shape_constants())
    tables.update(layouts({k: np.asarray(v) for k, v in inputs.items()}))
    nc = bacc.Bacc("TRN2", target_bir_lowering=False, num_devices=1)
    arrays, d = {}, {}
    for name, t in tables.items():
        t = np.ascontiguousarray(t)
        arrays["in_" + name] = t
        d[name] = nc.dram_tensor("in_" + name, t.shape, mybir.dt.from_np(t.dtype), kind="ExternalInput").ap()
    out = nc.dram_tensor("out_0", (NB, SEQ, D), F32, kind="ExternalOutput").ap()
    decoder_kernel(nc, d, out, DVE_STEPS)
    r = run_bass_kernel_spmd(nc, [arrays], core_ids=[0])
    return r.results[0]["out_0"]


DVE_STEPS = (140, 151, 196, 56, 45)
```

```python
from contextlib import ExitStack

import concourse.bass as bass
from concourse import mybir

F32 = mybir.dt.float32
F16 = mybir.dt.float16
BF16 = mybir.dt.bfloat16
I32 = mybir.dt.int32
U8 = mybir.dt.uint8
ALU = mybir.AluOpType
ACT = mybir.ActivationFunctionType
AX = mybir.AxisListType

P = 128
NB, SEQ, D = 8, 256, 128
QT = SEQ // P
CTX, DC = 1601, 96
NK = (CTX + P - 1) // P
LASTK = CTX - (NK - 1) * P
NH, HD = 16, 8
HALF = NH // 2
XH, XD = 12, 64
KE = DC + 3
SHIFT = DC
NE, EI = 32, 64
EC = NE * EI // P
NG = 8
E2 = 8
EPS = 1e-5
BIG = 60000.0
CHUNKS = [(0, 401), (401, 400), (801, 400), (1201, 400)]
NPAIR = (NK + 1) // 2


class Count:

    def __init__(self, sem, per):
        self.sem, self.per = sem, per

    def at(self, b, n):
        assert 1 <= n <= self.per, (n, self.per)
        return b * self.per + n


def weave(front, cross, weights, n_cross):
    total, done, b = sum(weights), 0, 0
    for w in weights:
        while (2 * b + 1) * total <= (2 * done + w) * n_cross and b < n_cross:
            next(cross)
            b += 1
        next(front)
        done += w
    while b < n_cross:
        next(cross)
        b += 1


def spans(n, *runs):
    out = [w for count, w in runs[:-1] for _ in range(count)]
    return out + [runs[-1][1]] * (n - len(out))


def chain(*parts):
    for p in parts:
        yield from p


def counted(pieces, n):
    taken = 0
    for p in pieces:
        taken += 1
        yield
    assert taken == n, (taken, n)


def pair_tiles(p):
    return [(kt, P if kt < NK - 1 else LASTK) for kt in (2 * p, 2 * p + 1) if kt < NK]


def next_chunks(h, p):
    if p >= 4:
        return [(h + 2, p - 4)] if h + 2 < XH else []
    return [(h + 1, q) for q in ((3,), (4,), (5, 6), (7,))[p]] if h + 1 < XH else []


CHUNK_BANK = [0, 0, 4, 0, 4, 0, 4, 4]
AHEAD = 3


def decoder_kernel(nc, d, out, dve_steps):
    ctx = ExitStack()
    with ctx:
        def sb(name, shape, dt=F32):
            return ctx.enter_context(nc.sbuf_tensor(name, shape, dt))

        def count(name, per=1):
            return Count(ctx.enter_context(nc.semaphore(name)), per)

        first_loads, loads, late = [], [], []

        qk = sb("qk", [P, 4, SEQ])
        pr = sb("pr", [P, 4, 2 * SEQ])
        qtmp = pr
        tok = sb("tok", [P, QT, 3, D])
        xq_h = sb("xq_h", [KE, XH, SEQ], F16)
        xp = sb("xp", [P, 3, 2 * SEQ])
        qm_h = sb("qm_h", [P, NH, SEQ], F16)
        qm_l = sb("qm_l", [P, NH, SEQ], F16)
        vm = sb("vm", [P, (QT * NH + 1) * P])
        xq_l = sb("xq_l", [KE, XH, SEQ], F16)
        cx_hl = sb("cx_hl", [KE, 2 * CTX], F16)
        cx_tok = sb("cx_tok", [P, 2 * NK * (DC + 1)], F16)
        x1k_e = cx_tok[:].bitcast(F32)[:, 0:XH * KE].rearrange("p (h n) -> p h n", h=XH)

        def flat(t):
            return t.rearrange("p a n -> p (a n)")

        tok_flat = tok[:].rearrange("p t a n -> p (t a n)")

        def const(name, home=None, at=0):
            src = d[name]
            if home is None:
                t = sb("c_" + name, list(src.shape))[:]
            else:
                t = home[0:src.shape[0], at:at + src.shape[1] * src.shape[2]].rearrange("p (a n) -> p a n", n=src.shape[2])
            early = ("ident", "rope", "tri", "hmask", "onehot", "xcol", "w0qk", "w0v", "w0o")
            (first_loads if name in early else late if name in ("wg", "wu", "wd") else loads).append((t, src))
            return t

        ident = const("ident")
        rope = const("rope")
        tri = const("tri", flat(qk[:]))
        hmask = const("hmask")
        onehot = const("onehot", flat(qm_h[:]).bitcast(F32))
        corner = const("corner")
        before = const("before")
        first = const("first")
        xcol = const("xcol")
        w0qk = const("w0qk")
        w0v = const("w0v")
        w0o = const("w0o")
        w1qk = const("w1qk")
        w1bqk = const("w1bqk")
        w1tok = const("w1tok")
        b1tok = const("b1tok", tok_flat, 0)
        r1k = const("r1k", tok_flat, 3 * D)
        r1v = const("r1v", flat(xp[:]), XH * DC)
        w1o = const("w1o")
        b1o = const("b1o")
        x0wq = const("x0wq")
        x0wk = const("x0wk")
        x0b = const("x0b")
        x0v = const("x0v")
        x1wq = const("x1wq", flat(xq_l[:]).bitcast(F32))
        x1wk = const("x1wk", flat(xq_h[:]).bitcast(F32))
        x1wv = const("x1wv", flat(xp[:]))
        x1wo = const("x1wo", cx_hl[:].bitcast(F32))
        x1b = const("x1b")
        x1bo = const("x1bo")
        gw = const("gw")
        gb = const("gb")
        wg = const("wg")
        wu = const("wu")
        wd = const("wd")
        sel3 = const("sel3", flat(wd))
        f_gate = const("f_gate")
        f_we = const("f_we")
        f_wo = const("f_wo")

        ident16 = sb("ident16", [P, P], F16)
        identb = sb("identb", [P, P], BF16)
        trib = sb("trib", [P, 4, P], BF16)
        onehotb = sb("onehotb", [NH, NH, P], BF16)
        cornerb = sb("cornerb", [1, 2 * P + 1], BF16)
        sel3b = sb("sel3b", [96, EC, P], BF16)
        k1b = sb("k1b", [P, 2])
        bias0 = sb("bias0", [P, 3, D])
        bias1 = sb("bias1", [P, 2, D])
        vfar = sb("vfar", [P, D])
        xk_e = x1k_e[0:XD]
        x0k_e = sb("x0k_e", [P, KE])
        a_mat = sb("a_mat", [P, 1 + XH, KE])
        a_c = sb("a_c", [KE, 1 + XH])
        g_mat = sb("g_mat", [DC + 1, 1 + XH, D + 1])
        f_m = sb("f_m", [P, 2 * D])

        xin = sb("xin", [P, QT, D])
        xsf = sb("xsf", [P, QT, D])
        xsx = sb("xsx", [P, QT, D])
        xst = sb("xst", [P, QT, D])
        ys = sb("ys", [P, QT, D])
        source = [xin, xsf, xsf, xsf, xsx, xst, ys]

        class Side:

            def __init__(self, c):
                self.xt = sb("xt" + c, [P, 1 + SEQ])
                self.res = sb("res" + c, [P, QT, D])
                self.st6 = sb("st6" + c, [P, QT, 6])
                self.mv = sb("mv" + c, [P, QT, 2])
                self.nr = sb("nr" + c, [P, 2, QT])
                self.nri = sb("nri" + c, [P, QT], I32)
                self.xmax = sb("xmax" + c, [P, QT, 4])
                self.xneg = sb("xneg" + c, [P, QT], F16)
                self.xo = sb("xo" + c, [DC + 1, SEQ])
                self.xr = sb("xr" + c, [P, QT])

        front, cross = Side("_f"), Side("_x")
        carrier = sb("carrier", [P, 1])

        qk_h = sb("qk_h", [P, 4, SEQ], F16)
        q_l = sb("q_l", [P, 2, SEQ], F16)
        smax = sb("smax", [P, QT, NH])
        nmb = sb("nmb", [P, QT, NH], BF16)
        nmt = sb("nmt", [NH, SEQ], BF16)
        rden = sb("rden", [P, SEQ])
        ot = sb("ot", [P, SEQ])
        tok1 = sb("tok1", [P, QT, 2, D])
        near = sb("near", [P, QT, 2, NH])
        prod = sb("prod", [P, QT, 2, D])
        esum = sb("esum", [P, QT, NH])
        wnear = sb("wnear", [P, QT, 2, 2, HALF * HD])

        pr_l = sb("pr_l", [P, 4, 2 * SEQ], F16)
        v32 = sb("v32", [P, D])

        ct32 = sb("ct32", [P, CTX])
        mrow_u8 = sb("mrow_u8", [P, CTX], U8)

        class Context:
            pass

        cf, cx = Context(), Context()
        cf.h = sb("c_h", [KE, CTX], F16)
        cf.l = sb("c_l", [DC, CTX], F16)
        cf.tok = sb("c_tok", [P, NK, DC + 1])
        cx.h, cx.l = cx_hl[:, 0:CTX], cx_hl[0:DC, CTX:]
        cx_tiles = cx_tok[:].rearrange("p (a c) -> p a c", c=DC + 1)
        cx.tok_h, cx.tok_l = cx_tiles[:, 0:NK, :], cx_tiles[:, NK:, :]
        xp_l = sb("xp_l", [P, 3, 2 * SEQ], F16)
        x0q_h = sb("x0q_h", [KE, 1, SEQ], F16)
        x0q_l = sb("x0q_l", [KE, 1, SEQ], F16)

        sg = sb("sg", [P, QT, NE])
        sc = sb("sc", [P, QT, NE])
        g2 = sb("g2", [P, 2, QT * NG, 2])
        g1 = sb("g1", [P, 6, QT, NG])
        gr = sb("gr", [P, 3, QT, NG, NG])
        msk = sb("msk", [P, QT, NE])
        rep = sb("rep", [P, QT, NE])
        v8 = sb("v8", [P, QT, 8])
        comb = sb("comb", [P, QT, NE])
        wsum = sb("wsum", [P, QT])
        combt = sb("combt", [NE, SEQ])
        combm = sb("combm", [NE, SEQ], BF16)
        comb3 = sb("comb3", [96, SEQ], BF16)
        h2 = sb("h2", [P, 2, SEQ])
        tnh = qk[:, 0:2, :]
        yt = qk[:, 2, :]
        qm_l32 = flat(qm_l[:]).bitcast(F32).rearrange("p (a n) -> p a n", n=SEQ)
        ga, ub = qm_l32[:, 0:2, :], qm_l32[:, 2:4, :]
        qm_h32 = flat(qm_h[:]).bitcast(F32).rearrange("p (a n) -> p a n", n=2 * SEQ)

        def spread(k):
            return pr[:, k, :] if k < 4 else qm_h32[:, k - 4, :]
        fp = sb("fp", [P, QT, E2])
        fq = sb("fq", [P, QT, E2])
        fs = sb("fs", [P, 4, QT])

        ps = ctx.enter_context(nc.psum_tensor("ps", [P, 8, 512], F32))

        def bank(i, rows=P, c0=0, n=512):
            return ps[0:rows, i, c0:c0 + n]

        def tiles(ap, n=P):
            return ap.rearrange("p (t n) -> p t n", n=n)

        vm16 = vm[:].bitcast(F16)
        v_h, v_l = vm16[:, 0:(QT * NH + 1) * P], vm16[:, (QT * NH + 1) * P:]

        def value_slots(vm, t, f, off):
            at = (t * NH + f * HALF) * P + off
            return vm[:, at:at + HALF * (P + HD)].rearrange("p (h c) -> p h c", c=P + HD)[:, :, 0:HD]

        def value_of(vm, t, h):
            at = (t * NH + h) * P
            return vm[:, at:at + P]

        def xp_slot(i, n):
            return xp[:, n % 3, :] if i == 1 else pr[:, n % 4, :]

        def pr_high(g):
            return pr[:, g % 4, :].bitcast(BF16)[:, 1::2]

        def xp_high(n, k_, c0, w):
            return xp[0:k_, n % 3, :].bitcast(BF16)[:, 2 * c0 + 1:2 * (c0 + w):2]

        loaded_first = ctx.enter_context(nc.semaphore("loaded_first"))
        loaded = ctx.enter_context(nc.semaphore("loaded"))
        loaded_late = ctx.enter_context(nc.semaphore("loaded_late"))
        made = ctx.enter_context(nc.semaphore("made"))
        folded = ctx.enter_context(nc.semaphore("folded"))
        unfolded = ctx.enter_context(nc.semaphore("unfolded"))
        dve_self = ctx.enter_context(nc.semaphore("dve_self"))
        dve_step = ctx.enter_context(nc.semaphore("dve_step"))
        x_in = count("x_in", 16)
        ct_in = count("ct_in", 32)
        tok_in = count("tok_in", 32)
        ct_copied = count("ct_copied", 32)
        x_out = count("x_out", 16)
        tr_ready = [count(f"tr_ready{n}") for n in range(6)]
        xt_ready = [count(f"xt_ready{n}") for n in range(6)]
        xs_ready = [count(f"xs_ready{n}") for n in range(7)]

        def both(name, per):
            return [count(f"{name}{i}", per) for i in range(2)]

        sa_proj = both("sa_proj", 4)
        sa_tok = [count("sa_tok0"), count("sa_tok1", 4)]
        sa_qk = both("sa_qk", 4)
        sa_hi = both("sa_hi", 1)
        sa_ks = both("sa_ks", 1)
        sa_ql = both("sa_ql", 1)
        sa_qm = both("sa_qm", 1)
        sa_qn = both("sa_qn", 1)
        sa_v = [count("sa_v0"), count("sa_v1", 4)]
        sa_x = both("sa_x", 12)
        sa_xd = both("sa_xd", 12)
        sa_nm = both("sa_nm", 1)
        sa_nt = both("sa_nt", 1)
        sa_ntc = both("sa_ntc", 1)
        sa_s = both("sa_s", 12)
        sa_e = both("sa_e", 12)
        sa_l = both("sa_l", 12)
        sa_vl = count("sa_vl")
        sa_u = both("sa_u", 1)
        sa_ot = both("sa_ot", 1)
        sa_y = both("sa_y", 1)
        sa_r = both("sa_r", 1)
        sa_ne = count("sa_ne")
        sa_nx = count("sa_nx")
        sa_w = count("sa_w")
        c_hi = count("c_hi")
        c_ext = count("c_ext")
        c_lo = count("c_lo")
        tok_hi = count("tok_hi")
        tok_lo = count("tok_lo")

        def heads_(name, per):
            return [count(f"{name}0", per), count(f"{name}1", per * XH)]

        xa_q = heads_("xa_q", 1)
        xa_qh = heads_("xa_qh", 1)
        xa_ql = heads_("xa_ql", 1)
        xa_x = heads_("xa_x", 8)
        xa_xd = heads_("xa_xd", 8)
        xa_nm = heads_("xa_nm", 1)
        xa_mr = heads_("xa_mr", 1)
        xa_mc = heads_("xa_mc", 1)
        xa_s = heads_("xa_s", NPAIR)
        xa_e = heads_("xa_e", NPAIR)
        xa_l = count("xa_l", XH * NPAIR)
        xa_pv = heads_("xa_pv", 1)
        xa_o = heads_("xa_o", 1)
        xa_f = heads_("xa_f", 1)
        xa_a = heads_("xa_a", 1)
        me_l = count("me_l")
        me_t = count("me_t")
        me_c = count("me_c")
        me_ct = count("me_ct")
        me_c3 = count("me_c3")
        me_gu = count("me_gu", EC + 1)
        me_tn = count("me_tn", EC + 1)
        me_cb = count("me_cb", EC // 2)
        me_cc = count("me_cc", EC // 2)
        me_h = count("me_h", EC + 1)
        me_d = count("me_d")
        me_yt = count("me_yt")
        me_y = count("me_y")
        qdone = [count("qdone", 4), sa_qk[1]]
        ff_l = count("ff_l")
        ff_d = count("ff_d")
        ff_e = count("ff_e")
        ff_r = count("ff_r")

        SETUP = 7
        SA_SCALE = HD ** -0.5
        block = ctx.enter_context(nc.Block())

        def run(eng, sublayer, begin=lambda part, i=None: None):
            def part(n, b):
                return counted(sublayer(n, b), PIECES[n])

            def front_chain(b, last):
                if b is None:
                    return part(5, last)
                return chain(part(0, b), part(1, b), *([part(5, last)] if last is not None else []), part(2, b), part(3, b))

            def rest(b):
                return chain(part(7, b), part(6, b))

            def weights(*parts):
                return [w for n in parts for w in spans(PIECES[n], *WEIGHT[n])]

            begin(0)
            weave(front_chain(0, None), part(8, 0), weights(0, 1, 2, 3), PIECES[8])
            begin(1)
            weave(front_chain(1, None), part(4, 0), weights(0, 1, 2, 3), PIECES[4])
            with eng.Fori(2, NB) as i:
                begin(2, i)
                weave(front_chain(i, i - 2), chain(rest(i - 2), part(4, i - 1)), weights(0, 1, 5, 2, 3),
                      PIECES[7] + PIECES[6] + PIECES[4])
            begin(3)
            weave(rest(NB - 2), iter(()), weights(7, 6), 0)
            weave(front_chain(None, NB - 2), part(4, NB - 1), weights(5), PIECES[4])
            begin(4)
            weave(chain(rest(NB - 1), part(5, NB - 1)), iter(()), weights(7, 6, 5), 0)

        NORM = 6
        WEIGHT = [[(0, 40)], [(0, 30)], [(8, 54), (4, 47), (17, 40), (0, 47)],
                  [(0, 46)], [(0, 0)], [(0, 30)], [(0, 30)], [(0, 10)], [(0, 0)]]
        CUT = 11
        QUOTIENTS = 2
        HIGH_AT = 3
        LOADING = 4
        ROUTING = 5
        PIECES = [19 + QUOTIENTS + NORM, 17 + NORM, EC + 4 + ROUTING + EC // 4 + NORM, 20 + QUOTIENTS + NORM, 1 + XH // 2 + 4 + 2 + CUT * NPAIR, 2 + NORM, NORM,
                  (XH - CUT) * NPAIR + 2, LOADING + 2 * XH + 4]

        @block.sync
        def _(sp):
            for t, src in first_loads:
                sp.dma_start(t, src).then_inc(loaded_first, 16)
            sp.sem_inc(x_out.sem, 16)

            def at_(b):
                return bass.ds(b, 1)

            def load_x(b):
                sp.dma_start(xin[:], d["x"][at_(b)].rearrange("a (t p) n -> p (a t) n", p=P)).then_inc(x_in.sem, 16)

            def load_context(b):
                sp.dma_start(ct32[0:DC, :], d["ctxT"][at_(b)].rearrange("a c k -> (a c) k")).then_inc(ct_in.sem, 16)
                sp.dma_start(mrow_u8[DC + 2:DC + 3, :], d["mask"][at_(b), :]).then_inc(ct_in.sem, 16)

            def load_tokens(b):
                if not (isinstance(b, int) and b == 0):
                    sp.wait_ge(tok_lo.sem, tok_lo.at(b - 1, 1))
                sp.dma_start(cf.tok[:, 0:NK - 1, 0:DC],
                             d["ctx"][at_(b), 0:(NK - 1) * P, :].rearrange("a (t p) c -> p (a t) c", p=P)).then_inc(tok_in.sem, 16)
                sp.dma_start(cf.tok[0:LASTK, NK - 1, 0:DC],
                             d["ctx"][at_(b), (NK - 1) * P:CTX, :].rearrange("a k c -> (a k) c")).then_inc(tok_in.sem, 16)

            def hand_over(b):
                sp.wait_ge(c_lo.sem, c_lo.at(b, 1))
                sp.wait_ge(c_ext.sem, c_ext.at(b, 1))
                sp.wait_ge(xs_ready[2].sem, xs_ready[2].at(b, 1))
                sp.dma_start(cx.h, cf.h[:]).then_inc(ct_copied.sem, 16)
                sp.dma_start(cx.l, cf.l[:]).then_inc(ct_copied.sem, 16)
                sp.wait_ge(ct_copied.sem, ct_copied.at(b, 32))

            def store(b):
                sp.wait_ge(xs_ready[6].sem, xs_ready[6].at(b, 1))
                sp.dma_start(out[at_(b)].rearrange("a (t p) n -> p (a t) n", p=P), ys[:]).then_inc(x_out.sem, 16)

            def next_x(b):
                sp.wait_ge(xs_ready[1].sem, xs_ready[1].at(b, 1))
                load_x(b + 1)

            load_x(0)
            for t, src in loads:
                sp.dma_start(t, src).then_inc(loaded, 16)
            load_context(0)
            load_tokens(0)
            for n, (t, src) in enumerate(late):
                if n == len(late) - 1:
                    sp.wait_ge(made, SETUP)
                sp.dma_start(t, src).then_inc(loaded_late, 16)
            next_x(0)
            sp.wait_ge(folded, 2 * XH + 3)
            hand_over(0)
            load_context(1)
            load_tokens(1)
            next_x(1)
            with sp.Fori(2, NB - 1) as i:
                sp.wait_ge(xa_a[1].sem, xa_a[1].at(i - 2, XH))
                hand_over(i - 1)
                load_context(i)
                load_tokens(i)
                next_x(i)
                store(i - 2)
            sp.wait_ge(xa_a[1].sem, xa_a[1].at(NB - 3, XH))
            hand_over(NB - 2)
            load_context(NB - 1)
            load_tokens(NB - 1)
            store(NB - 3)
            sp.wait_ge(xa_a[1].sem, xa_a[1].at(NB - 2, XH))
            hand_over(NB - 1)
            store(NB - 2)
            store(NB - 1)
            sp.wait_ge(x_out.sem, 16 * NB + 16)

        @block.tensor
        def _(pe):
            mm = nc.tensor.matmul
            pe.wait_ge(loaded_first, 16 * len(first_loads))
            pe.wait_ge(made, 1)

            def folding(_):
                for _ in range(LOADING):
                    yield
                pe.wait_ge(loaded, 16 * len(loads))
                pe.wait_ge(made, SETUP)
                for h in range(1 + XH):
                    wq, wk = (x0wq[:, :], x0k_e[:, :]) if h == 0 else (x1wq[:, h - 1, :], xk_e[:, h - 1, :])
                    bq = x0b[:, 0:1] if h == 0 else x1b[:, 0, h - 1:h]
                    if h >= 2:
                        pe.wait_ge(unfolded, 2 * (h - 1))
                    mm(bank(h % 2, P, 0, KE), wq, wk, start=True, stop=True)
                    mm(bank(h % 2, KE, 256, 1), wk, bq, start=False, stop=True, skip_group_check=True).then_inc(folded, 1)
                    yield
                for h in range(XH):
                    if h >= 2:
                        pe.wait_ge(unfolded, 2 * (1 + XH) + h - 1)
                    mm(bank(2 + h % 2, DC, 0, D), x1wv[:, h, :], x1wo[:, h, :], start=True, stop=True)
                    mm(ps[DC:DC + 1, 2 + h % 2, 0:D], x1b[:, 2, h:h + 1], x1wo[:, h, :], start=True, stop=True,
                       skip_group_check=True).then_inc(folded, 1)
                    yield
                for e in range(2):
                    if e == 1:
                        pe.wait_ge(unfolded, 2 * (1 + XH))
                    mm(bank(4 - 4 * e, P, 0, D), f_we[:, e, :], f_wo[:, :], start=True, stop=True).then_inc(folded, 1)
                    yield
                pe.wait_ge(unfolded, 2 * (1 + XH) + XH + 2)
                yield

            def transposes(b, n):
                if n == 0:
                    pe.wait_ge(x_in.sem, x_in.at(b, 16))
                else:
                    pe.wait_ge(xs_ready[n].sem, xs_ready[n].at(b, 1))
                for t in range(QT):
                    m = nc.tensor.transpose(bank(4 if n == 4 else 5, P, t * P, P), source[n][:, t, :], ident)
                m.then_inc(tr_ready[n].sem, 1)

            def self_attention(b, i):
                w = w0qk if i == 0 else w1qk
                xt = front.xt
                x = xt[:, 1:1 + SEQ]
                transposes(b, 3 * i)
                yield
                if i == 0 and not (isinstance(b, int) and b == 0):
                    pe.wait_ge(sa_r[1].sem, sa_r[1].at(b - 1, 1))
                pe.wait_ge(xt_ready[3 * i].sem, xt_ready[3 * i].at(b, 1))
                for j in range(4):
                    if j >= 2:
                        pe.wait_ge(qdone[i].sem, qdone[i].at(b, j - 1))
                    if i == 0:
                        mm(bank(6 + j % 2, P, 0, SEQ), w[:, 2 * j, :], x, start=True, stop=True)
                        m = mm(bank(6 + j % 2, P, SEQ, SEQ), w[:, 2 * j + 1, :], x, start=False, stop=True, skip_group_check=True)
                    else:
                        m = mm(bank(6 + j % 2, P, 0, SEQ), w[:, j, :], x, start=True, stop=True)
                    m.then_inc(sa_proj[i].sem, 1)
                    if j == 1:
                        if i == 0:
                            for t in range(QT):
                                m = mm(bank(5, P, t * P, P), xt[:, 1 + t * P:1 + (t + 1) * P], w0v, start=(t == 0), stop=True, skip_group_check=True)
                            m.then_inc(sa_tok[i].sem, 1)
                        else:
                            mm(bank(5, P, 0, 3 * D), xt[:, 1:1 + P], w1tok, start=True, stop=True).then_inc(sa_tok[i].sem, 1)
                        yield
                if i == 1:
                    pe.wait_ge(sa_v[i].sem, sa_v[i].at(b, 1))
                    mm(bank(5, P, 0, 2 * D), xt[:, 0:P], w1tok[:, D:], start=True, stop=True).then_inc(sa_tok[i].sem, 1)
                    yield
                    pe.wait_ge(qdone[i].sem, qdone[i].at(b, 4))
                    mm(bank(6, P, 0, 3 * D), xt[:, 1 + P:1 + 2 * P], w1tok, start=True, stop=True).then_inc(sa_tok[i].sem, 1)
                    mm(bank(7, P, 0, 2 * D), xt[:, P:2 * P], w1tok[:, D:], start=True, stop=True).then_inc(sa_tok[i].sem, 1)
                yield
                for _ in range(3):
                    yield
                pe.wait_ge(sa_ks[i].sem, sa_ks[i].at(b, 1))
                pe.wait_ge(sa_qm[i].sem, sa_qm[i].at(b, 1))
                if i == 0:
                    pe.wait_ge(sa_vl.sem, sa_vl.at(b, 1))
                else:
                    pe.wait_ge(sa_v[1].sem, sa_v[1].at(b, 4))
                g = 0
                trq = trib[:, 2 * i + 1, :]
                for t in range(QT):
                    n = (t + 1) * P
                    per = 512 // n
                    for h0 in range(0, NH, per):
                        if g >= 3:
                            pe.wait_ge(sa_xd[i].sem, sa_xd[i].at(b, g - 2))
                        o = ps[:, 5 + g % 3, :].rearrange("p (h n) -> p h n", n=n)
                        for k in range(per):
                            mm(o[:, k, t * P:n], identb[:], trq, start=(k == 0), stop=False, skip_group_check=True)
                            if i == 1 and t == 1:
                                mm(o[:, k, P - 1:P], cornerb[0:1, P:2 * P], cornerb[0:1, 2 * P:], start=False, stop=False, skip_group_check=True)
                        for k in range(per):
                            h = h0 + k
                            m = mm(o[:, k, :], qm_h[:, h, t * P:(t + 1) * P], qk_h[:, 2 + h // HALF, 0:n],
                                   start=False, stop=True, skip_group_check=True)
                        m.then_inc(sa_x[i].sem, 1)
                        g += 1
                        if g % 3 == 0:
                            yield
                yield
                pe.wait_ge(sa_nm[i].sem, sa_nm[i].at(b, 1))
                psb = ps[0:NH, 5, :].bitcast(BF16)
                for t in range(QT):
                    m = nc.tensor.transpose(psb[:, t * P:(t + 1) * P], nmb[:, t, :], identb[:])
                m.then_inc(sa_nt[i].sem, 1)
                yield
                pe.wait_ge(sa_ntc[i].sem, sa_ntc[i].at(b, 1))
                pe.wait_ge(sa_qn[i].sem, sa_qn[i].at(b, 1))
                trk = trib[:, 2 * i, :]

                def scores(g):
                    if g >= 2:
                        pe.wait_ge(sa_e[i].sem, sa_e[i].at(b, g - 1))
                    kt, per, h0 = (0, 2, 2 * g) if g < 8 else (1, 4, 4 * (g - 8))
                    n = SEQ if kt == 0 else P
                    o = ps[:, 6 + g % 2, :].rearrange("p (h n) -> p h n", n=n)
                    for k in range(per):
                        h = h0 + k
                        keys = qk_h[:, 2 + h // HALF, kt * P:(kt + 1) * P]
                        mm(o[:, k, :], keys, qm_h[:, h, SEQ - n:], start=(k == 0), stop=False, skip_group_check=True)
                        if i == 1 and kt == 0:
                            mm(o[:, k, P:P + 1], cornerb[0:1, 0:P], cornerb[0:1, 2 * P:], start=False, stop=False, skip_group_check=True)
                        mm(o[:, k, 0:P], identb[:], trk, start=False, stop=False, skip_group_check=True)
                        mm(o[:, k, :], onehotb[:, h, :], nmt[:, SEQ - n:], start=False, stop=False, skip_group_check=True)
                        m = mm(o[:, k, :], keys, qm_l[:, h, SEQ - n:], start=False, stop=True, skip_group_check=True)
                    m.then_inc(sa_s[i].sem, 1)

                def values(g):
                    pe.wait_ge(sa_l[i].sem, sa_l[i].at(b, g + 1))
                    kt, per, h0 = (0, 2, 2 * g) if g < 8 else (1, 4, 4 * (g - 8))
                    n = SEQ if kt == 0 else P
                    for k in range(per):
                        h = h0 + k
                        o = bank(5, P, (h // HALF) * SEQ + SEQ - n, n)
                        high, cols = pr_high(g)[:, k * n:(k + 1) * n], slice(k * n, (k + 1) * n)
                        mm(o, value_of(v_h, kt, h), high, start=(g == 0 and k == 0), stop=False, skip_group_check=True)
                        mm(o, value_of(v_l, kt, h), high, start=False, stop=False, skip_group_check=True)
                        m = mm(o, value_of(v_h, kt, h), pr_l[:, g % 4, cols], start=False,
                               stop=(kt == 1 or h % HALF == HALF - 1), skip_group_check=True)
                    return m

                for g in range(0, 12, 2):
                    scores(g)
                    scores(g + 1)
                    if g:
                        values(g - 2)
                        values(g - 1)
                    yield
                values(10)
                m = values(11)
                if i == 1:
                    pe.wait_ge(sa_w.sem, sa_w.at(b, 1))
                    for f in range(2):
                        for t in range(QT):
                            m = mm(bank(5, P, f * SEQ + t * P, P), wnear[:, t, f, :, :].rearrange("p a n -> p (a n)"),
                                   ident, start=False, stop=True, skip_group_check=True)
                m.then_inc(sa_u[i].sem, 1)
                for _ in range(1 + QUOTIENTS):
                    yield
                pe.wait_ge(sa_ot[i].sem, sa_ot[i].at(b, 1))
                for t in range(QT):
                    m = mm(bank(6, P, t * P, P), ot[:, t * P:(t + 1) * P], w0o if i == 0 else w1o,
                           start=(t == 0), stop=True, skip_group_check=True)
                m.then_inc(sa_y[i].sem, 1)
                for _ in range(NORM):
                    yield

            def cross_attention(b, i, h_from, h_to):
                n_heads, side, c, qh, ql = (1, front, cf, x0q_h, x0q_l) if i == 0 else (XH, cross, cx, xq_h, xq_l)
                b_row, b_s, b_o, b_y = (5, 6, 5, 6) if i == 0 else (4, 1, 3, 0)
                u_a = 0 if i == 0 else 1
                lag = 1 + i

                def max_pass(h, q, bk):
                    t, (k0, n) = q // 4, CHUNKS[q % 4]
                    mm(bank(bk, P, 0, n), qh[:, h, t * P:(t + 1) * P], c.h[:, k0:k0 + n], start=True, stop=True).then_inc(xa_x[i].sem, 1)

                def next_chunk(h, q):
                    if q == 0:
                        if h == 2:
                            pe.wait_ge(xa_xd[i].sem, xa_xd[i].at(b, 8 + 6))
                        elif h > 2:
                            pe.wait_ge(xa_a[i].sem, xa_a[i].at(b, h - 2))
                    elif q == 2:
                        if h > 0:
                            pe.wait_ge(xa_mc[i].sem, xa_mc[i].at(b, h))
                    else:
                        pe.wait_ge(xa_xd[i].sem, xa_xd[i].at(b, 8 * h + (q - 1 if 2 < q < 7 else q)))
                    max_pass(h, q, CHUNK_BANK[q])

                def max_row(h):
                    pe.wait_ge(xa_nm[i].sem, xa_nm[i].at(b, h + 1))
                    for t in range(QT):
                        m = mm(bank(b_row, 1, t * P, P), side.xneg[:, t:t + 1], ident16[:], start=(t == 0), stop=True, skip_group_check=True)
                    m.then_inc(xa_mr[i].sem, 1)

                def scores(h, p):
                    n = NPAIR * h + p
                    if n >= 2:
                        pe.wait_ge(xa_e[i].sem, xa_e[i].at(b, n - 1))
                    for j, (kt, k_) in enumerate(pair_tiles(p)):
                        o = bank(b_s + n % 2, k_, j * SEQ, SEQ)
                        ks = slice(kt * P, kt * P + k_)
                        mm(o, c.h[:, ks], qh[:, h, :], start=(j == 0), stop=False, skip_group_check=True)
                        mm(o, c.h[:, ks], ql[:, h, :], start=False, stop=False, skip_group_check=True)
                        m = mm(o, c.l[:, ks], qh[0:DC, h, :], start=False, stop=True, skip_group_check=True)
                    m.then_inc(xa_s[i].sem, 1)

                def values(h, p):
                    n = NPAIR * h + p
                    if i == 0:
                        pe.wait_ge(xa_e[i].sem, xa_e[i].at(b, n + 1))
                    else:
                        pe.wait_ge(xa_l.sem, xa_l.at(b, n + 1))
                    if p == 0 and h > 0:
                        pe.wait_ge(xa_o[i].sem, xa_o[i].at(b, h))
                    for j, (kt, k_) in enumerate(pair_tiles(p)):
                        o = bank(b_o, DC + 1, 0, SEQ)
                        if i == 0:
                            m = mm(o, cf.tok[0:k_, kt, :], xp_slot(i, n)[0:k_, j * SEQ:(j + 1) * SEQ],
                                   start=(kt == 0), stop=(kt == NK - 1), skip_group_check=True)
                            continue
                        mm(o, cx.tok_h[0:k_, kt, :], xp_high(n, k_, j * SEQ, SEQ), start=(kt == 0), stop=False, skip_group_check=True)
                        mm(o, cx.tok_l[0:k_, kt, :], xp_high(n, k_, j * SEQ, SEQ), start=False, stop=False, skip_group_check=True)
                        m = mm(o, cx.tok_h[0:k_, kt, :], xp_l[0:k_, n % 3, j * SEQ:(j + 1) * SEQ], start=False, stop=(kt == NK - 1),
                               skip_group_check=True)
                    if p == NPAIR - 1:
                        m.then_inc(xa_pv[i].sem, 1)

                def output(h):
                    pe.wait_ge(xa_o[i].sem, xa_o[i].at(b, h + 1))
                    if h + 2 >= n_heads and h > 0:
                        pe.wait_ge(xa_a[i].sem, xa_a[i].at(b, h))
                    elif i == 1:
                        pe.wait_ge(xa_xd[i].sem, xa_xd[i].at(b, 8 * (h + 2) + 6))
                    for t in range(QT):
                        m = mm(ps[:, b_y, t * 256:t * 256 + D + 1], side.xo[:, t * P:(t + 1) * P], g_mat[:, u_a + h, :],
                               start=(t == 0), stop=True, skip_group_check=True)
                    m.then_inc(xa_f[i].sem, 1)

                def start():
                    transposes(b, 1 + 3 * i)
                    yield
                    x = side.xt[:, 1:1 + SEQ]
                    pe.wait_ge(xt_ready[1 + 3 * i].sem, xt_ready[1 + 3 * i].at(b, 1))
                    if i == 1 and not (isinstance(b, int) and b == 0):
                        pe.wait_ge(xa_a[1].sem, xa_a[1].at(b - 1, XH))
                    for h in range(n_heads):
                        if h >= 5:
                            pe.wait_ge(xa_ql[i].sem, xa_ql[i].at(b, h - 4))
                        mm(bank(6 if i == 0 else h % 5, KE, 0, SEQ), a_mat[:, u_a + h, :], x, start=True, stop=True).then_inc(xa_q[i].sem, 1)
                        if h % 2 == 1 or n_heads == 1:
                            yield

                    if i == 0:
                        pe.wait_ge(c_ext.sem, c_ext.at(b, 1))
                        pe.wait_ge(c_hi.sem, c_hi.at(b, 1))
                    else:
                        pe.wait_ge(ct_copied.sem, ct_copied.at(b, 32))
                    pe.wait_ge(xa_ql[i].sem, xa_ql[i].at(b, n_heads))
                    for q in range(8):
                        if i == 1:
                            next_chunk(0, q)
                        else:
                            if q >= 3:
                                pe.wait_ge(xa_xd[0].sem, xa_xd[0].at(b, q - 2))
                            max_pass(0, q, 5 + q % 3)
                        if q % 2:
                            yield
                    yield
                    max_row(0)
                    if i == 1:
                        for q in range(AHEAD):
                            next_chunk(1, q)
                    yield
                    if i == 0:
                        pe.wait_ge(c_lo.sem, c_lo.at(b, 1))
                        pe.wait_ge(tok_in.sem, tok_in.at(b, 32))
                    else:
                        pe.wait_ge(tok_lo.sem, tok_lo.at(b, 1))

                if h_from == 0:
                    yield from start()
                for h in range(h_from, h_to):
                    for p in range(NPAIR):
                        n = NPAIR * h + p
                        chunks = next_chunks(h, p) if i == 1 else []
                        if i == 1 and p == 5 and h + 1 < n_heads:
                            max_row(h + 1)
                        elif chunks:
                            next_chunk(*chunks.pop(0))
                        if p == 0:
                            pe.wait_ge(xa_mc[i].sem, xa_mc[i].at(b, h + 1))
                        scores(h, p)
                        for hc, q in chunks:
                            next_chunk(hc, q)
                        if n >= lag:
                            values(*divmod(n - lag, NPAIR))
                        if p == 2 and h > 0:
                            output(h - 1)
                        yield
                if h_to == n_heads:
                    for p in range(NPAIR - lag, NPAIR):
                        values(n_heads - 1, p)
                    yield
                    output(n_heads - 1)
                    yield
                    if i == 0:
                        for _ in range(NORM):
                            yield

            def experts(b):
                if not (isinstance(b, int) and b < 2):
                    pe.wait_ge(ff_r.sem, ff_r.at(b - 2, 1))
                transposes(b, 2)
                yield
                pe.wait_ge(xt_ready[2].sem, xt_ready[2].at(b, 1))
                x = front.xt[:, 1:1 + SEQ]
                for t in range(QT):
                    m = mm(bank(7, P, t * NE, NE), front.xt[:, 1 + t * P:1 + (t + 1) * P], gw, start=(t == 0), stop=True, skip_group_check=True)
                m.then_inc(me_l.sem, 1)

                def up(c):
                    if c >= 2:
                        pe.wait_ge(me_h.sem, me_h.at(b, c - 1))
                    mm(bank(6 + c % 2, P, 0, SEQ), wg[:, c, :], x, start=True, stop=True)
                    mm(bank(6 + c % 2, P, SEQ, SEQ), wu[:, c, :], x, start=False, stop=True, skip_group_check=True).then_inc(me_gu.sem, 1)

                def weights(k):
                    if k >= 2:
                        pe.wait_ge(me_cc.sem, me_cc.at(b, k - 1))
                    for j in range(2):
                        m = mm(bank(7 - 2 * (k % 2), P, j * SEQ, SEQ), sel3b[:, 2 * k + j, :], comb3[:], start=(j == 0), stop=True, skip_group_check=True)
                    m.then_inc(me_cb.sem, 1)

                def down(c):
                    pe.wait_ge(me_h.sem, me_h.at(b, c + 1))
                    m = mm(bank(5, P, 0, SEQ), wd[:, c, :], h2[:, c % 2, :], start=(c == 0), stop=(c == EC), skip_group_check=True)
                    if c == EC:
                        m.then_inc(me_d.sem, 1)

                yield
                if isinstance(b, int) and b == 0:
                    pe.wait_ge(loaded_late, 16 * len(late))
                up(0)
                for _ in range(ROUTING):
                    yield
                pe.wait_ge(me_c.sem, me_c.at(b, 1))
                for t in range(QT):
                    m = nc.tensor.transpose(bank(7, NE, t * P, P), comb[:, t, :], ident)
                m.then_inc(me_ct.sem, 1)
                yield
                pe.wait_ge(me_c3.sem, me_c3.at(b, 1))
                for k in range(EC // 2):
                    weights(k)
                    if k % 2:
                        yield
                pe.wait_ge(me_cc.sem, me_cc.at(b, EC // 2))
                for c in range(1, EC + 1):
                    if c >= 2:
                        down(c - 2)
                    up(c)
                    yield
                down(EC - 1)
                down(EC)
                yield
                pe.wait_ge(me_yt.sem, me_yt.at(b, 1))
                for t in range(QT):
                    m = nc.tensor.transpose(bank(6, P, t * P, P), yt[:, t * P:(t + 1) * P], ident)
                m.then_inc(me_y.sem, 1)
                for _ in range(NORM):
                    yield

            def last_ffn(b):
                transposes(b, 5)
                yield
                if not isinstance(b, int):
                    pe.wait_ge(xa_a[0].sem, xa_a[0].at(b + 2, 1))
                elif b == NB - 2:
                    pe.wait_ge(sa_r[1].sem, sa_r[1].at(NB - 1, 1))
                else:
                    pe.wait_ge(ff_r.sem, ff_r.at(NB - 2, 1))
                pe.wait_ge(xt_ready[5].sem, xt_ready[5].at(b, 1))
                for t in range(QT):
                    xx = front.xt[:, 1 + t * P:1 + (t + 1) * P]
                    mm(bank(6, P, t * E2, E2), xx, f_gate, start=(t == 0), stop=True, skip_group_check=True)
                    m = mm(bank(7, P, t * 2 * D, 2 * D), xx, f_m[:], start=(t == 0), stop=True, skip_group_check=True)
                m.then_inc(ff_l.sem, 1)
                yield
                for _ in range(NORM):
                    yield

            def left_over(b):
                for _ in range(NORM):
                    yield

            run(pe, lambda n, b: [lambda: self_attention(b, 0), lambda: cross_attention(b, 0, 0, 1), lambda: experts(b),
                                  lambda: self_attention(b, 1), lambda: cross_attention(b, 1, 0, CUT), lambda: last_ffn(b),
                                  lambda: left_over(b), lambda: cross_attention(b, 1, CUT, XH), lambda: folding(b)][n]())

        @block.scalar
        def _(act):
            fn = nc.scalar.activation

            def stream(b, n):
                act.wait_ge(tr_ready[n].sem, tr_ready[n].at(b, 1))
                side, bk = (cross, 4) if n == 4 else (front, 5)
                nc.scalar.copy(side.xt[:, 1:1 + SEQ], bank(bk, P, 0, SEQ)).then_inc(xt_ready[n].sem, 1)

            def self_attention(b, i):
                stream(b, 3 * i)
                yield
                for j in range(4):
                    if i == 1:
                        act.wait_ge(sa_proj[1].sem, sa_proj[1].at(b, j + 1))
                        bias = w1bqk[:, j:j + 1] if j < 2 else k1b[:, j - 2:j - 1]
                        fn(qk[:, j, :], bank(6 + j % 2, P, 0, SEQ), ACT.Identity, bias=bias).then_inc(sa_qk[1].sem, 1)
                    elif j == 1:
                        act.wait_ge(sa_tok[0].sem, sa_tok[0].at(b, 1))
                        for t in range(QT):
                            for f in range(2):
                                m = nc.scalar.copy(value_slots(v_h, t, f, 0), bank(5, P, t * P + f * HALF * HD, HALF * HD).rearrange("p (h c) -> p h c", c=HD))
                        m.then_inc(sa_v[0].sem, 1)
                    if j == 1:
                        yield
                if i == 1:
                    yield
                yield
                act.wait_ge(sa_qk[i].sem, sa_qk[i].at(b, 4))
                nc.scalar.copy(qk_h[:], qk[:]).then_inc(sa_hi[i].sem, 1)
                yield
                yield
                for piece in range(6):
                    act.wait_ge(sa_ql[i].sem, sa_ql[i].at(b, 1))
                    for h in range(16 * piece // 6, 16 * (piece + 1) // 6):
                        m = fn(qm_l[:, h, :], q_l[:, h // HALF, :], ACT.Copy, scale=hmask[:, h % HALF:h % HALF + 1])
                    if piece == 5:
                        m.then_inc(sa_qn[i].sem, 1)
                    yield
                act.wait_ge(sa_nt[i].sem, sa_nt[i].at(b, 1))
                nc.scalar.copy(nmt[:], ps[0:NH, 5, :].bitcast(BF16)[:, 0:SEQ]).then_inc(sa_ntc[i].sem, 1)
                if i == 1:
                    act.wait_ge(sa_ne.sem, sa_ne.at(b, 1))
                    fn(near[:], near[:], ACT.Exp, scale=SA_SCALE).then_inc(sa_nx.sem, 1)
                yield
                for g in range(12):
                    act.wait_ge(sa_s[i].sem, sa_s[i].at(b, g + 1))
                    fn(pr[:, g % 4, :], bank(6 + g % 2), ACT.Exp, scale=SA_SCALE).then_inc(sa_e[i].sem, 1)
                    if g % 2:
                        yield
                for piece in range(1 + QUOTIENTS + NORM):
                    if i == 0 and piece == HIGH_AT:
                        act.wait_ge(ct_in.sem, ct_in.at(b, 32))
                        fn(cf.h[DC:KE, :], mrow_u8[DC:KE, :], ACT.Identity, bias=xcol[DC:KE, 1:2], scale=xcol[DC:KE, 0:1]).then_inc(c_ext.sem, 1)
                    if i == 0 and piece == HIGH_AT + 1:
                        act.wait_ge(ct_in.sem, ct_in.at(b, 32))
                        nc.scalar.copy(cf.h[0:DC, :], ct32[0:DC, :]).then_inc(c_hi.sem, 1)
                    yield

            def cross_attention(b, i, h_from, h_to):
                n_heads, side, qh = (1, front, x0q_h) if i == 0 else (XH, cross, xq_h)
                b_row, b_s, b_o = (5, 6, 5) if i == 0 else (4, 1, 3)
                u_a = 0 if i == 0 else 1
                scale = 1.0 if i == 0 else XD ** -0.5
                def row(h):
                    act.wait_ge(xa_mr[i].sem, xa_mr[i].at(b, h + 1))
                    nc.scalar.copy(qh[SHIFT:SHIFT + 1, h, :], bank(b_row, 1, 0, SEQ)).then_inc(xa_mc[i].sem, 1)

                def exps(h, p):
                    n = NPAIR * h + p
                    act.wait_ge(xa_s[i].sem, xa_s[i].at(b, n + 1))
                    w, k_ = (2 * SEQ, P) if p < NPAIR - 1 else (SEQ, LASTK)
                    fn(xp_slot(i, n)[0:k_, 0:w], bank(b_s + n % 2, k_, 0, w), ACT.Exp, scale=scale).then_inc(xa_e[i].sem, 1)

                def sums(h):
                    act.wait_ge(xa_pv[i].sem, xa_pv[i].at(b, h + 1))
                    if h > 0:
                        act.wait_ge(xa_f[i].sem, xa_f[i].at(b, h))
                    nc.scalar.copy(side.xo[:], bank(b_o, DC + 1, 0, SEQ)).then_inc(xa_o[i].sem, 1)

                if h_from == 0:
                    stream(b, 1 + 3 * i)
                    if i == 1:
                        act.wait_ge(tok_in.sem, tok_in.at(b, 32))
                        if not (isinstance(b, int) and b == 0):
                            act.wait_ge(xa_pv[1].sem, xa_pv[1].at(b - 1, XH))
                        nc.scalar.copy(cx.tok_h[:, 0:NK - 1, :], cf.tok[:, 0:NK - 1, :])
                        nc.scalar.copy(cx.tok_h[0:LASTK, NK - 1, :], cf.tok[0:LASTK, NK - 1, :]).then_inc(tok_hi.sem, 1)
                    yield
                    for h in range(n_heads):
                        act.wait_ge(xa_q[i].sem, xa_q[i].at(b, h + 1))
                        fn(qh[:, h, :], bank(6 if i == 0 else h % 5, KE, 0, SEQ), ACT.Identity, bias=a_c[:, u_a + h:u_a + h + 1]).then_inc(xa_qh[i].sem, 1)
                        if h % 2 == 1 or n_heads == 1:
                            yield

                    for _ in range(4):
                        yield
                    yield
                    row(0)
                    yield
                for h in range(h_from, h_to):
                    for p in range(NPAIR):
                        if i == 1 and p == 5 and h + 1 < n_heads:
                            row(h + 1)
                        exps(h, p)
                        if p == 1 and h > 0:
                            sums(h - 1)
                        yield
                if h_to == n_heads:
                    sums(n_heads - 1)
                    yield
                    yield
                    if i == 0:
                        for _ in range(NORM):
                            yield

            def experts(b):
                stream(b, 2)
                yield
                act.wait_ge(me_l.sem, me_l.at(b, 1))
                fn(sg[:].rearrange("p t n -> p (t n)"), bank(7, P, 0, QT * NE), ACT.Tanh, scale=0.5).then_inc(me_t.sem, 1)
                for _ in range(1 + ROUTING):
                    yield
                for c in range(EC + 1):
                    act.wait_ge(me_gu.sem, me_gu.at(b, c + 1))
                    fn(tnh[:, c % 2, :], bank(6 + c % 2, P, 0, SEQ), ACT.Tanh, scale=0.5).then_inc(me_tn.sem, 1)
                    yield
                    for k in range(EC // 2 if c == 0 else 0):
                        act.wait_ge(me_cb.sem, me_cb.at(b, k + 1))
                        nc.scalar.copy(spread(k), bank(7 - 2 * (k % 2))).then_inc(me_cc.sem, 1)
                        if k % 2:
                            yield
                act.wait_ge(me_d.sem, me_d.at(b, 1))
                nc.scalar.copy(yt, bank(5, P, 0, SEQ)).then_inc(me_yt.sem, 1)
                yield
                for _ in range(NORM):
                    yield

            def last_ffn(b):
                stream(b, 5)
                yield
                act.wait_ge(ff_d.sem, ff_d.at(b, 1))
                fn(fp[:], fp[:], ACT.Exp).then_inc(ff_e.sem, 1)
                yield
                for _ in range(NORM):
                    yield

            def left_over(b):
                for _ in range(NORM):
                    yield

            def folding(_):
                for _ in range(PIECES[8]):
                    yield

            run(act, lambda n, b: [lambda: self_attention(b, 0), lambda: cross_attention(b, 0, 0, 1), lambda: experts(b),
                                   lambda: self_attention(b, 1), lambda: cross_attention(b, 1, 0, CUT), lambda: last_ffn(b),
                                  lambda: left_over(b), lambda: cross_attention(b, 1, CUT, XH), lambda: folding(b)][n]())

        @block.gpsimd
        def _(pool):
            sub = lambda out, a, b_: nc.gpsimd.tensor_tensor(out, a, b_, ALU.subtract)

            def idle(n):
                for _ in range(PIECES[n]):
                    yield

            def attention_low(b, i):
                after = 1 + QUOTIENTS + NORM
                for _ in range(PIECES[3 * i] - after - 6):
                    yield
                for g in range(12):
                    pool.wait_ge(sa_e[i].sem, sa_e[i].at(b, g + 1))
                    sub(pr_l[:, g % 4, :], pr[:, g % 4, :], pr_high(g)).then_inc(sa_l[i].sem, 1)
                    if g % 2:
                        yield
                for _ in range(after):
                    yield

            def context_low(b):
                for piece in range(PIECES[1]):
                    if piece == 2:
                        pool.wait_ge(c_hi.sem, c_hi.at(b, 1))
                    if 2 <= piece < 6:
                        k0, n = CHUNKS[piece - 2]
                        m = sub(cf.l[:, k0:k0 + n], ct32[0:DC, k0:k0 + n], cf.h[0:DC, k0:k0 + n])
                        if piece == 5:
                            m.then_inc(c_lo.sem, 1)
                    yield

            def probabilities_low(b, h_from, h_to):
                if h_from == 0:
                    pieces = PIECES[4] - h_to * NPAIR
                    pool.wait_ge(tok_hi.sem, tok_hi.at(b, 1))
                    for piece in range(pieces):
                        if 1 <= piece < 5:
                            ks = slice(3 * (piece - 1), 3 * piece)
                            sub(cx.tok_l[:, ks, :], cf.tok[:, ks, :], cx.tok_h[:, ks, :])
                        if piece == 5:
                            sub(cx.tok_l[0:LASTK, NK - 1, :], cf.tok[0:LASTK, NK - 1, :], cx.tok_h[0:LASTK, NK - 1, :]).then_inc(tok_lo.sem, 1)
                        yield
                for n in range(h_from * NPAIR, h_to * NPAIR):
                    w, k_ = (2 * SEQ, P) if n % NPAIR < NPAIR - 1 else (SEQ, LASTK)
                    pool.wait_ge(xa_e[1].sem, xa_e[1].at(b, n + 1))
                    sub(xp_l[0:k_, n % 3, 0:w], xp_slot(1, n)[0:k_, 0:w], xp_high(n, k_, 0, w)).then_inc(xa_l.sem, 1)
                    yield
                if h_to == XH:
                    yield
                    yield

            run(pool, lambda n, b: [lambda: attention_low(b, 0), lambda: context_low(b), lambda: idle(2), lambda: attention_low(b, 1),
                                    lambda: probabilities_low(b, 0, CUT), lambda: idle(5), lambda: idle(6),
                                    lambda: probabilities_low(b, CUT, XH), lambda: idle(8)][n]())

        @block.vector
        def _(dve):
            v = nc.vector
            tt, ts, stt, red = v.tensor_tensor, v.tensor_scalar, v.scalar_tensor_tensor, v.tensor_reduce
            v.memset(xk_e, 0.0).then_inc(dve_self, 1)
            v.memset(x0k_e[:], 0.0).then_inc(dve_self, 1)
            v.memset(g_mat[:, :, D:D + 1], 0.0).then_inc(dve_self, 1)
            v.memset(mrow_u8[DC:DC + 2, :], 0.0).then_inc(dve_self, 1)
            v.memset(front.xt[:, 0:1], 0.0)
            v.memset(cf.tok[:, :, DC:DC + 1], 1.0)
            v.memset(vm[:], 0.0).then_inc(dve_self, 1)
            dve.wait_ge(dve_self, 5)
            v.memset(g_mat[DC:DC + 1, :, D:D + 1], 1.0)
            for t in range(QT):
                for f in range(2):
                    v.memset(value_slots(v_h, t, f, HALF * HD), 1.0)
            dve.wait_ge(loaded_first, 16 * len(first_loads))
            for dst, src in ((identb, ident), (trib, tri), (onehotb, onehot)):
                m = v.tensor_copy(dst[:], src)
            m.then_inc(made, 1)

            def folding(_):
                for _ in range(LOADING - 1):
                    yield
                dve.wait_ge(loaded, 16 * len(loads))
                for dst, src in ((ident16, ident), (cornerb, corner), (sel3b, sel3)):
                    v.tensor_copy(dst[:], src)
                ts(k1b[:], w1bqk[:, 2:4], w1bqk[:, 4:5], None, ALU.add)
                v.tensor_copy(bias0[:, 0, :], b1tok[:, 0, :])
                tt(bias0[:, 1, :], b1tok[:, 1, :], r1k[:, 2, :], ALU.add)
                tt(bias0[:, 2, :], b1tok[:, 2, :], r1v[:, 2, :], ALU.add)
                tt(bias1[:, 0, :], b1tok[:, 1, :], r1k[:, 1, :], ALU.add)
                tt(bias1[:, 1, :], b1tok[:, 2, :], r1v[:, 1, :], ALU.add)
                tt(vfar[:], b1tok[:, 2, :], r1v[:, 0, :], ALU.add).then_inc(made, 1)
                v.tensor_copy(xk_e[:, :, 0:DC], x1wk[:]).then_inc(made, 1)
                v.tensor_copy(xk_e[:, :, DC + 1], x1b[:, 1, :]).then_inc(made, 1)
                v.tensor_copy(x0k_e[:, 0:DC], x0wk[:]).then_inc(made, 1)
                v.tensor_copy(x0k_e[:, DC + 1:DC + 2], x0b[:, 1:2]).then_inc(made, 1)
                v.tensor_copy(g_mat[:, 0, 0:D], x0v[:]).then_inc(made, 1)
                yield
                for h in range(1 + XH):
                    dve.wait_ge(folded, h + 1)
                    v.tensor_copy(a_mat[:, h, :], bank(h % 2, P, 0, KE)).then_inc(unfolded, 1)
                    xc = xcol[0:KE, 2:3] if h == 0 else xcol[0:KE, 3:4]
                    tt(a_c[:, h:h + 1], bank(h % 2, KE, 256, 1), xc, ALU.add).then_inc(unfolded, 1)
                    yield
                for h in range(XH):
                    dve.wait_ge(folded, 1 + XH + h + 1)
                    v.tensor_copy(g_mat[:, 1 + h, 0:D], bank(2 + h % 2, DC + 1, 0, D)).then_inc(unfolded, 1)
                    yield
                for e in range(2):
                    dve.wait_ge(folded, 1 + 2 * XH + e + 1)
                    v.tensor_copy(f_m[:, e * D:(e + 1) * D], bank(4 - 4 * e, P, 0, D)).then_inc(unfolded, 1)
                    yield
                yield

            base, taken, counts = [0], [0], []

            def begin(part, i=None):
                if part > 0:
                    counts.append(taken[0])
                taken[0] = 0
                if part < 3:
                    base[0] = sum(dve_steps[0:part]) + (0 if i is None else (i - 2) * dve_steps[2])
                else:
                    base[0] = sum(dve_steps[0:part]) + (NB - 3) * dve_steps[2]

            def step(ins):
                ins.then_inc(dve_step, 1)
                taken[0] += 1

            def settle():
                dve.wait_ge(dve_step, base[0] + taken[0])

            def pace():
                v.memset(carrier[:], 0.0)

            def over(ap, n):
                return ap.unsqueeze(ap.ndim).to_broadcast(list(ap.shape) + [n])

            def normalise(b, n, side):
                res, st6, mv, nr, nri, xs = side.res, side.st6, side.mv, side.nr, side.nri, source[n]
                for t in range(QT):
                    m = v.bn_stats(st6[:, t, :], res[:, t, :])
                step(m)
                settle()
                pace()
                for t in range(QT):
                    m = v.bn_aggr(mv[:, t, :], st6[:, t, :])
                step(m)
                settle()
                yield
                var, y, q = nr[:, 0, :], nri[:].bitcast(F32), nr[:, 1, :]
                step(ts(var, mv[:, :, 1], EPS, None, ALU.add))
                settle()
                step(ts(nri[:], nr[:, 0, :].bitcast(I32), 1, None, ALU.logical_shift_right))
                settle()
                step(ts(nri[:], nri[:], -1.0, float(0x5F3759DF), ALU.mult, ALU.add))
                settle()
                yield
                for _ in range(3):
                    step(tt(q, y, y, ALU.mult))
                    settle()
                    step(tt(q, q, var, ALU.mult))
                    settle()
                    step(ts(q, q, -0.5, 1.5, ALU.mult, ALU.add))
                    settle()
                    step(tt(y, y, q, ALU.mult))
                    settle()
                    yield
                if n == 6:
                    dve.wait_ge(x_out.sem, b * 16 + 16)
                for t in range(QT):
                    m = ts(xs[:, t, :], res[:, t, :], mv[:, t, 0:1], y[:, t:t + 1], ALU.subtract, ALU.mult)
                m.then_inc(xs_ready[n].sem, 1)
                yield

            def self_attention(b, i):
                res, xs = front.res, source[3 * i]
                yield
                if i == 0:
                    dve.wait_ge(x_in.sem, x_in.at(b, 16))
                    for j in range(4):
                        dve.wait_ge(sa_proj[0].sem, sa_proj[0].at(b, j + 1))
                        tt(qtmp[:, j, :], bank(6 + j % 2), rope.rearrange("p a n -> p (a n)"), ALU.mult).then_inc(qdone[0].sem, 1)
                        if j % 2:
                            dve.wait_ge(qdone[0].sem, qdone[0].at(b, j + 1))
                            if j == 3:
                                dve.wait_ge(sa_v[0].sem, sa_v[0].at(b, 1))
                                for t in range(QT):
                                    for f in range(2):
                                        m = tt(value_slots(v_l, t, f, 0), bank(5, P, t * P + f * HALF * HD, HALF * HD).rearrange("p (h c) -> p h c", c=HD),
                                               value_slots(v_h, t, f, 0), ALU.subtract)
                                m.then_inc(sa_vl.sem, 1)
                            for k in (j - 1, j):
                                tt(qk[:, k, :], qtmp[:, k, 0:SEQ], qtmp[:, k, SEQ:], ALU.add).then_inc(sa_qk[0].sem, 1)
                            yield
                else:
                    def token(t):
                        bk = 5 if t == 0 else 6
                        tt(tok[:, t, :, :].rearrange("p a n -> p (a n)"), bank(bk, P, 0, 3 * D), bias0[:].rearrange("p a n -> p (a n)"), ALU.add)
                        step(tt(v32[:], bank(bk, P, 2 * D, D), vfar[:], ALU.add))
                        settle()
                        for f in range(2):
                            far = v32[:, f * HALF * HD:(f + 1) * HALF * HD].rearrange("p (h c) -> p h c", c=HD)
                            m = v.tensor_copy(value_slots(v_h, t, f, 0), far)
                        step(m)
                        settle()
                        for f in range(2):
                            far = v32[:, f * HALF * HD:(f + 1) * HALF * HD].rearrange("p (h c) -> p h c", c=HD)
                            m = tt(value_slots(v_l, t, f, 0), far, value_slots(v_h, t, f, 0), ALU.subtract)
                        m.then_inc(sa_v[1].sem, 1)

                    def shifted(t):
                        bk = 5 if t == 0 else 7
                        tt(tok1[:, t, :, :].rearrange("p a n -> p (a n)"), bank(bk, P, 0, 2 * D), bias1[:].rearrange("p a n -> p (a n)"), ALU.add).then_inc(sa_v[1].sem, 1)

                    dve.wait_ge(sa_tok[1].sem, sa_tok[1].at(b, 1))
                    token(0)
                    yield
                    dve.wait_ge(sa_tok[1].sem, sa_tok[1].at(b, 2))
                    shifted(0)
                    yield
                    dve.wait_ge(sa_tok[1].sem, sa_tok[1].at(b, 3))
                    token(1)
                    dve.wait_ge(sa_tok[1].sem, sa_tok[1].at(b, 4))
                    shifted(1)
                    yield
                yield
                dve.wait_ge(sa_hi[i].sem, sa_hi[i].at(b, 1))
                dve.wait_ge(sa_qk[i].sem, sa_qk[i].at(b, 4))
                hi = slice(P // 2, P)
                tt(qk_h[hi, 2:4, :], qk[hi, 2:4, :], qk_h[hi, 2:4, :], ALU.subtract).then_inc(sa_ks[i].sem, 1)
                tt(q_l[:], qk[:, 0:2, :], qk_h[:, 0:2, :], ALU.subtract).then_inc(sa_ql[i].sem, 1)
                for h in range(NH):
                    if h == HALF:
                        yield
                    m = ts(qm_h[:, h, :], qk_h[:, h // HALF, :], hmask[:, h % HALF:h % HALF + 1], None, ALU.mult)
                m.then_inc(sa_qm[i].sem, 1)
                yield
                g = 0
                for t in range(QT):
                    n = (t + 1) * P
                    per = 512 // n
                    for h0 in range(0, NH, per):
                        dve.wait_ge(sa_x[i].sem, sa_x[i].at(b, g + 1))
                        red(smax[:, t, h0:h0 + per], ps[:, 5 + g % 3, :].rearrange("p (h n) -> p h n", n=n), AX.X, ALU.max).then_inc(sa_xd[i].sem, 1)
                        g += 1
                        if g % 3 == 0:
                            yield
                dve.wait_ge(sa_xd[i].sem, sa_xd[i].at(b, 12))
                if i == 0:
                    ts(nmb[:], smax[:], -1.0, None, ALU.mult).then_inc(sa_nm[0].sem, 1)
                    yield
                    yield
                else:
                    dve.wait_ge(sa_v[1].sem, sa_v[1].at(b, 4))
                    tt(prod[:, :, 0, :], tok[:, :, 0, :], tok[:, :, 1, :], ALU.mult)
                    step(tt(prod[:, :, 1, :], tok[:, :, 0, :], tok1[:, :, 0, :], ALU.mult))
                    settle()
                    step(red(near[:], prod[:].rearrange("p t a (h c) -> p (t a h) c", c=HD), AX.X, ALU.add))
                    settle()
                    step(tt(near[:, :, 1, :], near[:, :, 1, :], first, ALU.add))
                    step(tt(smax[:], smax[:], near[:, :, 0, :], ALU.max))
                    settle()
                    step(tt(smax[:], smax[:], near[:, :, 1, :], ALU.max))
                    settle()
                    ts(nmb[:], smax[:], -1.0, None, ALU.mult).then_inc(sa_nm[1].sem, 1)
                    dve.wait_ge(sa_nm[1].sem, sa_nm[1].at(b, 1))
                    for j in range(2):
                        m = tt(near[:, :, j, :], near[:, :, j, :], nmb[:], ALU.add)
                    m.then_inc(sa_ne.sem, 1)
                    step(tt(res[:], xs[:], b1o.unsqueeze(1).to_broadcast([P, QT, D]), ALU.add))
                    yield
                    yield
                if i == 1:
                    dve.wait_ge(sa_nx.sem, sa_nx.at(b, 1))
                    for t in range(QT):
                        tt(prod[:, t, 0, :].rearrange("p (h c) -> p h c", c=HD), tok[:, t, 2, :].rearrange("p (h c) -> p h c", c=HD), over(near[:, t, 0, :], HD), ALU.mult)
                        m = tt(prod[:, t, 1, :].rearrange("p (h c) -> p h c", c=HD), tok1[:, t, 1, :].rearrange("p (h c) -> p h c", c=HD), over(near[:, t, 1, :], HD), ALU.mult)
                    step(m)
                    step(tt(esum[:], near[:, :, 0, :], near[:, :, 1, :], ALU.add))
                    settle()
                    for t in range(QT):
                        tt(wnear[:, t, :, 0, :], prod[:, t, 0, :].rearrange("p (f n) -> p f n", f=2), prod[:, t, 1, :].rearrange("p (f n) -> p f n", f=2), ALU.add)
                        for f in range(2):
                            m = v.tensor_copy(wnear[:, t, f, 1, :].rearrange("p (h c) -> p h c", c=HD), over(esum[:, t, f * HALF:(f + 1) * HALF], HD))
                    m.then_inc(sa_w.sem, 1)
                for _ in range(6):
                    yield
                dve.wait_ge(sa_u[i].sem, sa_u[i].at(b, 1))
                for f in range(2):
                    m = v.reciprocal(rden[64 * f:64 * f + 64, :], ps[64:128, 5, f * SEQ:(f + 1) * SEQ])
                    yield
                step(m)
                settle()
                for f in range(2):
                    m = tt(ot[64 * f:64 * f + 64, :], ps[0:64, 5, f * SEQ:(f + 1) * SEQ], rden[64 * f:64 * f + 64, :], ALU.mult)
                m.then_inc(sa_ot[i].sem, 1)
                for _ in range(QUOTIENTS - 1):
                    yield
                dve.wait_ge(sa_y[i].sem, sa_y[i].at(b, 1))
                tt(res[:], tiles(bank(6, P, 0, SEQ)), xs[:] if i == 0 else res[:], ALU.add).then_inc(sa_r[i].sem, 1)
                dve.wait_ge(sa_r[i].sem, sa_r[i].at(b, 1))
                yield from normalise(b, 3 * i + 1, front)

            def cross_attention(b, i, h_from, h_to):
                n_heads, side, qh, ql = (1, front, x0q_h, x0q_l) if i == 0 else (XH, cross, xq_h, xq_l)
                b_row, b_s, b_o, b_y = (5, 6, 5, 6) if i == 0 else (4, 1, 3, 0)
                u_a = 0 if i == 0 else 1
                res, xs = side.res, source[1 + 3 * i]
                def chunk(h, q, bk):
                    t, c = q // 4, q % 4
                    dve.wait_ge(xa_x[i].sem, xa_x[i].at(b, 8 * h + q + 1))
                    red(side.xmax[:, t, c:c + 1], bank(bk, P, 0, CHUNKS[c][1]), AX.X, ALU.max).then_inc(xa_xd[i].sem, 1)

                def highest(h):
                    dve.wait_ge(xa_xd[i].sem, xa_xd[i].at(b, 8 * h + 8))
                    if h > 0:
                        dve.wait_ge(xa_mr[i].sem, xa_mr[i].at(b, h))
                    red(side.xneg[:], side.xmax[:], AX.X, ALU.max, negate=True).then_inc(xa_nm[i].sem, 1)

                def add(h):
                    dve.wait_ge(xa_f[i].sem, xa_f[i].at(b, h + 1))
                    step(v.reciprocal(side.xr[:], ps[:, b_y, :].rearrange("p (t n) -> p t n", n=256)[:, :, D]))
                    settle()
                    for t in range(QT):
                        m = stt(res[:, t, :], ps[:, b_y, t * 256:t * 256 + D], side.xr[:, t:t + 1],
                                xs[:, t, :] if i == 0 else res[:, t, :], ALU.mult, ALU.add)
                    m.then_inc(xa_a[i].sem, 1)

                if h_from == 0:
                    if i == 1:
                        dve.wait_ge(xs_ready[4].sem, xs_ready[4].at(b, 1))
                        if not (isinstance(b, int) and b == 0):
                            dve.wait_ge(xs_ready[5].sem, xs_ready[5].at(b - 1, 1))
                        step(tt(res[:], xs[:], x1bo.unsqueeze(1).to_broadcast([P, QT, D]), ALU.add))
                    yield
                    for h in range(n_heads):
                        dve.wait_ge(xa_qh[i].sem, xa_qh[i].at(b, h + 1))
                        stt(ql[:, h, :], bank(6 if i == 0 else h % 5, KE, 0, SEQ), a_c[:, u_a + h:u_a + h + 1], qh[:, h, :], ALU.add, ALU.subtract).then_inc(xa_ql[i].sem, 1)
                        if h % 2 == 1 or n_heads == 1:
                            yield

                    for q in range(8):
                        chunk(0, q, 5 + q % 3 if i == 0 else CHUNK_BANK[q])
                        if q % 2:
                            yield
                    highest(0)
                    yield
                    if i == 1:
                        dve.wait_ge(xa_nm[i].sem, xa_nm[i].at(b, 1))
                        for q in range(AHEAD):
                            chunk(1, q, CHUNK_BANK[q])
                    yield
                for h in range(h_from, h_to):
                    for p in range(NPAIR):
                        for hc, q in next_chunks(h, p) if i == 1 else ():
                            if q == 0:
                                dve.wait_ge(xa_nm[i].sem, xa_nm[i].at(b, hc))
                            chunk(hc, q, CHUNK_BANK[q])
                            if q == 7:
                                highest(hc)
                        if p == 2 and h > 0:
                            add(h - 1)
                        yield
                if h_to == n_heads:
                    yield
                    add(n_heads - 1)
                    yield
                    if i == 0:
                        dve.wait_ge(xa_a[0].sem, xa_a[0].at(b, 1))
                        yield from normalise(b, 2, side)

            def left_over(b):
                dve.wait_ge(xa_a[1].sem, xa_a[1].at(b, XH))
                yield from normalise(b, 5, cross)

            def experts(b):
                res, xs = front.res, source[2]
                yield
                dve.wait_ge(me_t.sem, me_t.at(b, 1))
                step(ts(sg[:], sg[:], 0.5, 0.5, ALU.mult, ALU.add))
                settle()
                step(tt(sc[:], sg[:], gb.unsqueeze(1).to_broadcast([P, QT, NE]), ALU.add))
                settle()
                pair = sc[:].rearrange("p t (g a c) -> p (t g) a c", a=2, c=2)
                tt(g2[:, 0, :, :], pair[:, :, :, 0], pair[:, :, :, 1], ALU.max)
                step(tt(g2[:, 1, :, :], pair[:, :, :, 0], pair[:, :, :, 1], ALU.min))
                settle()
                gg = g1[:].rearrange("p a t g -> p a (t g)")
                tt(gg[:, 0, :], g2[:, 0, :, 0], g2[:, 0, :, 1], ALU.max)
                tt(gg[:, 1, :], g2[:, 0, :, 0], g2[:, 0, :, 1], ALU.min)
                step(tt(gg[:, 2, :], g2[:, 1, :, 0], g2[:, 1, :, 1], ALU.max))
                settle()
                step(tt(gg[:, 1, :], gg[:, 1, :], gg[:, 2, :], ALU.max))
                settle()
                step(tt(gg[:, 3, :], gg[:, 0, :], gg[:, 1, :], ALU.add))
                settle()
                yield
                for t in range(QT):
                    gj = g1[:, 3, t, :].unsqueeze(1).to_broadcast([P, NG, NG])
                    gi = over(g1[:, 3, t, :], NG)
                    tt(gr[:, 0, t, :, :], gj, gi, ALU.is_gt)
                    m = tt(gr[:, 1, t, :, :], gj, gi, ALU.is_equal)
                step(m)
                settle()
                for t in range(QT):
                    m = tt(gr[:, 1, t, :, :], gr[:, 1, t, :, :], before, ALU.mult)
                step(m)
                settle()
                yield
                step(tt(gr[:, 2, :, :, :], gr[:, 0, :, :, :], gr[:, 1, :, :, :], ALU.add))
                settle()
                step(red(g1[:, 4, :, :], gr[:, 2, :, :, :], AX.X, ALU.add))
                settle()
                step(ts(g1[:, 5, :, :], g1[:, 4, :, :], 4.0, None, ALU.is_lt))
                settle()
                yield
                step(tt(msk[:].rearrange("p t (g c) -> p (t g) c", c=NE // NG), sc[:].rearrange("p t (g c) -> p (t g) c", c=NE // NG),
                        over(gg[:, 5, :], NE // NG), ALU.mult))
                settle()
                step(ts(msk[:], msk[:], 0.0, None, ALU.add))
                settle()
                pace()
                for t in range(QT):
                    m = v.max(v8[:, t, :], msk[:, t, :])
                step(m)
                settle()
                yield
                pace()
                for t in range(QT):
                    m = v.match_replace(rep[:, t, :], v8[:, t, :], msk[:, t, :], -1e30)
                step(m)
                settle()
                step(tt(rep[:], rep[:], msk[:], ALU.not_equal))
                settle()
                step(tt(comb[:], rep[:], sg[:], ALU.mult))
                settle()
                yield
                step(red(wsum[:], comb[:], AX.X, ALU.add))
                settle()
                step(ts(wsum[:], wsum[:], 1e-20, None, ALU.add))
                settle()
                step(v.reciprocal(wsum[:], wsum[:]))
                settle()
                for t in range(QT):
                    m = ts(comb[:, t, :], comb[:, t, :], wsum[:, t:t + 1], 1.25, ALU.mult, ALU.mult)
                m.then_inc(me_c.sem, 1)
                yield
                dve.wait_ge(me_ct.sem, me_ct.at(b, 1))
                step(v.tensor_copy(combt[:], bank(7, NE, 0, SEQ)))
                settle()
                step(v.tensor_copy(comb3[0:NE, :], combt[:]))
                settle()
                step(tt(combt[:], combt[:], comb3[0:NE, :], ALU.subtract))
                settle()
                step(v.tensor_copy(combm[:], combt[:]))
                settle()
                v.tensor_copy(comb3[NE:2 * NE, :], combm[:])
                step(tt(combt[:], combt[:], combm[:], ALU.subtract))
                settle()
                v.tensor_copy(comb3[2 * NE:, :], combt[:]).then_inc(me_c3.sem, 1)
                for c in range(EC + 1):
                    dve.wait_ge(me_tn.sem, me_tn.at(b, c + 1))
                    stt(ga[:, c % 2, :], tnh[:, c % 2, :], 1.0, bank(6 + c % 2, P, 0, SEQ), ALU.add, ALU.mult)
                    u = bank(6 + c % 2, P, SEQ, SEQ)
                    if c == 0:
                        step(ts(ub[:, 0, :], u, 0.5, None, ALU.mult))
                    else:
                        if c == 1:
                            dve.wait_ge(me_cc.sem, me_cc.at(b, EC // 2))
                        step(tt(ub[:, c % 2, :], u, spread((c - 1) // 2)[:, (c - 1) % 2 * SEQ:((c - 1) % 2 + 1) * SEQ], ALU.mult))
                    settle()
                    tt(h2[:, c % 2, :], ga[:, c % 2, :], ub[:, c % 2, :], ALU.mult).then_inc(me_h.sem, 1)
                    yield
                    if c == 0:
                        for _ in range(EC // 4):
                            yield
                yield
                dve.wait_ge(me_y.sem, me_y.at(b, 1))
                step(tt(res[:], tiles(bank(6, P, 0, SEQ)), xs[:], ALU.add))
                settle()
                yield from normalise(b, 3, front)

            def last_ffn(b):
                res, xs = front.res, xst
                yield
                lg = bank(6, P, 0, QT * E2).rearrange("p (t n) -> p t n", n=E2)
                dve.wait_ge(ff_l.sem, ff_l.at(b, 1))
                step(red(fs[:, 0, :], lg, AX.X, ALU.max))
                settle()
                tt(fp[:], lg, over(fs[:, 0, :], E2), ALU.subtract).then_inc(ff_d.sem, 1)
                dve.wait_ge(ff_e.sem, ff_e.at(b, 1))
                step(red(fs[:, 1, :], fp[:], AX.X, ALU.add))
                settle()
                step(v.reciprocal(fs[:, 1, :], fs[:, 1, :]))
                settle()
                step(tt(fp[:], fp[:], over(fs[:, 1, :], E2), ALU.mult))
                settle()
                step(ts(fq[:], fp[:], 0.3, None, ALU.is_gt))
                settle()
                step(red(fs[:, 2, :], fq[:], AX.X, ALU.add))
                settle()
                step(ts(fs[:, 3, :], fs[:, 2, :], -1.0, float(E2), ALU.mult, ALU.add))
                settle()
                tt(fs[:, 3, :], fs[:, 3, :], fp[:, :, 0], ALU.mult)
                step(tt(fs[:, 2, :], fs[:, 2, :], fp[:, :, 1], ALU.mult))
                settle()
                for t in range(QT):
                    m = stt(res[:, t, :], bank(7, P, t * 2 * D, D), fs[:, 3, t:t + 1], xs[:, t, :], ALU.mult, ALU.add)
                step(m)
                settle()
                for t in range(QT):
                    m = stt(res[:, t, :], bank(7, P, t * 2 * D + D, D), fs[:, 2, t:t + 1], res[:, t, :], ALU.mult, ALU.add)
                m.then_inc(ff_r.sem, 1)
                dve.wait_ge(ff_r.sem, ff_r.at(b, 1))
                yield
                yield from normalise(b, 6, front)

            run(dve, lambda n, b: [lambda: self_attention(b, 0), lambda: cross_attention(b, 0, 0, 1), lambda: experts(b),
                                   lambda: self_attention(b, 1), lambda: cross_attention(b, 1, 0, CUT), lambda: last_ffn(b),
                                  lambda: left_over(b), lambda: cross_attention(b, 1, CUT, XH), lambda: folding(b)][n](), begin)
            counts.append(taken[0])
            assert counts == list(dve_steps), counts


def shape_constants():
    import numpy as np
    f = np.float32
    c = {"ident": np.eye(P, dtype=f)}
    inv = (1.0 / f(10000.0) ** (np.arange(0, HD, 2, dtype=f) / f(HD))).astype(f)
    fr = (np.arange(SEQ, dtype=f)[:, None] * inv[None, :]).astype(f)
    emb = np.repeat(fr, 2, axis=-1)
    cos, sin = np.cos(emb).astype(f).T, np.sin(emb).astype(f).T
    sign = np.where(np.arange(HD) % 2 == 0, -1.0, 1.0).astype(f)[:, None]
    c["rope"] = np.stack([np.tile(cos, (P // HD, 1)), np.tile(sin * sign, (P // HD, 1))], 1).astype(f)
    k, q = np.arange(P)[:, None], np.arange(P)[None, :]
    no = f(-1e30)
    c["tri"] = np.stack([np.where(k > q, no, 0), np.where(q > k, no, 0),
                         np.where(k > q - 2, no, 0), np.where(q > k - 2, no, 0)], 1).astype(f)
    c["hmask"] = ((np.arange(P) % 64 // HD)[:, None] == np.arange(HALF)[None, :]).astype(f)
    c["onehot"] = np.repeat(np.eye(NH, dtype=f)[:, :, None], P, 2)
    corner = np.zeros((1, 2 * P + 1), f)
    corner[0, P - 1], corner[0, P], corner[0, 2 * P] = 1, 1, no
    c["corner"] = corner
    j, g = np.arange(NG)[None, :], np.arange(NG)[:, None]
    c["before"] = np.broadcast_to((j < g).astype(f), (P, NG, NG)).copy()
    e, cc, m = np.arange(96) % NE, np.arange(EC), np.arange(P)
    c["sel3"] = (e[:, None, None] == 2 * cc[None, :, None] + m[None, None, :] // EI).astype(f)
    first = np.zeros((P, QT, NH), f)
    first[0, 0] = no
    c["first"] = first
    xcol = np.zeros((P, 4), f)
    xcol[DC:DC + 2, 1] = 1
    xcol[DC + 2, 0] = -BIG
    xcol[DC + 2, 3] = BIG
    c["xcol"] = xcol
    return c


def layouts(a):
    import numpy as np
    f = np.float32
    c = {}

    def halves(w):
        return np.stack([np.concatenate([w[:, 64 * k:64 * k + 64]] * 2, 1) for k in range(2)], 1)

    def rows(r):
        return np.ascontiguousarray(np.broadcast_to(r, (P,) + r.shape))

    swap = np.arange(D) ^ 1
    wq, wk = a["L0_attn_Wq"].T, a["L0_attn_Wk"].T
    c["w0qk"] = np.stack([x for w in (wq, wk) for k in range(2) for x in (halves(w)[:, k], halves(w[:, swap])[:, k])], 1)
    c["w0v"], c["w0o"] = a["L0_attn_Wv"].T, a["L0_attn_Wo"].T
    c["w1qk"] = np.concatenate([halves(a["L1_attn_W_q"]), halves(a["L1_attn_W_k"])], 1)
    bq, bk = a["L1_attn_b_q"], a["L1_attn_b_k"]
    rk, rv = a["L1_attn_rel_k_table"], a["L1_attn_rel_v_table"]
    twice = lambda x: [np.tile(x[:64], 2), np.tile(x[64:], 2)]
    c["w1bqk"] = np.stack(twice(bq) + twice(bk) + [np.tile(rk[0], P // HD)], 1)
    c["w1tok"] = np.concatenate([a["L1_attn_W_q"], a["L1_attn_W_k"], a["L1_attn_W_v"]], 1)
    c["b1tok"] = rows(np.stack([bq, bk, a["L1_attn_b_v"]]))
    c["r1k"] = rows(np.stack([np.tile(rk[n], NH) for n in range(3)]))
    c["r1v"] = rows(np.stack([np.tile(rv[n], NH) for n in range(3)]))
    c["w1o"], c["b1o"] = a["L1_attn_W_o"], rows(a["L1_attn_b_o"])
    c["x0wq"], c["x0wk"] = a["L0_xattn_Wq"].T, a["L0_xattn_Wk"].T
    c["x0b"] = np.stack([a["L0_xattn_bq"], a["L0_xattn_bk"]], 1)
    c["x0v"] = np.concatenate([a["L0_xattn_Wv"], a["L0_xattn_bv"][None]], 0)
    heads = lambda w: w.reshape(XH, XD, -1).transpose(1, 0, 2)
    c["x1wq"], c["x1wk"], c["x1wv"] = heads(a["L1_xattn_Wq"]), heads(a["L1_xattn_Wk"]), heads(a["L1_xattn_Wv"])
    c["x1wo"] = heads(a["L1_xattn_Wo"].T)
    c["x1b"] = np.stack([a[n].reshape(XH, XD).T for n in ("L1_xattn_bq", "L1_xattn_bk", "L1_xattn_bv")], 1)
    c["x1bo"] = rows(a["L1_xattn_bo"])
    c["gw"], c["gb"] = a["L0_ffn_gate_w"].T, rows(a["L0_ffn_gate_bias"])
    up = lambda w, s: np.concatenate([s.T[:, None, :], w.reshape(EC, P, D).transpose(2, 0, 1)], 1)
    c["wg"], c["wu"] = up(a["L0_ffn_w_gate"], a["L0_ffn_sh_gate"]), up(a["L0_ffn_w_up"], a["L0_ffn_sh_up"])
    wd = a["L0_ffn_w_down"].transpose(0, 2, 1).reshape(EC, P, D).transpose(1, 0, 2)
    c["wd"] = np.concatenate([a["L0_ffn_sh_down"].T[:, None, :], wd], 1)
    c["f_gate"] = a["L1_ffn_gate_W"].T
    c["f_we"] = a["L1_ffn_expert_W"][0:2].transpose(1, 0, 2)
    c["f_wo"] = a["L1_ffn_out_W"].T
    c["x"], c["ctx"] = a["x"], a["ctx_768"]
    c["ctxT"] = a["ctx_768"].transpose(0, 2, 1)
    c["mask"] = a["mask_BxS2_bk0"]
    return c


def kernel(**inputs):
    import numpy as np
    import concourse.bacc as bacc
    from concourse.bass_utils import run_bass_kernel_spmd

    tables = dict(shape_constants())
    tables.update(layouts({k: np.asarray(v) for k, v in inputs.items()}))
    nc = bacc.Bacc("TRN2", target_bir_lowering=False, num_devices=1)
    arrays, d = {}, {}
    for name, t in tables.items():
        t = np.ascontiguousarray(t)
        arrays["in_" + name] = t
        d[name] = nc.dram_tensor("in_" + name, t.shape, mybir.dt.from_np(t.dtype), kind="ExternalInput").ap()
    out = nc.dram_tensor("out_0", (NB, SEQ, D), F32, kind="ExternalOutput").ap()
    decoder_kernel(nc, d, out, DVE_STEPS)
    r = run_bass_kernel_spmd(nc, [arrays], core_ids=[0])
    return r.results[0]["out_0"]


DVE_STEPS = (126, 137, 182, 56, 45)
```
